# Optimizing a Trainium2 kernel written in Bass

```python
import numpy as np
import jax
import jax.numpy as jnp

def _softmax(x, axis=-1):
    return jax.nn.softmax(x, axis=axis)

def _gelu(x):
    return jax.nn.gelu(x, approximate=True)

def _silu(x):
    return jax.nn.silu(x)

def _sigmoid(x):
    return jax.nn.sigmoid(x)

def _layernorm(x, axis=-1, eps=1e-05):
    m = jnp.mean(x, axis=axis, keepdims=True)
    v = jnp.var(x, axis=axis, keepdims=True)
    return (x - m) / jnp.sqrt(v + eps)

def _scatter_add(tgt, idx, src, axis=0):
    return tgt.at[idx].add(src)

def _segment_sum(src, seg, n):
    return jax.ops.segment_sum(src, seg, n)
kernel_name = 'mk_flamingo_gated_d2_seqx_r8_db6221'

def setup_inputs(seed: int=0):
    np.random.seed(seed)
    _w = jnp.asarray

    def _rec_inputs():
        import jax
        import jax.numpy as jnp
        _rk = jax.random.key(seed)
        x = -0.0002928 + 1 * jax.random.normal(jax.random.fold_in(_rk, 1), (128, 64, 128), jnp.float32)
        _lenS = 64 - jax.random.randint(jax.random.fold_in(_rk, 7), (128,), 0, max(1, 64 // 4) + 1, jnp.int32)
        _lenS2 = 64 - jax.random.randint(jax.random.fold_in(_rk, 8), (128,), 0, max(1, 64 // 4) + 1, jnp.int32)
        _ctx_1024P = jax.random.normal(jax.random.fold_in(_rk, 11), (128, 16, 128), jnp.float32)
        _ctx_1024c = jax.random.dirichlet(jax.random.fold_in(_rk, 511), 0.3 * jnp.ones((16,), jnp.float32), (128, 64))
        _ctx_1024t = jnp.einsum('bsk,bkd->bsd', _ctx_1024c, _ctx_1024P)
        _ctx_1024t = _ctx_1024t * jax.lax.rsqrt(jnp.mean(jnp.square(_ctx_1024t)) + 1e-12) * 0.953939
        ctx_1024 = -1.39393e-06 + 0.999914 * (_ctx_1024t + 0.3 * jax.random.normal(jax.random.fold_in(_rk, 611), (128, 64, 128), jnp.float32))
        _g = jax.random.normal(jax.random.fold_in(_rk, 9001), (2, 2), jnp.float32)
        _g = jnp.sign(_g) * jnp.maximum(jnp.abs(_g), 1.0) + (_g == 0) * 1.0
        g_xattn = _g[0]
        g_ffn = _g[1]
        return (x, ctx_1024, g_xattn, g_ffn)
    x, ctx_1024, g_xattn, g_ffn = _rec_inputs()

    def _L0_xattn_setup():
        import jax, jax.numpy as jnp
        import numpy as np
        import math
        D_MODEL = 128
        N_HEAD = 16

        def _split_heads(x, n_head):
            B, S, D = x.shape
            return x.reshape(B, S, n_head, D // n_head).transpose(0, 2, 1, 3)
        key = jax.random.key(seed)
        ks = jax.random.split(key, 11)
        B, S, D = (2, 256, D_MODEL)
        s = 1.0 / math.sqrt(D)
        return {'q': jax.random.normal(ks[0], (B, S, D), dtype=jnp.float32), 'k': jax.random.normal(ks[1], (B, S, D), dtype=jnp.float32), 'v': jax.random.normal(ks[2], (B, S, D), dtype=jnp.float32), 'w_q': jax.random.normal(ks[3], (D, D), dtype=jnp.float32) * s, 'b_q': jnp.zeros((D,), dtype=jnp.float32), 'w_k': jax.random.normal(ks[4], (D, D), dtype=jnp.float32) * s, 'b_k': jnp.zeros((D,), dtype=jnp.float32), 'w_v': jax.random.normal(ks[5], (D, D), dtype=jnp.float32) * s, 'b_v': jnp.zeros((D,), dtype=jnp.float32), 'w_out': jax.random.normal(ks[6], (D, D), dtype=jnp.float32) * s, 'b_out': jnp.zeros((D,), dtype=jnp.float32)}
    _L0_xattn_all = _L0_xattn_setup()
    _L0_xattn_in = {k: v for k, v in _L0_xattn_all.items() if k in ('w_q', 'b_q', 'w_k', 'b_k', 'w_v', 'b_v', 'w_out', 'b_out')}
    del _L0_xattn_all

    def _L0_ffn_setup():
        import jax, jax.numpy as jnp
        import numpy as np
        D = 128
        H = 512
        E = 8
        K = 2
        B, S = (4, 256)
        key = jax.random.key(seed)
        ks = jax.random.split(key, 8)

        def lin(k, fan_in, shape):
            bound = 1.0 / np.sqrt(fan_in)
            return jax.random.uniform(k, shape, jnp.float32, -bound, bound)
        return {'x': jax.random.normal(ks[0], (B, S, D), jnp.float32), 'Wg': lin(ks[1], D, (D, E)), 'bg': lin(ks[2], D, (E,)), 'W1': lin(ks[3], D, (E, D, H)), 'b1': lin(ks[4], D, (E, H)), 'W2': lin(ks[5], H, (E, H, D)), 'b2': lin(ks[6], H, (E, D))}
    _L0_ffn_all = _L0_ffn_setup()
    _L0_ffn_in = {k: v for k, v in _L0_ffn_all.items() if k in ('Wg', 'bg', 'W1', 'b1', 'W2', 'b2')}
    del _L0_ffn_all

    def _L1_xattn_setup():
        import jax, jax.numpy as jnp
        import numpy as np
        B, S, D = (4, 256, 128)
        NEG = -1000000000.0
        key = jax.random.key(seed)
        ks = jax.random.split(key, 12)
        sc = 1.0 / np.sqrt(D)
        inp = {'query': jax.random.normal(ks[0], (B, S, D), jnp.float32), 'key': jax.random.normal(ks[1], (B, S, D), jnp.float32), 'value': jax.random.normal(ks[2], (B, S, D), jnp.float32), 'Wq': jax.random.normal(ks[3], (D, D), jnp.float32) * sc, 'bq': jnp.zeros((D,), jnp.float32), 'Wk': jax.random.normal(ks[4], (D, D), jnp.float32) * sc, 'bk': jnp.zeros((D,), jnp.float32), 'Wv': jax.random.normal(ks[5], (D, D), jnp.float32) * sc, 'bv': jnp.zeros((D,), jnp.float32), 'Wo': jax.random.normal(ks[6], (D, D), jnp.float32) * sc, 'bo': jnp.zeros((D,), jnp.float32)}
        return inp
    _L1_xattn_all = _L1_xattn_setup()
    _L1_xattn_in = {k: v for k, v in _L1_xattn_all.items() if k in ('Wq', 'bq', 'Wk', 'bk', 'Wv', 'bv', 'Wo', 'bo')}
    del _L1_xattn_all

    def _L1_ffn_setup():
        import jax, jax.numpy as jnp
        import numpy as np
        DIM = 128
        NUM_EXPERTS = 8
        HIDDEN = 512
        CAP_FACTOR = 2.0
        B, S = (4, 256)
        key = jax.random.key(seed)
        ks = jax.random.split(key, 6)
        scale_r = 1.0 / np.sqrt(DIM)
        scale_1 = 1.0 / np.sqrt(DIM)
        scale_2 = 1.0 / np.sqrt(HIDDEN)
        return {'x': jax.random.normal(ks[0], (B, S, DIM), dtype=jnp.float32), 'router_w': jax.random.uniform(ks[1], (NUM_EXPERTS, DIM), jnp.float32, -scale_r, scale_r), 'w1': jax.random.uniform(ks[2], (NUM_EXPERTS, DIM, HIDDEN), jnp.float32, -scale_1, scale_1), 'b1': jax.random.uniform(ks[3], (NUM_EXPERTS, HIDDEN), jnp.float32, -scale_1, scale_1), 'w2': jax.random.uniform(ks[4], (NUM_EXPERTS, HIDDEN, DIM), jnp.float32, -scale_2, scale_2), 'b2': jax.random.uniform(ks[5], (NUM_EXPERTS, DIM), jnp.float32, -scale_2, scale_2)}
    _L1_ffn_all = _L1_ffn_setup()
    _L1_ffn_in = {k: v for k, v in _L1_ffn_all.items() if k in ('router_w', 'w1', 'b1', 'w2', 'b2')}
    del _L1_ffn_all
    return {'x': x, 'ctx_1024': ctx_1024, 'g_xattn': g_xattn, 'g_ffn': g_ffn, 'L0_xattn_w_q': _L0_xattn_in['w_q'], 'L0_xattn_b_q': _L0_xattn_in['b_q'], 'L0_xattn_w_k': _L0_xattn_in['w_k'], 'L0_xattn_b_k': _L0_xattn_in['b_k'], 'L0_xattn_w_v': _L0_xattn_in['w_v'], 'L0_xattn_b_v': _L0_xattn_in['b_v'], 'L0_xattn_w_out': _L0_xattn_in['w_out'], 'L0_xattn_b_out': _L0_xattn_in['b_out'], 'L0_ffn_Wg': _L0_ffn_in['Wg'], 'L0_ffn_bg': _L0_ffn_in['bg'], 'L0_ffn_W1': _L0_ffn_in['W1'], 'L0_ffn_b1': _L0_ffn_in['b1'], 'L0_ffn_W2': _L0_ffn_in['W2'], 'L0_ffn_b2': _L0_ffn_in['b2'], 'L1_xattn_Wq': _L1_xattn_in['Wq'], 'L1_xattn_bq': _L1_xattn_in['bq'], 'L1_xattn_Wk': _L1_xattn_in['Wk'], 'L1_xattn_bk': _L1_xattn_in['bk'], 'L1_xattn_Wv': _L1_xattn_in['Wv'], 'L1_xattn_bv': _L1_xattn_in['bv'], 'L1_xattn_Wo': _L1_xattn_in['Wo'], 'L1_xattn_bo': _L1_xattn_in['bo'], 'L1_ffn_router_w': _L1_ffn_in['router_w'], 'L1_ffn_w1': _L1_ffn_in['w1'], 'L1_ffn_b1': _L1_ffn_in['b1'], 'L1_ffn_w2': _L1_ffn_in['w2'], 'L1_ffn_b2': _L1_ffn_in['b2']}

def reference(x, ctx_1024, g_xattn, g_ffn, L0_xattn_w_q, L0_xattn_b_q, L0_xattn_w_k, L0_xattn_b_k, L0_xattn_w_v, L0_xattn_b_v, L0_xattn_w_out, L0_xattn_b_out, L0_ffn_Wg, L0_ffn_bg, L0_ffn_W1, L0_ffn_b1, L0_ffn_W2, L0_ffn_b2, L1_xattn_Wq, L1_xattn_bq, L1_xattn_Wk, L1_xattn_bk, L1_xattn_Wv, L1_xattn_bv, L1_xattn_Wo, L1_xattn_bo, L1_ffn_router_w, L1_ffn_w1, L1_ffn_b1, L1_ffn_w2, L1_ffn_b2):
    import jax
    import jax.numpy as jnp

    def _L0_xattn_ref(q, k, v, w_q, b_q, w_k, b_k, w_v, b_v, w_out, b_out):
        import jax, jax.numpy as jnp
        import numpy as np
        import math
        D_MODEL = 128
        N_HEAD = 16

        def _split_heads(x, n_head):
            B, S, D = x.shape
            return x.reshape(B, S, n_head, D // n_head).transpose(0, 2, 1, 3)
        qh = _split_heads(q @ w_q + b_q, N_HEAD)
        kh = _split_heads(k @ w_k + b_k, N_HEAD)
        vh = _split_heads(v @ w_v + b_v, N_HEAD)
        d_k = qh.shape[-1]
        scores = jnp.einsum('bhqd,bhkd->bhqk', qh, kh) / jnp.sqrt(jnp.float32(d_k))
        attn = jax.nn.softmax(scores, axis=-1)
        context = jnp.einsum('bhqk,bhkd->bhqd', attn, vh)
        B, H, S, dk = context.shape
        context = context.transpose(0, 2, 1, 3).reshape(B, S, H * dk)
        return context @ w_out + b_out

    def _L0_ffn_ref(x, Wg, bg, W1, b1, W2, b2):
        import jax, jax.numpy as jnp
        import numpy as np
        D = 128
        H = 512
        E = 8
        K = 2
        B, S = (4, 256)
        B_, S_, D_ = x.shape
        xt = x.reshape(-1, D_)
        logits = xt @ Wg + bg
        scores = jax.nn.softmax(logits, axis=-1)
        topk_probs, topk_idx = jax.lax.top_k(scores, K)
        h = jnp.einsum('nd,edh->enh', xt, W1) + b1[:, None, :]
        h = jax.nn.gelu(h, approximate=False)
        eo = jnp.einsum('enh,ehd->end', h, W2) + b2[:, None, :]
        eo = jnp.transpose(eo, (1, 0, 2))
        sel = jnp.take_along_axis(eo, topk_idx[:, :, None], axis=1)
        out = jnp.einsum('nk,nkd->nd', topk_probs, sel)
        return out.reshape(B_, S_, D_)

    def _L1_xattn_ref(query, key, value, Wq, bq, Wk, bk, Wv, bv, Wo, bo):
        import jax, jax.numpy as jnp
        import numpy as np
        B, S, D = (4, 256, 128)
        NEG = -1000000000.0
        d_model = query.shape[-1]
        q = query @ Wq + bq
        k = key @ Wk + bk
        v = value @ Wv + bv
        scores = jnp.einsum('bqd,bkd->bqk', q, k) / jnp.sqrt(jnp.float32(d_model))
        s = scores.shape[-1]
        causal = jnp.tril(jnp.ones((s, s), bool))
        scores = jnp.where(causal, scores, NEG)
        attn = jnp.exp(jax.nn.log_softmax(scores, axis=-1))
        out = jnp.einsum('bqk,bkd->bqd', attn, v)
        return out @ Wo + bo

    def _L1_ffn_ref(x, router_w, w1, b1, w2, b2):
        import jax, jax.numpy as jnp
        import numpy as np
        DIM = 128
        NUM_EXPERTS = 8
        HIDDEN = 512
        CAP_FACTOR = 2.0
        B, S = (4, 256)
        Bz, Sz, Dz = x.shape
        E = router_w.shape[0]
        capacity = max(1, int(Sz * CAP_FACTOR / E) + 1)
        scores = jax.nn.softmax(jnp.einsum('bsd,ed->bse', x, router_w), axis=-1)
        scores_t = jnp.swapaxes(scores, 1, 2)
        gate_vals, sel_idx = jax.lax.top_k(scores_t, capacity)
        b_idx = jnp.arange(Bz)[:, None, None]
        tokens = x[b_idx, sel_idx]
        h = jnp.einsum('becd,edh->bech', tokens, w1) + b1[None, :, None, :]
        h = jax.nn.gelu(h, approximate=False)
        y = jnp.einsum('bech,ehd->becd', h, w2) + b2[None, :, None, :]
        gated = y * gate_vals[..., None]
        out = jnp.zeros_like(x).at[b_idx, sel_idx].add(gated)
        return out
    x = x + jnp.tanh(g_xattn[0]) * _L0_xattn_ref(_layernorm(x, axis=-1), ctx_1024, ctx_1024, L0_xattn_w_q, L0_xattn_b_q, L0_xattn_w_k, L0_xattn_b_k, L0_xattn_w_v, L0_xattn_b_v, L0_xattn_w_out, L0_xattn_b_out)
    x = x + jnp.tanh(g_ffn[0]) * _L0_ffn_ref(_layernorm(x, axis=-1), L0_ffn_Wg, L0_ffn_bg, L0_ffn_W1, L0_ffn_b1, L0_ffn_W2, L0_ffn_b2)
    x = x + jnp.tanh(g_xattn[1]) * _L1_xattn_ref(_layernorm(x, axis=-1), ctx_1024, ctx_1024, L1_xattn_Wq, L1_xattn_bq, L1_xattn_Wk, L1_xattn_bk, L1_xattn_Wv, L1_xattn_bv, L1_xattn_Wo, L1_xattn_bo)
    x = x + jnp.tanh(g_ffn[1]) * _L1_ffn_ref(_layernorm(x, axis=-1), L1_ffn_router_w, L1_ffn_w1, L1_ffn_b1, L1_ffn_w2, L1_ffn_b2)
    return x

_drawn_inputs = setup_inputs


def setup_inputs(seed=0):
    import zlib

    import numpy as np

    out = dict(_drawn_inputs(seed))
    spreads = {'g_ffn': (-1.0, 0.6),
     'L0_xattn_b_q': (0.0, 0.404),
     'L0_xattn_b_k': (0.0, 0.8),
     'L0_xattn_b_v': (0.0, 0.1),
     'L0_xattn_b_out': (0.0, 0.1),
     'L1_xattn_bq': (0.0, 0.37),
     'L1_xattn_bk': (0.0, 0.8),
     'L1_xattn_bv': (0.0, 0.1),
     'L1_xattn_bo': (0.0, 0.1)}
    factors = {'L0_ffn_bg': 5.681, 'L0_ffn_b1': 8.0, 'L0_ffn_b2': 8.0, 'L1_ffn_b1': 8.0, 'L1_ffn_b2': 8.0}
    for name, (base, spread) in spreads.items():
        noise = np.random.default_rng([zlib.crc32(name.encode()), seed]).standard_normal(out[name].shape)
        drawn = base * np.exp(spread * noise) if base else spread * noise
        out[name] = jnp.asarray(drawn.astype(out[name].dtype))
    for name, factor in factors.items():
        out[name] = (out[name] * factor).astype(out[name].dtype)
    return out
```

```python
from contextlib import ExitStack
from functools import partial

import numpy as np
import concourse.bass as bass
from concourse import mybir

ALU = mybir.AluOpType
ACT = mybir.ActivationFunctionType
F32 = mybir.dt.float32
I32 = mybir.dt.int32
AX_X = mybir.AxisListType.X

P = 128
D = 128
NB, S = 128, 64
NT = NB * S // P
TG = 4
NG = NT // TG
GC = TG * P
HEADS, DH = 16, 8
QUADS = 4
PAIRS = HEADS // 2
NE, HID = 8, 512
HC = HID // P
CAP = max(1, int(S * 2.0 / NE) + 1)
SLOTS = 2 * CAP
TS = 8
NSG = NT // TS
EPS = 1e-5
NEG = -1.0e9
OUTSIDE = -3.0e38


class Sem:

    def __init__(self, handle):
        self.handle, self.n = handle, 0


class Plan:

    ENGINES = ("sp", "act", "pe", "dve", "pool")

    def __init__(self):
        self.queue = {e: [] for e in self.ENGINES}
        self.seen = {}

    def do(self, engine, emit, sem=None, by=1):
        self.queue[engine].append((emit, sem, by))
        if sem is not None:
            sem.n += by
            return (sem, sem.n)
        return None

    def wait(self, engine, *events):
        for event in events:
            if event is None:
                continue
            sem, n = event
            if self.seen.get((engine, sem), 0) < n:
                self.seen[(engine, sem)] = n
                self.queue[engine].append((None, sem, n))

    def run(self, engine, handle):
        for emit, sem, n in self.queue[engine]:
            if emit is None:
                handle.wait_ge(sem.handle, n)
                continue
            ins = emit()
            if sem is not None:
                ins.then_inc(sem.handle, n)


class Bank:
    def __init__(self, ap):
        self.ap, self.free = ap, None


def build(nc, t_in, out):
    with ExitStack() as ctx:
        def sb(name, shape, dt=F32):
            return ctx.enter_context(nc.sbuf_tensor(name, shape, dt))

        def sem(name):
            return Sem(ctx.enter_context(nc.semaphore(name)))

        plan = Plan()
        do, wait = plan.do, plan.wait

        x_sb = sb("x_sb", [P, NT, D])
        ctx_sb = sb("ctx_sb", [D, NT * P])
        w_sb = sb("w_sb", [P, 8, D])
        wo1_sb = sb("wo1_sb", [P, D])
        vec_sb = sb("vec_sb", [P, t_in["vecs"].shape[1]])
        row_sb = sb("row_sb", [P, 4, D])
        ident = sb("ident", [P, P])
        small_sb = sb("small_sb", [P, 4, NE])
        mask_sb = sb("mask_sb", [P, 2, P])
        wr_sb = sb("wr_sb", [P, 2, NE])
        w1_sb = sb("w1_sb", [D, NE, HID])
        w2_sb = sb("w2_sb", [P, NE, HC, D])
        b1_sb = sb("b1_sb", [P, 2, NE * HC])
        b2_sb = sb("b2_sb", [NE, 2, D])
        b2T_sb = sb("b2T_sb", [D, NE])
        slot_sb = sb("slot_sb", [P, SLOTS])
        ln1 = sb("ln1", [P, 2, D])
        tg_sb = sb("tg_sb", [P, 4])
        tbo_sb = sb("tbo_sb", [P, 2, D])

        stats = sb("stats", [P, 16, 6])
        mv = sb("mv", [P, NT, 2])
        rstd = sb("rstd", [P, NT])
        half_v = sb("half_v", [P, 16])
        newton = sb("newton", [P, 16])
        ln_sb = sb("ln_sb", [P, 2, TG, D])
        lnT = sb("lnT", [D, 2, GC])
        work = sb("work", [P, 10880])

        def cut(at, shape, names):
            n = int(np.prod(list(shape.values())))
            return work[:, at:at + n].rearrange(f"p ({names}) -> p {names}", **shape)

        kx = cut(0, dict(i=2, b=2 * TG, j=QUADS, k=S), "i b j k")
        pr = cut(4096, dict(i=2, h=HEADS, k=S), "i h k")
        pT = cut(6144, dict(i=2, r=PAIRS, q=P), "i r q")
        qT = cut(8192, dict(i=2, n=GC), "i n")
        kT = cut(9216, dict(i=2, n=GC), "i n")
        vx = sb("vx", [P, 2, PAIRS, 2, 2, DH])
        mx = sb("mx", [P, 2, HEADS])
        den = sb("den", [P, 2, HEADS])
        rden = sb("rden", [P, 2, HEADS])
        rdm = sb("rdm", [P, 2, PAIRS, 2, 2, DH])
        ctxn = sb("ctxn", [P, 2, 2, P])
        h_sb = sb("h_sb", [P, 4, GC])

        psum = ctx.enter_context(nc.psum_tensor("psum", [P, 8, 512], F32))
        banks = [Bank(psum[:, i, :]) for i in range(8)]

        V = {n: i for i, n in enumerate(["bq0", "bk0", "bq1", "bk1", "gx0", "gx1", "gf0", "gf1",
                                         "quad0", "quad1", "quad2", "quad3", "row0", "row1"])}

        def vec(name, n=1):
            return vec_sb[:, V[name]:V[name] + n]

        ld = {}

        def load(name, dst, src, eng="sp"):
            ld[name] = do(eng, partial((nc.sync if eng == "sp" else nc.scalar).dma_start, dst, src), sem("ld_" + name), 16)

        load("vecs", vec_sb[:], t_in["vecs"])
        load("ident", ident[:], t_in["ident"], "act")
        for g in range(4):
            load(f"x{g}", x_sb[:, TG * g:TG * g + TG, :], t_in["x"][:, TG * g:TG * g + TG, :])
            load(f"c{g}", ctx_sb[:, GC * g:GC * g + GC], t_in["ctxT"][:, GC * g:GC * g + GC], "act")
            if g == 0:
                load("w", w_sb[:], t_in["w"])
                load("rows", row_sb[:], t_in["rows"], "act")
        for g in range(1, 4):
            load(f"x{3 + g}", x_sb[:, 16 * g:16 * g + 16, :], t_in["x"][:, 16 * g:16 * g + 16, :])
            load(f"c{3 + g}", ctx_sb[:, 2048 * g:2048 * g + 2048],
                 t_in["ctxT"][:, 2048 * g:2048 * g + 2048], "act")
        load("wo1", wo1_sb[:], t_in["wo1"])
        load("small", small_sb[:], t_in["small"])
        load("mask", mask_sb[:], t_in["mask"])
        load("wr", wr_sb[:], t_in["wr"])
        load("w1", w1_sb[:], t_in["w1a"])
        load("w2", w2_sb[:], t_in["w2a"])
        load("b1", b1_sb[:], t_in["b1"])
        load("b2", b2_sb[:], t_in["b2"])
        load("b2T", b2T_sb[:], t_in["b2T"])
        load("slot", slot_sb[:], t_in["slot"])

        def xload(g):
            return ld[f"x{g}"] if g < 4 else ld[f"x{3 + g // 4}"]

        def cload(g):
            return ld[f"c{g}"] if g < 4 else ld[f"c{3 + g // 4}"]

        s_tg, s_tbo = sem("s_tg"), sem("s_tbo")
        wait("act", ld["vecs"])
        e_tg = do("act", partial(nc.scalar.activation, tg_sb[:], vec("gx0", 4), ACT.Tanh), s_tg)
        wait("dve", ld["vecs"], ld["rows"], e_tg)
        for l in range(2):
            e_tbo = do("dve", partial(nc.vector.tensor_scalar, tbo_sb[:, l, :], row_sb[:, 2 * l + 1, :],
                                                           tg_sb[:, l:l + 1], None, ALU.mult), s_tbo)
        TGX = [tg_sb[:, 0:1], tg_sb[:, 1:2]]
        TGF = [tg_sb[:, 2:3], tg_sb[:, 3:4]]

        s_st, s_mv, s_rs, s_ln = sem("s_st"), sem("s_mv"), sem("s_rs"), sem("s_ln")
        s_lt, s_lnT = sem("s_lt"), sem("s_lnT")
        ln_free = [None, None]
        lnT_free = [None, None]

        def statistics(lo, n, ready):
            def step(fn, counter=s_rs):
                wait("dve", do("dve", fn, counter))

            wait("dve", *ready)
            for t in range(n):
                e = do("dve", partial(nc.vector.bn_stats, stats[:, t, :], x_sb[:, lo + t, :]), s_st)
            wait("dve", e)
            for t in range(n):
                e = do("dve", partial(nc.vector.bn_aggr, mv[:, lo + t, :], stats[:, t, :]), s_mv)
            wait("dve", e)
            var, y, h, w = mv[:, lo:lo + n, 1], rstd[:, lo:lo + n], half_v[:, 0:n], newton[:, 0:n]
            step(partial(nc.vector.tensor_scalar, w, var, EPS, None, ALU.add))
            step(partial(nc.vector.tensor_scalar, h, w, -0.5, None, ALU.mult))
            step(partial(nc.vector.tensor_scalar, w.bitcast(I32), w.bitcast(I32), 1, None, ALU.arith_shift_right))
            step(partial(nc.vector.tensor_scalar, y.bitcast(I32), w.bitcast(I32), -1.0, float(0x5F3759DF), ALU.mult, ALU.add))
            for _ in range(3):
                step(partial(nc.vector.tensor_tensor, w, y, y, ALU.mult))
                step(partial(nc.vector.tensor_tensor, w, w, h, ALU.mult))
                step(partial(nc.vector.scalar_tensor_tensor, out=y, in0=w, scalar=1.5, in1=y, op0=ALU.add, op1=ALU.mult))

        def norm(g):
            i = g % 2
            wait("dve", ln_free[i])
            for t in range(TG):
                tt = TG * g + t
                e = do("dve", partial(nc.vector.tensor_scalar, 
                    ln_sb[:, i, t, :], x_sb[:, tt, :], mv[:, tt, 0:1], rstd[:, tt:tt + 1],
                    ALU.subtract, ALU.mult), s_ln)
            return e

        def turn(g, e_ln, bank):
            i = g % 2
            wait("pe", ld["ident"], e_ln, bank.free)
            for t in range(TG):
                e = do("pe", partial(nc.tensor.transpose, bank.ap[:, t * P:t * P + P], ln_sb[:, i, t, :], ident[:]), s_lt)
            ln_free[i] = e
            wait("act", e, lnT_free[i])
            bank.free = do("act", partial(nc.scalar.copy, lnT[:, i, :], bank.ap), s_lnT)
            return bank.free

        s_q, s_qe, s_k, s_ke, s_kx = sem("s_q"), sem("s_qe"), sem("s_k"), sem("s_ke"), sem("s_kx")
        s_v, s_vx, s_sc, s_mx, s_sub, s_exp = (sem("s_v"), sem("s_vx"), sem("s_sc"), sem("s_mx"),
                                               sem("s_sub"), sem("s_exp"))
        s_den, s_rden, s_rdm, s_pt, s_pT = sem("s_den"), sem("s_rden"), sem("s_rdm"), sem("s_pt"), sem("s_pT")
        s_av, s_cn, s_o, s_x1, s_xb = sem("s_av"), sem("s_cn"), sem("s_o"), sem("s_x1"), sem("s_xb")
        s_zero = sem("s_zero")
        e_zero = do("pool", partial(nc.gpsimd.memset, vx[:], 0.0), s_zero)
        SCALE0 = float(1.0 / np.sqrt(np.float32(DH)))
        ev = {}
        B_S, B_T, B_C, B_P = [(0, 1), (2, 3)], (4, 5), 6, 7

        def project(name, g, w, src, e_src, dst, bias, sem_mm, sem_ev):
            bank = banks[B_P]
            wait("pe", ld["w"], *e_src, bank.free)
            e = do("pe", partial(nc.tensor.matmul, bank.ap, w, src, start=True, stop=True), sem_mm)
            wait("act", e, ld["vecs"])
            bank.free = do("act", partial(nc.scalar.activation, dst, bank.ap, ACT.Identity, bias=bias), sem_ev)
            return bank.free

        def prep_norm(g):
            if g == 0:
                statistics(0, TG, [xload(0)])
            elif g == 1 or g % 4 == 0:
                n = (4 - g % 4) * TG
                statistics(TG * g, n, [xload(k) for k in range(g, g + n // TG)])
            ev["ln", g] = norm(g)
            wait("pool", e_tbo, ev["ln", g])
            ev["xb", g] = do("pool", partial(nc.gpsimd.tensor_tensor, 
                x_sb[:, TG * g:TG * g + TG, :], x_sb[:, TG * g:TG * g + TG, :],
                tbo_sb[:, 0:1, :].to_broadcast([P, TG, D]), ALU.add), s_xb)

        def prep_turn(g):
            ev["lnT", g] = turn(g, ev["ln", g], banks[B_P])

        def prep_q(g):
            i = g % 2
            wait("act", ev.get(("sc", TG * (g - 2) + TG - 1)))
            ev["q", g] = project("q", g, w_sb[:, 0, :], lnT[:, i, :], [ev["lnT", g]], qT[:, i, :], vec("bq0"), s_q, s_qe)
            lnT_free[i] = ev["q", g]

        def prep_k(g):
            i = g % 2
            wait("act", ev.get(("kx", g - 2)))
            ev["k", g] = project("k", g, w_sb[:, 1, :], ctx_sb[:, g * GC:g * GC + GC], [cload(g)], kT[:, i, :],
                                 vec("bk0"), s_k, s_ke)
            wait("pool", ev["k", g], ev.get(("sc", TG * (g - 2) + TG - 1)))
            for j in range(QUADS):
                ev["kx", g] = do("pool", partial(nc.gpsimd.tensor_scalar, 
                    kx[:, i, :, j, :], kT[:, i, :].rearrange("p (b k) -> p b k", k=S),
                    vec(f"quad{j}"), 1.0, ALU.mult, ALU.mult), s_kx)

        def prep_v(t):
            bank = banks[B_P]
            wait("pe", ld["w"], cload(t // TG), bank.free)
            e = do("pe", partial(nc.tensor.matmul, bank.ap[:, 0:D], ctx_sb[:, t * P:t * P + P], w_sb[:, 2, :],
                                            start=True, stop=True), s_v)
            wait("dve", e, e_zero, ld["rows"], ev.get(("av", t - 2)))
            for hp in range(2):
                q = slice(64 * hp, 64 * hp + 64)
                for b in range(2):
                    src = bank.ap[64 * b:64 * b + 64, 0:D].rearrange("p (r h d) -> p r h d", r=PAIRS, h=2)
                    e = do("dve", partial(nc.vector.tensor_tensor, 
                        vx[q, t % 2, :, b, hp, :], src[:, :, hp, :],
                        row_sb[q, 0, :].rearrange("p (r h d) -> p r h d", r=PAIRS, h=2)[:, :, hp, :],
                        ALU.add), s_vx)
            ev["vx", t] = bank.free = e

        def scores(t):
            g, i = t // TG, (t // TG) % 2
            two = [banks[n] for n in B_S[t % 2]]
            wait("pe", ev["q", g], ev["kx", g], *[b.free for b in two])
            done = []
            for quad in range(QUADS):
                q = slice(32 * quad, 32 * quad + 32)
                if quad >= 2:
                    wait("pe", done[quad - 2])
                for b in range(2):
                    c = (t % TG) * P + b * S
                    dst = two[quad % 2].ap[64 * b:64 * b + 64, 256 * (quad // 2):256 * (quad // 2) + 256]
                    e = do("pe", partial(nc.tensor.matmul, 
                        dst, qT[q, i, c:c + S], kx[q, i, 2 * (t % TG) + b, :, :], start=True, stop=True), s_sc)
                done.append(e)
            ev["sc", t] = e

        def largest(t):
            two = B_S[t % 2]
            src = psum[:, two[0]:two[1] + 1, :].rearrange("p a (h k) -> p (a h) k", k=S)
            i = t % 2
            wait("dve", ev["sc", t], ev.get(("pt", t - 2)))
            e = do("dve", partial(nc.vector.tensor_reduce, mx[:, i, :], src, AX_X, ALU.max), s_mx)
            wait("dve", e)
            e = do("dve", partial(nc.vector.tensor_tensor, pr[:, i, :, :], src, mx[:, i, :].unsqueeze(2).to_broadcast([P, HEADS, S]),
                                                    ALU.subtract), s_sub)
            for n in two:
                banks[n].free = e
            ev["sub", t] = e

        def exponentials(t):
            i = t % 2
            wait("act", ev["sub", t])
            ev["exp", t] = do("act", partial(nc.scalar.activation, pr[:, i, :, :], pr[:, i, :, :], ACT.Exp, scale=SCALE0), s_exp)

        def denominators(t):
            i = t % 2
            wait("dve", ev["exp", t], ev.get(("av", t - 2)))
            e = do("dve", partial(nc.vector.tensor_reduce, den[:, i, :], pr[:, i, :, :], AX_X, ALU.add), s_den)
            wait("dve", e)
            e = do("dve", partial(nc.vector.reciprocal, rden[:, i, :], den[:, i, :]), s_rden)
            wait("dve", e)
            wait("pool", e)
            for b in range(2):
                e = do("pool", partial(nc.gpsimd.tensor_scalar, 
                    rdm[:, i, :, b, :, :],
                    rden[:, i, :].rearrange("p (r h) -> p r h", h=2).unsqueeze(3).to_broadcast([P, PAIRS, 2, DH]),
                    vec(f"row{b}"), 1.0, ALU.mult, ALU.mult), s_rdm)
            ev["rdm", t] = e

        def turn_p(t):
            i = t % 2
            wait("pe", ev["exp", t])
            for half in range(2):
                bank = banks[B_T[half]]
                wait("pe", bank.free)
                for r in range(4):
                    pair = 4 * half + r
                    e = do("pe", partial(nc.tensor.transpose, 
                        bank.ap[:, r * P:r * P + P], pr[:, i, 2 * pair:2 * pair + 2, :], ident[:]), s_pt)
                wait("act", e, ev.get(("av", t - 2)))
                bank.free = do("act", partial(nc.scalar.copy, 
                    pT[:, i, 4 * half:4 * half + 4, :], bank.ap), s_pT)
            ev["pt", t] = e
            ev["pT", t] = bank.free

        def attend(t):
            i = t % 2
            bank = banks[B_C]
            wait("pe", ev["pT", t], ev["vx", t], ev["rdm", t], bank.free)
            for pair in range(PAIRS):
                q = 32 * (pair % 4)
                dst = bank.ap[q:q + 32, (pair // 4) * P:(pair // 4) * P + P]
                do("pe", partial(nc.tensor.matmul, dst, vx[:, i, pair, :, :, :], pT[:, i, pair, :],
                                                              start=True, stop=True), s_av)
            for half in range(2):
                dst = bank.ap[:, 256 + half * P:256 + half * P + P]
                rep = rdm[:, i, 4 * half:4 * half + 4, :, :, :].rearrange("p r b h d -> p (r b h d)")
                e = do("pe", partial(nc.tensor.transpose, dst, rep, ident[:]), s_av)
            ev["av", t] = e
            wait("act", e, ev.get(("cn", t - 2)))
            e = do("act", partial(nc.scalar.copy, ctxn[:, i, :, :], bank.ap[:, 256:512].rearrange("p (a q) -> p a q", a=2)), s_rc)
            wait("dve", e, ev.get(("o", t - 2)))
            bank.free = ev["cn", t] = do("dve", partial(nc.vector.tensor_tensor, 
                ctxn[:, i, :, :], bank.ap[:, 0:256].rearrange("p (a q) -> p a q", a=2), ctxn[:, i, :, :], ALU.mult), s_cn)

        s_rc = sem("s_rc")

        def output(t):
            bank = banks[B_P]
            wait("pe", ev["cn", t], bank.free)
            for half in range(2):
                e = do("pe", partial(nc.tensor.matmul, bank.ap[:, 0:D], ctxn[:, t % 2, half, :], w_sb[:, 3 + half, :],
                                                         start=(half == 0), stop=(half == 1)), s_o)
            ev["o", t] = e
            wait("dve", e, ev["xb", t // TG])
            ev["x1", t] = bank.free = do("dve", partial(nc.vector.scalar_tensor_tensor, 
                out=x_sb[:, t, :], in0=bank.ap[:, 0:D], scalar=TGX[0], in1=x_sb[:, t, :],
                op0=ALU.mult, op1=ALU.add), s_x1)

        for f in (prep_norm, prep_turn, prep_q, prep_k):
            f(0)
        for t in range(NT + 2):
            g, r = t // TG + 1, t % TG
            if 0 <= t - 1 < NT:
                denominators(t - 1)
                prep_v(t - 1)
            if t < NT:
                scores(t)
                if r == 0 and g < NG:
                    prep_norm(g)
                largest(t)
            if 0 <= t - 2 < NT:
                attend(t - 2)
            if r > 0 and g < NG:
                (prep_turn, prep_q, prep_k)[r - 1](g)
            if t < NT:
                exponentials(t)
            if 0 <= t - 1 < NT:
                turn_p(t - 1)
            if 0 <= t - 2 < NT:
                output(t - 2)

        lg_sb = sb("lg_sb", [P, NT, NE])
        tmp = [sb(f"tmp{i}", [P, 16, NE]) for i in range(3)]
        red = sb("red", [P, 16])
        sel = sb("sel", [P, 16, NE])
        gT = sb("gT", [NE, 2, GC])
        s_lg, s_r, s_ex, s_gt, s_gT, s_h, s_hg, s_y, s_x2, s_b2 = [sem("m" + str(i)) for i in range(10)]
        ones_row = sb("ones_row", [P, S])
        s_one = sem("s_one")
        e_one = do("pool", partial(nc.gpsimd.memset, ones_row[:], 1.0), s_one)
        NS = 16

        def dve(fn, *w):
            wait("dve", *w)
            e = do("dve", fn, s_r)
            wait("dve", e)
            return e

        def softmax8(lo):
            L = lg_sb[:, lo:lo + NS, :]
            bc = red[:].unsqueeze(2).to_broadcast([P, NS, NE])
            dve(partial(nc.vector.tensor_reduce, red[:], L, AX_X, ALU.max))
            e = dve(partial(nc.vector.tensor_tensor, L, L, bc, ALU.subtract))
            wait("act", e)
            e = do("act", partial(nc.scalar.activation, L, L, ACT.Exp), s_ex)
            dve(partial(nc.vector.tensor_reduce, red[:], L, AX_X, ALU.add), e)
            dve(partial(nc.vector.reciprocal, red[:], red[:]))
            return dve(partial(nc.vector.tensor_tensor, L, L, bc, ALU.mult))

        def choose_top2(lo):
            L = lg_sb[:, lo:lo + NS, :]
            bc = red[:].unsqueeze(2).to_broadcast([P, NS, NE])
            order = small_sb[:, 1:2, :].to_broadcast([P, NS, NE])
            w, left, one = tmp[0][:], tmp[1][:], tmp[2][:]
            for k in range(2):
                src = L if k == 0 else left
                dve(partial(nc.vector.tensor_reduce, red[:], src, AX_X, ALU.max))
                dve(partial(nc.vector.tensor_tensor, w, src, bc, ALU.is_equal))
                dve(partial(nc.vector.tensor_tensor, w, w, order, ALU.mult), ld["small"])
                dve(partial(nc.vector.tensor_reduce, red[:], w, AX_X, ALU.max))
                dve(partial(nc.vector.tensor_tensor, one if k else sel[:], w, bc, ALU.is_equal))
                if k == 0:
                    dve(partial(nc.vector.tensor_scalar, w, sel[:], -2.0, None, ALU.mult))
                    dve(partial(nc.vector.tensor_tensor, left, L, w, ALU.add))
            dve(partial(nc.vector.tensor_tensor, sel[:], sel[:], one, ALU.add))
            dve(partial(nc.vector.tensor_tensor, sel[:], sel[:], L, ALU.mult))
            return dve(partial(nc.vector.tensor_scalar, L, sel[:], TGF[0], None, ALU.mult))

        def moe(layer, x_ready):
            for g in range(NG):
                if g % 4 == 0:
                    statistics(TG * g, 16, [x_ready(TG * g + t) for t in range(16)])
                e_ln = norm(g)
                e_lnT = turn(g, e_ln, banks[7])
                i = g % 2
                bank = banks[6]
                wait("pe", e_lnT, ld["wr"], bank.free)
                for t in range(TG):
                    e = do("pe", partial(nc.tensor.matmul, bank.ap[:, NE * t:NE * t + NE], lnT[:, i, t * P:t * P + P],
                                                       wr_sb[:, layer, :], start=True, stop=True), s_lg)
                lnT_free[i] = e
                dst = lg_sb[:, TG * g:TG * g + TG, :]
                src = bank.ap[:, 0:TG * NE].rearrange("p (t e) -> p t e", e=NE)
                if layer == 0:
                    bank.free = dve(partial(nc.vector.tensor_tensor, dst, src, small_sb[:, 0:1, :].to_broadcast([P, TG, NE]),
                                                              ALU.add), e, ld["small"])
                else:
                    bank.free = dve(partial(nc.vector.tensor_copy, dst, src), e)
            for lo in range(0, NT, NS):
                ev["routed", lo] = softmax8(lo)
                ev["gates", layer, lo] = choose_top2(lo) if layer == 0 else choose_tokens(lo)
            for g in range(NG):
                i = g % 2
                e_ln = norm(g)
                e_lnT = turn(g, e_ln, banks[7])
                gates = ev["gates", layer, (TG * g) // NS * NS]
                bank = banks[6]
                wait("pe", gates, bank.free)
                for t in range(TG):
                    e = do("pe", partial(nc.tensor.transpose, bank.ap[0:NE, t * P:t * P + P], lg_sb[:, TG * g + t, :], ident[:]), s_gt)
                wait("dve", e, ev.get(("b2", layer, g - 2)))
                bank.free = e_gT = do("dve", partial(nc.vector.tensor_copy, gT[:, i, :], bank.ap[0:NE, :]), s_gT)
                wait("pe", e_gT, ld["b2"], banks[7].free)
                for t in range(TG):
                    e = do("pe", partial(nc.tensor.matmul, banks[7].ap[:, t * D:t * D + D], gT[:, i, t * P:t * P + P],
                                                       b2_sb[:, layer, :], start=True, stop=True), s_b2)
                ev["b2", layer, g] = e
                xg = x_sb[:, TG * g:TG * g + TG, :]
                wait("dve", e)
                banks[7].free = e_x = do("dve", partial(nc.vector.tensor_tensor, 
                    xg, xg, banks[7].ap.rearrange("p (t d) -> p t d", d=D), ALU.add), s_x2)
                wait("pe", ld["w1"], ld["w2"], e_lnT)

                def up(ex, c):
                    bank = banks[c]
                    wait("pe", bank.free)
                    e = do("pe", partial(nc.tensor.matmul, bank.ap, w1_sb[:, ex, c * P:c * P + P], lnT[:, i, :],
                                                    start=True, stop=True), s_h)
                    wait("act", e, ld["b1"], ev.get(("y", c)))
                    bank.free = ev["hg", c] = do("act", partial(nc.scalar.activation, 
                        h_sb[:, c, :], bank.ap, ACT.Gelu, bias=b1_sb[:, layer, ex * HC + c:ex * HC + c + 1]), s_hg)
                    return e

                def down(ex):
                    nonlocal e_x
                    bank = banks[4 + ex % 2]
                    wait("pe", bank.free)
                    for t in range(TG):
                        for c in range(HC):
                            wait("pe", ev["hg", c])
                            e = do("pe", partial(nc.tensor.matmul, 
                                bank.ap[:, t * D:t * D + D], h_sb[:, c, t * P:t * P + P], w2_sb[:, ex, c, :],
                                start=(c == 0), stop=(c == HC - 1)), s_y)
                            if t == TG - 1:
                                ev["y", c] = e
                    wait("dve", e, e_x)
                    for t in range(TG):
                        tt = TG * g + t
                        bank.free = e_x = do("dve", partial(nc.vector.scalar_tensor_tensor, 
                            out=x_sb[:, tt, :], in0=bank.ap[:, t * D:t * D + D], scalar=lg_sb[:, tt, ex:ex + 1],
                            in1=x_sb[:, tt, :], op0=ALU.mult, op1=ALU.add), s_x2)

                for ex in range(NE):
                    for c in range(HC):
                        e = up(ex, c)
                    down(ex)
                lnT_free[i] = e
                for t in range(TG):
                    ev["x2", layer, TG * g + t] = e_x

        moe(0, lambda t: ev["x1", t])
        load_free = [ev["x2", 0, NT - 1]]
        wait("sp", *load_free)
        load("w1_1", w1_sb[:], t_in["w1b"])
        load("w2_1", w2_sb[:], t_in["w2b"])
        ld["w1"], ld["w2"] = ld["w1_1"], ld["w2_1"]

        kT1 = kx[:, :, :, :, :].rearrange("p i b j k -> p i (b j k)")[:, :, 0:GC]
        v1 = vx[:].rearrange("p i r b h d -> p i (r b h d)")[:, :, 0:D]
        t1 = sb("t1", [P, 2, P])
        sm = sb("sm", [P, 2, 4])
        s1 = {n: sem("n_" + n) for n in ["v", "ve", "s", "t", "m", "n", "e", "r", "p", "pt", "pT", "c", "cT", "o", "x", "xb"]}
        SCALE1 = float(1.0 / np.sqrt(np.float32(D)))
        pT1 = pT[:].rearrange("p i r q -> p i (r q)")[:, :, 0:P]
        cT1 = ctxn[:, :, 0, :]

        def prep1(g):
            i = g % 2
            if g % 4 == 0:
                statistics(TG * g, 16, [ev["x2", 0, TG * g + t] for t in range(16)])
            ev["ln1", g] = norm(g)
            wait("pool", e_tbo, ev["ln1", g])
            ev["xb1", g] = do("pool", partial(nc.gpsimd.tensor_tensor, 
                x_sb[:, TG * g:TG * g + TG, :], x_sb[:, TG * g:TG * g + TG, :],
                tbo_sb[:, 1:2, :].to_broadcast([P, TG, D]), ALU.add), s1["xb"])
            e = turn(g, ev["ln1", g], banks[7])
            wait("act", ev.get(("s1", TG * (g - 2) + TG - 1)))
            ev["q1", g] = project("q1", g, w_sb[:, 5, :], lnT[:, i, :], [e], qT[:, i, :], vec("bq1"), s_q, s_qe)
            lnT_free[i] = ev["q1", g]
            ev["k1", g] = project("k1", g, w_sb[:, 6, :], ctx_sb[:, g * GC:g * GC + GC], [], kT1[:, i, :], vec("bk1"), s_k, s_ke)

        def scores1(t):
            g, i, j = t // TG, (t // TG) % 2, t % 2
            c = (t % TG) * P
            bank = banks[j]
            wait("pe", ev["q1", g], ev["k1", g], bank.free)
            ev["s1", t] = e = do("pe", partial(nc.tensor.matmul, bank.ap[:, 0:P], qT[:, i, c:c + P], kT1[:, i, c:c + P],
                                                       start=True, stop=True), s1["s"])
            wait("dve", e, ld["mask"])
            bank.free = e = do("dve", partial(nc.vector.scalar_tensor_tensor, 
                out=t1[:, j, :], in0=bank.ap[:, 0:P], scalar=SCALE1, in1=mask_sb[:, 0, :], op0=ALU.mult, op1=ALU.mult), s1["t"])
            wait("dve", e)
            e = do("dve", partial(nc.vector.tensor_tensor, pr[:, j, 0:2, :], t1[:, j, :].rearrange("p (b k) -> p b k", b=2),
                                                    mask_sb[:, 1, :].rearrange("p (b k) -> p b k", b=2), ALU.add), s1["m"])
            wait("dve", e)
            e = do("dve", partial(nc.vector.tensor_reduce, sm[:, j, 0:1], pr[:, j, 0:2, :].rearrange("p b k -> p (b k)"), AX_X, ALU.max,
                                                    negate=True), s1["n"])
            wait("act", e)
            ev["e1", t] = do("act", partial(nc.scalar.activation, t1[:, j, :], pr[:, j, 0:2, :].rearrange("p b k -> p (b k)"), ACT.Exp,
                                                        bias=sm[:, j, 0:1], accum_out=sm[:, j, 1:2]), s1["e"])
            bank = banks[2 + j]
            wait("pe", ld["w"], bank.free)
            e = do("pe", partial(nc.tensor.matmul, bank.ap[:, 0:D], ctx_sb[:, t * P:t * P + P], w_sb[:, 7, :], start=True, stop=True), s1["v"])
            wait("dve", e, ev.get(("c1", t - 2)))
            bank.free = ev["v1", t] = do("dve", partial(nc.vector.tensor_tensor, v1[:, j, :], bank.ap[:, 0:D], row_sb[:, 2, :], ALU.add), s1["ve"])

        def attend1(t):
            j = t % 2
            wait("dve", ev["e1", t])
            e = do("dve", partial(nc.vector.reciprocal, sm[:, j, 2:3], sm[:, j, 1:2]), s1["r"])
            wait("dve", e)
            e = do("dve", partial(nc.vector.tensor_scalar, t1[:, j, :], t1[:, j, :], sm[:, j, 2:3], None, ALU.mult), s1["p"])
            bank = banks[4 + j]
            wait("pe", e, bank.free)
            e = do("pe", partial(nc.tensor.transpose, bank.ap[:, 0:P], t1[:, j, :], ident[:]), s1["pt"])
            wait("act", e, ev.get(("c1", t - 2)))
            bank.free = e = do("act", partial(nc.scalar.copy, pT1[:, j, :], bank.ap[:, 0:P]), s1["pT"])
            wait("pe", e, ev["v1", t])
            ev["c1", t] = e = do("pe", partial(nc.tensor.matmul, bank.ap[:, 0:P], v1[:, j, :], pT1[:, j, :], start=True, stop=True), s1["c"])
            wait("act", e, ev.get(("o1", t - 2)))
            bank.free = ev["cT1", t] = do("act", partial(nc.scalar.copy, cT1[:, j, :], bank.ap[:, 0:P]), s1["cT"])

        def output1(t):
            j = t % 2
            bank = banks[6]
            wait("pe", ev["cT1", t], ld["wo1"], bank.free)
            ev["o1", t] = e = do("pe", partial(nc.tensor.matmul, bank.ap[:, 0:D], cT1[:, j, :], wo1_sb[:], start=True, stop=True), s1["o"])
            wait("dve", e, ev["xb1", t // TG])
            ev["x3", t] = bank.free = do("dve", partial(nc.vector.scalar_tensor_tensor, 
                out=x_sb[:, t, :], in0=bank.ap[:, 0:D], scalar=TGX[1], in1=x_sb[:, t, :],
                op0=ALU.mult, op1=ALU.add), s1["x"])

        prep1(0)
        for t in range(NT + 2):
            if t < NT:
                scores1(t)
                if t % TG == 0 and t // TG + 1 < NG:
                    prep1(t // TG + 1)
            if 0 <= t - 1 < NT:
                attend1(t - 1)
            if 0 <= t - 2 < NT:
                output1(t - 2)

        scores_r = sb("scores_r", [P, 2, S])
        left_r = sb("left_r", [P, 2, S])
        mask_r = sb("mask_r", [P, 2, S])
        both_r = sb("both_r", [P, 2, 2, S])
        count_r = sb("count_r", [P, 2, S])
        top = sb("top", [P, 3, 8])
        gp = sb("gp", [P, 2, 2, NS, NE])
        pick = sb("pick", [P, 2, NE, SLOTS])
        pickg = sb("pickg", [P, 2, NE, SLOTS])
        arena = ctx_sb[:].rearrange("p n -> p n")
        pickT = arena[:, 0:2 * TS * 3 * P].rearrange("p (i t k q) -> p i t k q", i=2, t=TS, k=3)
        n_xg = TS * NE * SLOTS
        xgT = [cut(n_xg * i, dict(e=NE, t=TS, s=SLOTS), "e t s") for i in range(2)]
        yT = [cut(n_xg * (2 + i), dict(t=TS, e=NE, s=SLOTS), "t e s") for i in range(2)]
        hid = cut(n_xg * 4, dict(i=2, c=HC, t=TS, s=SLOTS), "i c t s")
        yr = sb("yr", [P, 2, 3, D])
        KS = [(0, 3), (3, 6), (6, 8)]
        z = {n: sem("z_" + n) for n in ["tr", "tb", "gp", "pk", "pg", "ga", "xg", "pt", "pT", "up", "hg", "dn", "y",
                                        "yt", "yr", "sc", "x"]}

        def route1(lo):
            for g in range(lo // TG, lo // TG + 4):
                if g % 4 == 0:
                    statistics(TG * g, 16, [ev["x3", TG * g + t] for t in range(16)])
                    yield
                i = g % 2
                e_ln = norm(g)
                e_lnT = turn(g, e_ln, banks[7])
                bank = banks[6]
                wait("pe", e_lnT, ld["wr"], bank.free)
                for t in range(TG):
                    e = do("pe", partial(nc.tensor.matmul, bank.ap[:, NE * t:NE * t + NE], lnT[:, i, t * P:t * P + P],
                                         wr_sb[:, 1, :], start=True, stop=True), s_lg)
                lnT_free[i] = e
                bank.free = dve(partial(nc.vector.tensor_copy, lg_sb[:, TG * g:TG * g + TG, :],
                                        bank.ap[:, 0:TG * NE].rearrange("p (t e) -> p t e", e=NE)), e)
                yield
            L = lg_sb[:, lo:lo + NS, :]
            e = softmax8(lo)
            yield
            bank = banks[6]
            wait("pe", e, bank.free)
            e = do("pe", partial(nc.tensor.transpose, bank.ap[:, 0:P], L.rearrange("p t e -> p (t e)"), ident[:]), z["tr"])
            src = bank.ap[:, 0:P].rearrange("p (b k) -> p b k", k=S)
            wait("dve", e)
            do("dve", partial(nc.vector.tensor_copy, scores_r[:], src), s_r)
            bank.free = dve(partial(nc.vector.tensor_copy, left_r[:], src))
            yield
            for b in range(2):
                a, w, m, c = scores_r[:, b, :], left_r[:, b, :], mask_r[:, b, :], count_r[:, b, :]
                for k in range(CAP // 8):
                    dve(partial(nc.vector.max, top[:, k, :], w))
                    dve(partial(nc.vector.match_replace, out=w, in_to_replace=top[:, k, :], in_values=w, imm_value=-1.0))
                    yield
                dve(partial(nc.vector.max, top[:, 2, :], w))
                dve(partial(nc.vector.tensor_scalar, m, w, top[:, 2, 0:1], None, ALU.is_equal))
                dve(partial(nc.vector.tensor_tensor_scan, out=c, data0=ones_row[:], data1=m, initial=0.0,
                            op0=ALU.mult, op1=ALU.add), e_one)
                dve(partial(nc.vector.scalar_tensor_tensor, out=m, in0=c, scalar=1.0, in1=m, op0=ALU.is_equal, op1=ALU.mult))
                dve(partial(nc.vector.scalar_tensor_tensor, out=m, in0=w, scalar=0.0, in1=m, op0=ALU.is_lt, op1=ALU.add))
                yield
                dve(partial(nc.vector.scalar_tensor_tensor, out=both_r[:, 0, b, :], in0=a, scalar=TGF[1], in1=m,
                            op0=ALU.mult, op1=ALU.mult))
                dve(partial(nc.vector.tensor_tensor_scan, out=c, data0=ones_row[:], data1=m, initial=float(CAP * b),
                            op0=ALU.mult, op1=ALU.add))
                dve(partial(nc.vector.tensor_tensor, c, c, m, ALU.mult))
                e = dve(partial(nc.vector.tensor_scalar, both_r[:, 1, b, :], c, -1.0, None, ALU.add))
                yield
            wait("pe", e, bank.free)
            for k in range(2):
                e = do("pe", partial(nc.tensor.transpose, bank.ap[:, k * P:k * P + P],
                                     both_r[:, k, :, :].rearrange("p b k -> p (b k)"), ident[:]), z["tb"])
            h = (lo // NS) % 2
            wait("dve", e, ev.get(("pickg", lo - NS - 1)))
            ev["gp", lo] = bank.free = do("dve", partial(
                nc.vector.tensor_copy, gp[:, h, :, :, :], bank.ap[:, 0:2 * P].rearrange("p (k t e) -> p k t e", k=2, e=NE)), z["gp"])

        def gather(t):
            sg, i, h = t // TS, t % 2, (t // NS) % 2
            place = gp[:, h, 1, t % NS, :].unsqueeze(2).to_broadcast([P, NE, SLOTS])
            gate = gp[:, h, 0, t % NS, :].unsqueeze(2).to_broadcast([P, NE, SLOTS])
            wait("dve", ev["gp", t // NS * NS], ld["slot"], ev.get(("ga", t - 2)), ev.get(("pickg", t - 2)))
            e_pick = do("dve", partial(nc.vector.tensor_tensor, pick[:, i, :, :], slot_sb[:].unsqueeze(1).to_broadcast([P, NE, SLOTS]),
                                        place, ALU.is_equal), z["pk"])
            wait("pool", e_pick, ev.get(("pt", t - 2)))
            ev["pickg", t] = e_pg = do("pool", partial(nc.gpsimd.tensor_tensor, pickg[:, i, :, :], pick[:, i, :, :], gate, ALU.mult), z["pg"])
            e_ln = do("dve", partial(nc.vector.tensor_scalar, ln1[:, i, :], x_sb[:, t, :], mv[:, t, 0:1], rstd[:, t:t + 1],
                                     ALU.subtract, ALU.mult), s_ln)
            bank = banks[6]
            wait("pe", e_pick, e_ln, bank.free)
            ev["ga", t] = e = do("pe", partial(nc.tensor.matmul, bank.ap[:, 0:NE * SLOTS], ln1[:, i, :],
                                               pick[:, i, :, :].rearrange("p e s -> p (e s)"), start=True, stop=True), z["ga"])
            wait("act", e, ev.get(("up", sg - 2)))
            ev["xg", sg] = bank.free = do("act", partial(
                nc.scalar.copy, xgT[sg % 2][:, :, t % TS, :], bank.ap[:, 0:NE * SLOTS].rearrange("p (e s) -> p e s", s=SLOTS)), z["xg"])
            bank = banks[7]
            wait("pe", e_pg, bank.free)
            for k, (a, b) in enumerate(KS):
                ev["pt", t] = e = do("pe", partial(
                    nc.tensor.transpose, bank.ap[0:(b - a) * SLOTS, k * P:k * P + P],
                    pickg[:, i, a:b, :].rearrange("p e s -> p (e s)"), ident[:]), z["pt"])
            wait("dve", e, ev.get(("sc", t - 2 * TS)))
            rows = KS[0][1] * SLOTS
            do("dve", partial(nc.vector.tensor_copy, pickT[0:rows, sg % 2, t % TS, 0:2, :],
                              bank.ap[0:rows, 0:2 * P].rearrange("p (k q) -> p k q", q=P)), z["pT"])
            rows = (KS[2][1] - KS[2][0]) * SLOTS
            bank.free = ev["pT", t] = do("dve", partial(nc.vector.tensor_copy, pickT[0:rows, sg % 2, t % TS, 2, :],
                                                       bank.ap[0:rows, 2 * P:3 * P]), z["pT"])

        def up1(sg, ex):
            for c in range(HC):
                bank = banks[c]
                wait("pe", ev["xg", sg], ld["w1"], bank.free)
                e = do("pe", partial(nc.tensor.matmul, bank.ap[:, 0:TS * SLOTS], w1_sb[:, ex, c * P:c * P + P],
                                     xgT[sg % 2][:, ex, :, :].rearrange("p t s -> p (t s)"), start=True, stop=True), z["up"])
                wait("act", e, ld["b1"], ev.get(("dn", ex % 2)))
                ev["hg", ex % 2] = bank.free = do("act", partial(
                    nc.scalar.activation, hid[:, ex % 2, c, :, :].rearrange("p t s -> p (t s)"), bank.ap[:, 0:TS * SLOTS],
                    ACT.Gelu, bias=b1_sb[:, 1, ex * HC + c:ex * HC + c + 1]), z["hg"])
            ev["up", sg] = e

        def down1(sg, ex):
            bank = banks[4 + ex % 2]
            wait("pe", ev["hg", ex % 2], ld["w2"], bank.free)
            for c in range(HC):
                e = do("pe", partial(nc.tensor.matmul, bank.ap[:, 0:TS * SLOTS], w2_sb[:, ex, c, :],
                                     hid[:, ex % 2, c, :, :].rearrange("p t s -> p (t s)"), start=(c == 0), stop=(c == HC - 1)), z["dn"])
            ev["dn", ex % 2] = e
            wait("dve", e, ld["b2T"], ev.get(("yt", (sg - 1) * TS - 1)))
            ev["y", sg] = bank.free = do("dve", partial(
                nc.vector.tensor_scalar, yT[sg % 2][:, :, ex, :], bank.ap[:, 0:TS * SLOTS].rearrange("p (t s) -> p t s", s=SLOTS),
                b2T_sb[:, ex:ex + 1], None, ALU.add), z["y"])

        def scatter(t):
            sg, i = t // TS, t % 2
            bank = banks[7]
            wait("pe", ev["y", sg], bank.free)
            for k, (a, b) in enumerate(KS):
                e = do("pe", partial(nc.tensor.transpose, bank.ap[0:(b - a) * SLOTS, k * D:k * D + D],
                                     yT[sg % 2][:, t % TS, a:b, :].rearrange("p e s -> p (e s)"), ident[:]), z["yt"])
            ev["yt", t] = e
            wait("act", e, ev.get(("sc", t - 2)))
            rows = KS[0][1] * SLOTS
            do("act", partial(nc.scalar.copy, yr[0:rows, i, 0:2, :], bank.ap[0:rows, 0:2 * D].rearrange("p (k q) -> p k q", q=D)), z["yr"])
            rows = (KS[2][1] - KS[2][0]) * SLOTS
            e = bank.free = do("act", partial(nc.scalar.copy, yr[0:rows, i, 2, :], bank.ap[0:rows, 2 * D:3 * D]), z["yr"])
            bank = banks[6]
            wait("pe", e, ev["pT", t], bank.free)
            for k, (a, b) in enumerate(KS):
                rows = (b - a) * SLOTS
                e = do("pe", partial(nc.tensor.matmul, bank.ap[:, 0:D], pickT[0:rows, sg % 2, t % TS, k, :], yr[0:rows, i, k, :],
                                     start=(k == 0), stop=(k == 2)), z["sc"])
            ev["sc", t] = e
            wait("dve", e)
            ev["x4", t] = bank.free = do("dve", partial(nc.vector.tensor_tensor, x_sb[:, t, :], bank.ap[:, 0:D], x_sb[:, t, :], ALU.add), z["x"])

        for _ in route1(0):
            pass
        for t in range(TS):
            gather(t)
        routing = iter(())
        for sg in range(NSG + 1):
            if sg % 2 == 0 and (sg // 2 + 1) * NS < NT:
                routing = route1((sg // 2 + 1) * NS)
            if sg % 2 == 1:
                for _ in routing:
                    pass
            for ex in range(NE):
                if sg < NSG:
                    up1(sg, ex)
                for _ in range(3):
                    next(routing, None)
                if sg > 0:
                    scatter((sg - 1) * TS + ex)
                if sg + 1 < NSG:
                    gather((sg + 1) * TS + ex)
                if sg < NSG and ex > 0:
                    down1(sg, ex - 1)
            if sg < NSG:
                down1(sg, NE - 1)

        s_out = sem("s_out")
        for g in range(NG):
            wait("sp", ev["x4", TG * g + TG - 1])
            e = do("sp", partial(nc.sync.dma_start, out[:, TG * g:TG * g + TG, :], x_sb[:, TG * g:TG * g + TG, :]), s_out, 16)
        wait("sp", e)

        block = ctx.enter_context(nc.Block())

        @block.sync
        def _(e):
            plan.run("sp", e)

        @block.scalar
        def _(e):
            plan.run("act", e)

        @block.tensor
        def _(e):
            plan.run("pe", e)

        @block.vector
        def _(e):
            plan.run("dve", e)

        @block.gpsimd
        def _(e):
            plan.run("pool", e)


def lay_out(i):
    a = {k: np.asarray(v) for k, v in i.items()}
    col = lambda v: np.broadcast_to(v.reshape(-1, 1) if v.size > 1 else v.reshape(1, 1), (P, 1))
    f = lambda *c: np.ascontiguousarray(np.concatenate(c, axis=1), np.float32)
    r = np.arange(P)
    quad = [((r // DH) % QUADS == j).astype(np.float32).reshape(P, 1) for j in range(QUADS)]
    row = [(r // S == b).astype(np.float32).reshape(P, 1) for b in range(2)]
    gx, gf = a["g_xattn"], a["g_ffn"]
    rr, bb, hh, dd = np.meshgrid(np.arange(4), np.arange(2), np.arange(2), np.arange(DH), indexing="ij")
    head = np.array([4 * quad + j for quad in (0, 2, 1, 3) for j in range(4)])
    dims = (head[:, None] * DH + np.arange(DH)).ravel()
    src = [(head[half * 8 + rr * 2 + hh] * DH + dd).ravel() for half in range(2)]
    w = [a["L0_xattn_w_q"], a["L0_xattn_w_k"], a["L0_xattn_w_v"][:, dims], a["L0_xattn_w_out"][src[0]], a["L0_xattn_w_out"][src[1]],
         a["L1_xattn_Wq"], a["L1_xattn_Wk"], a["L1_xattn_Wv"]]
    rows = [a["L0_xattn_b_v"][dims], a["L0_xattn_b_out"], a["L1_xattn_bv"], a["L1_xattn_bo"]]
    q, k = r[:, None], r[None, :]
    same = q // S == k // S
    mask = np.stack([(same & (k <= q)), np.where(same, np.where(k <= q, 0.0, NEG), OUTSIDE)], 1).astype(np.float32)
    small = np.zeros((P, 4, NE), np.float32)
    small[:, 0, :] = a["L0_ffn_bg"]
    small[:, 1, :] = NE - np.arange(NE)
    c = np.ascontiguousarray
    return {
        "x": c(a["x"].reshape(NT, P, D).transpose(1, 0, 2)),
        "ctxT": c(a["ctx_1024"].reshape(NT * P, D).T),
        "w": c(np.stack(w, 1)),
        "wo1": c(a["L1_xattn_Wo"]),
        "vecs": f(col(a["L0_xattn_b_q"]), col(a["L0_xattn_b_k"]), col(a["L1_xattn_bq"]), col(a["L1_xattn_bk"]),
                  col(gx[0:1]), col(gx[1:2]), col(gf[0:1]), col(gf[1:2]), *quad, *row),
        "rows": c(np.broadcast_to(np.stack(rows, 0)[None], (P, 4, D))),
        "ident": np.eye(P, dtype=np.float32),
        "small": small,
        "mask": mask,
        "wr": c(np.stack([a["L0_ffn_Wg"], a["L1_ffn_router_w"].T], 1)),
        "w1a": c(a["L0_ffn_W1"].transpose(1, 0, 2)),
        "w1b": c(a["L1_ffn_w1"].transpose(1, 0, 2)),
        "w2a": c(a["L0_ffn_W2"].reshape(NE, HC, P, D).transpose(2, 0, 1, 3)),
        "w2b": c(a["L1_ffn_w2"].reshape(NE, HC, P, D).transpose(2, 0, 1, 3)),
        "b1": c(np.stack([a["L0_ffn_b1"].reshape(NE * HC, P).T, a["L1_ffn_b1"].reshape(NE * HC, P).T], 1)),
        "b2T": c(a["L1_ffn_b2"].T),
        "slot": c(np.broadcast_to(np.arange(SLOTS, dtype=np.float32), (P, SLOTS))),
        "b2": c(np.stack([a["L0_ffn_b2"], a["L1_ffn_b2"]], 1)),
    }


def kernel(**inputs):
    import concourse.bacc as bacc
    from concourse.bass_utils import run_bass_kernel_spmd

    arrays = lay_out(inputs)
    nc = bacc.Bacc("TRN2", target_bir_lowering=False, num_devices=1)
    t_in = {n: nc.dram_tensor("in_" + n, v.shape, mybir.dt.from_np(v.dtype), kind="ExternalInput").ap()
            for n, v in arrays.items()}
    out = nc.dram_tensor("out_x", (P, NT, D), F32, kind="ExternalOutput").ap()
    build(nc, t_in, out)
    r = run_bass_kernel_spmd(nc, [{"in_" + n: v for n, v in arrays.items()}], core_ids=[0])
    got = r.results[0]["out_x"]
    return np.ascontiguousarray(got.transpose(1, 0, 2)).reshape(NB, S, D)
```

```python
from contextlib import ExitStack
from functools import partial

import numpy as np
import concourse.bass as bass
from concourse import mybir

ALU = mybir.AluOpType
ACT = mybir.ActivationFunctionType
F32 = mybir.dt.float32
I32 = mybir.dt.int32
AX_X = mybir.AxisListType.X

P = 128
D = 128
NB, S = 128, 64
NT = NB * S // P
TG = 4
NG = NT // TG
GC = TG * P
HEADS, DH = 16, 8
QUADS = 4
PAIRS = HEADS // 2
NE, HID = 8, 512
HC = HID // P
CAP = max(1, int(S * 2.0 / NE) + 1)
SLOTS = 2 * CAP
TS = 8
NSG = NT // TS
BLOCK = 256
HALF = NT // 2
TOP = 2
NBLOCKS = (HALF * P * TOP + NE * (BLOCK - 1)) // BLOCK
BS = BLOCK // P
EPS = 1e-5
NEG = -1.0e9
OUTSIDE = -3.0e38


class Sem:

    def __init__(self, handle):
        self.handle, self.n = handle, 0


class Plan:

    ENGINES = ("sp", "act", "pe", "dve", "pool")

    def __init__(self):
        self.queue = {e: [] for e in self.ENGINES}
        self.seen = {}

    def do(self, engine, emit, sem=None, by=1):
        self.queue[engine].append((emit, sem, by))
        if sem is not None:
            sem.n += by
            return (sem, sem.n)
        return None

    def wait(self, engine, *events):
        for event in events:
            if event is None:
                continue
            sem, n = event
            if self.seen.get((engine, sem), 0) < n:
                self.seen[(engine, sem)] = n
                self.queue[engine].append((None, sem, n))

    def run(self, engine, handle):
        for emit, sem, n in self.queue[engine]:
            if emit is None:
                handle.wait_ge(sem.handle, n)
                continue
            ins = emit()
            if sem is not None:
                ins.then_inc(sem.handle, n)


class Bank:
    def __init__(self, ap):
        self.ap, self.free = ap, None


def build(nc, t_in, out):
    with ExitStack() as ctx:
        def sb(name, shape, dt=F32):
            return ctx.enter_context(nc.sbuf_tensor(name, shape, dt))

        def sem(name):
            return Sem(ctx.enter_context(nc.semaphore(name)))

        plan = Plan()
        do, wait = plan.do, plan.wait

        x_sb = sb("x_sb", [P, NT, D])
        ctx_sb = sb("ctx_sb", [D, NT * P])
        w_sb = sb("w_sb", [P, 8, D])
        wo1_sb = sb("wo1_sb", [P, D])
        vec_sb = sb("vec_sb", [P, t_in["vecs"].shape[1]])
        row_sb = sb("row_sb", [P, 4, D])
        ident = sb("ident", [P, P])
        small_sb = sb("small_sb", [P, 4, NE])
        mask_sb = sb("mask_sb", [P, 2, P])
        wr_sb = sb("wr_sb", [P, 2, NE])
        w1_sb = sb("w1_sb", [D, NE, HID])
        w2_sb = sb("w2_sb", [P, NE, HC, D])
        b1_sb = sb("b1_sb", [P, 2, NE * HC])
        b2_sb = sb("b2_sb", [P, NE, D])
        before_sb = sb("before_sb", [P, 2, P])
        block_sb = sb("block_sb", [1, NBLOCKS])
        b2T_sb = sb("b2T_sb", [D, NE])
        slot_sb = sb("slot_sb", [P, SLOTS])
        ln1 = sb("ln1", [P, 4, D])
        tg_sb = sb("tg_sb", [P, 4])
        tbo_sb = sb("tbo_sb", [P, 2, D])

        stats = sb("stats", [P, 16, 6])
        mv = sb("mv", [P, NT, 2])
        rstd = sb("rstd", [P, NT])
        half_v = sb("half_v", [P, 16])
        newton = sb("newton", [P, 16])
        ln_sb = sb("ln_sb", [P, 3, TG, D])
        lnT = sb("lnT", [D, 2, GC])
        work = sb("work", [P, 10880])

        def cut(at, shape, names):
            n = int(np.prod(list(shape.values())))
            return work[:, at:at + n].rearrange(f"p ({names}) -> p {names}", **shape)

        kx = cut(0, dict(i=2, b=2 * TG, j=QUADS, k=S), "i b j k")
        pr = cut(4096, dict(i=2, h=HEADS, k=S), "i h k")
        pT = cut(6144, dict(i=2, r=PAIRS, q=P), "i r q")
        qT = cut(8192, dict(i=2, n=GC), "i n")
        kT = cut(9216, dict(i=2, n=GC), "i n")
        vx = sb("vx", [P, 2, PAIRS, 2, 2, DH])
        mx = sb("mx", [P, 2, HEADS])
        den = sb("den", [P, 2, HEADS])
        rden = sb("rden", [P, 2, HEADS])
        rdm = sb("rdm", [P, 2, PAIRS, 2, 2, DH])
        ctxn = sb("ctxn", [P, 2, 2, P])
        hid0 = sb("hid0", [P, 2, HC, BLOCK])

        psum = ctx.enter_context(nc.psum_tensor("psum", [P, 8, 512], F32))
        banks = [Bank(psum[:, i, :]) for i in range(8)]

        V = {n: i for i, n in enumerate(["bq0", "bk0", "bq1", "bk1", "gx0", "gx1", "gf0", "gf1",
                                         "quad0", "quad1", "quad2", "quad3", "row0", "row1"])}

        def vec(name, n=1):
            return vec_sb[:, V[name]:V[name] + n]

        ld = {}

        def load(name, dst, src, eng="sp"):
            ld[name] = do(eng, partial((nc.sync if eng == "sp" else nc.scalar).dma_start, dst, src), sem("ld_" + name), 16)

        load("vecs", vec_sb[:], t_in["vecs"])
        load("ident", ident[:], t_in["ident"], "act")
        for g in range(4):
            load(f"x{g}", x_sb[:, TG * g:TG * g + TG, :], t_in["x"][:, TG * g:TG * g + TG, :])
            load(f"c{g}", ctx_sb[:, GC * g:GC * g + GC], t_in["ctxT"][:, GC * g:GC * g + GC], "act")
            if g == 0:
                load("w", w_sb[:], t_in["w"])
                load("rows", row_sb[:], t_in["rows"], "act")
        for g in range(1, 4):
            load(f"x{3 + g}", x_sb[:, 16 * g:16 * g + 16, :], t_in["x"][:, 16 * g:16 * g + 16, :])
            load(f"c{3 + g}", ctx_sb[:, 2048 * g:2048 * g + 2048],
                 t_in["ctxT"][:, 2048 * g:2048 * g + 2048], "act")
        load("wo1", wo1_sb[:], t_in["wo1"])
        load("small", small_sb[:], t_in["small"])
        load("mask", mask_sb[:], t_in["mask"])
        load("wr", wr_sb[:], t_in["wr"])
        load("w1", w1_sb[:], t_in["w1a"])
        load("w2", w2_sb[:], t_in["w2a"])
        load("b1", b1_sb[:], t_in["b1"])
        load("b2", b2_sb[:], t_in["b2"])
        load("before", before_sb[:], t_in["before"])
        load("block", block_sb[:], t_in["block"])
        load("b2T", b2T_sb[:], t_in["b2T"])
        load("slot", slot_sb[:], t_in["slot"])

        def xload(g):
            return ld[f"x{g}"] if g < 4 else ld[f"x{3 + g // 4}"]

        def cload(g):
            return ld[f"c{g}"] if g < 4 else ld[f"c{3 + g // 4}"]

        s_tg, s_tbo = sem("s_tg"), sem("s_tbo")
        wait("act", ld["vecs"])
        e_tg = do("act", partial(nc.scalar.activation, tg_sb[:], vec("gx0", 4), ACT.Tanh), s_tg)
        wait("dve", ld["vecs"], ld["rows"], e_tg)
        for l in range(2):
            e_tbo = do("dve", partial(nc.vector.tensor_scalar, tbo_sb[:, l, :], row_sb[:, 2 * l + 1, :],
                                                           tg_sb[:, l:l + 1], None, ALU.mult), s_tbo)
        TGX = [tg_sb[:, 0:1], tg_sb[:, 1:2]]
        TGF = [tg_sb[:, 2:3], tg_sb[:, 3:4]]

        s_st, s_mv, s_rs, s_ln = sem("s_st"), sem("s_mv"), sem("s_rs"), sem("s_ln")
        s_lt, s_lnT = sem("s_lt"), sem("s_lnT")
        ln_free = [None] * 3
        lnT_free = [None, None]

        def moments(lo, n, ready):
            wait("dve", *ready)
            for t in range(lo, lo + n):
                e = do("dve", partial(nc.vector.bn_stats, stats[:, t % 16, :], x_sb[:, t, :]), s_st)
            wait("dve", e)
            for t in range(lo, lo + n):
                e = do("dve", partial(nc.vector.bn_aggr, mv[:, t, :], stats[:, t % 16, :]), s_mv)
            wait("dve", e)

        def inverse_std(lo, n):
            def step(fn, counter=s_rs):
                wait("dve", do("dve", fn, counter))

            var, y, h, w = mv[:, lo:lo + n, 1], rstd[:, lo:lo + n], half_v[:, 0:n], newton[:, 0:n]
            step(partial(nc.vector.tensor_scalar, w, var, EPS, None, ALU.add))
            step(partial(nc.vector.tensor_scalar, h, w, -0.5, None, ALU.mult))
            step(partial(nc.vector.tensor_scalar, w.bitcast(I32), w.bitcast(I32), 1, None, ALU.arith_shift_right))
            step(partial(nc.vector.tensor_scalar, y.bitcast(I32), w.bitcast(I32), -1.0, float(0x5F3759DF), ALU.mult, ALU.add))
            for _ in range(3):
                step(partial(nc.vector.tensor_tensor, w, y, y, ALU.mult))
                step(partial(nc.vector.tensor_tensor, w, w, h, ALU.mult))
                step(partial(nc.vector.scalar_tensor_tensor, out=y, in0=w, scalar=1.5, in1=y, op0=ALU.add, op1=ALU.mult))

        def statistics(lo, n, ready):
            moments(lo, n, ready)
            inverse_std(lo, n)

        def norm(g, i):
            wait("dve", ln_free[i])
            for t in range(TG):
                tt = TG * g + t
                e = do("dve", partial(nc.vector.tensor_scalar, 
                    ln_sb[:, i, t, :], x_sb[:, tt, :], mv[:, tt, 0:1], rstd[:, tt:tt + 1],
                    ALU.subtract, ALU.mult), s_ln)
            return e

        def turn(g, j, e_ln, bank):
            i = g % 2
            wait("pe", ld["ident"], e_ln, bank.free)
            for t in range(TG):
                e = do("pe", partial(nc.tensor.transpose, bank.ap[:, t * P:t * P + P], ln_sb[:, j, t, :], ident[:]), s_lt)
            ln_free[j] = e
            wait("act", e, lnT_free[i])
            bank.free = do("act", partial(nc.scalar.copy, lnT[:, i, :], bank.ap), s_lnT)
            return bank.free

        s_q, s_qe, s_k, s_ke, s_kx = sem("s_q"), sem("s_qe"), sem("s_k"), sem("s_ke"), sem("s_kx")
        s_v, s_vx, s_sc, s_mx, s_sub, s_exp = (sem("s_v"), sem("s_vx"), sem("s_sc"), sem("s_mx"),
                                               sem("s_sub"), sem("s_exp"))
        s_den, s_rden, s_rdm, s_pt, s_pT = sem("s_den"), sem("s_rden"), sem("s_rdm"), sem("s_pt"), sem("s_pT")
        s_av, s_cn, s_o, s_x1, s_xb = sem("s_av"), sem("s_cn"), sem("s_o"), sem("s_x1"), sem("s_xb")
        s_zero = sem("s_zero")
        e_zero = do("pool", partial(nc.gpsimd.memset, vx[:], 0.0), s_zero)
        SCALE0 = float(1.0 / np.sqrt(np.float32(DH)))
        ev = {}
        B_S, B_T, B_C, B_P = [(0, 1), (2, 3)], (4, 5), 6, 7

        def project(name, g, w, src, e_src, dst, bias, sem_mm, sem_ev):
            bank = banks[B_P]
            wait("pe", ld["w"], *e_src, bank.free)
            e = do("pe", partial(nc.tensor.matmul, bank.ap, w, src, start=True, stop=True), sem_mm)
            wait("act", e, ld["vecs"])
            bank.free = do("act", partial(nc.scalar.activation, dst, bank.ap, ACT.Identity, bias=bias), sem_ev)
            return bank.free

        def prep_norm(g):
            if g == 0:
                statistics(0, TG, [xload(0)])
            elif g == 1 or g % 4 == 0:
                n = (4 - g % 4) * TG
                statistics(TG * g, n, [xload(k) for k in range(g, g + n // TG)])
            ev["ln", g] = norm(g, g % 2)
            wait("pool", e_tbo, ev["ln", g])
            ev["xb", g] = do("pool", partial(nc.gpsimd.tensor_tensor, 
                x_sb[:, TG * g:TG * g + TG, :], x_sb[:, TG * g:TG * g + TG, :],
                tbo_sb[:, 0:1, :].to_broadcast([P, TG, D]), ALU.add), s_xb)

        def prep_turn(g):
            ev["lnT", g] = turn(g, g % 2, ev["ln", g], banks[B_P])

        def prep_q(g):
            i = g % 2
            wait("act", ev.get(("sc", TG * (g - 2) + TG - 1)))
            ev["q", g] = project("q", g, w_sb[:, 0, :], lnT[:, i, :], [ev["lnT", g]], qT[:, i, :], vec("bq0"), s_q, s_qe)
            lnT_free[i] = ev["q", g]

        def prep_k(g):
            i = g % 2
            wait("act", ev.get(("kx", g - 2)))
            ev["k", g] = project("k", g, w_sb[:, 1, :], ctx_sb[:, g * GC:g * GC + GC], [cload(g)], kT[:, i, :],
                                 vec("bk0"), s_k, s_ke)
            wait("pool", ev["k", g], ev.get(("sc", TG * (g - 2) + TG - 1)))
            for j in range(QUADS):
                ev["kx", g] = do("pool", partial(nc.gpsimd.tensor_scalar, 
                    kx[:, i, :, j, :], kT[:, i, :].rearrange("p (b k) -> p b k", k=S),
                    vec(f"quad{j}"), 1.0, ALU.mult, ALU.mult), s_kx)

        def prep_v(t):
            bank = banks[B_P]
            wait("pe", ld["w"], cload(t // TG), bank.free)
            e = do("pe", partial(nc.tensor.matmul, bank.ap[:, 0:D], ctx_sb[:, t * P:t * P + P], w_sb[:, 2, :],
                                            start=True, stop=True), s_v)
            wait("dve", e, e_zero, ld["rows"], ev.get(("av", t - 2)))
            for hp in range(2):
                q = slice(64 * hp, 64 * hp + 64)
                for b in range(2):
                    src = bank.ap[64 * b:64 * b + 64, 0:D].rearrange("p (r h d) -> p r h d", r=PAIRS, h=2)
                    e = do("dve", partial(nc.vector.tensor_tensor, 
                        vx[q, t % 2, :, b, hp, :], src[:, :, hp, :],
                        row_sb[q, 0, :].rearrange("p (r h d) -> p r h d", r=PAIRS, h=2)[:, :, hp, :],
                        ALU.add), s_vx)
            ev["vx", t] = bank.free = e

        def scores(t):
            g, i = t // TG, (t // TG) % 2
            two = [banks[n] for n in B_S[t % 2]]
            wait("pe", ev["q", g], ev["kx", g], *[b.free for b in two])
            done = []
            for quad in range(QUADS):
                q = slice(32 * quad, 32 * quad + 32)
                if quad >= 2:
                    wait("pe", done[quad - 2])
                for b in range(2):
                    c = (t % TG) * P + b * S
                    dst = two[quad % 2].ap[64 * b:64 * b + 64, 256 * (quad // 2):256 * (quad // 2) + 256]
                    e = do("pe", partial(nc.tensor.matmul, 
                        dst, qT[q, i, c:c + S], kx[q, i, 2 * (t % TG) + b, :, :], start=True, stop=True), s_sc)
                done.append(e)
            ev["sc", t] = e

        def largest(t):
            two = B_S[t % 2]
            src = psum[:, two[0]:two[1] + 1, :].rearrange("p a (h k) -> p (a h) k", k=S)
            i = t % 2
            wait("dve", ev["sc", t], ev.get(("pt", t - 2)))
            e = do("dve", partial(nc.vector.tensor_reduce, mx[:, i, :], src, AX_X, ALU.max), s_mx)
            wait("dve", e)
            e = do("dve", partial(nc.vector.tensor_tensor, pr[:, i, :, :], src, mx[:, i, :].unsqueeze(2).to_broadcast([P, HEADS, S]),
                                                    ALU.subtract), s_sub)
            for n in two:
                banks[n].free = e
            ev["sub", t] = e

        def exponentials(t):
            i = t % 2
            wait("act", ev["sub", t])
            ev["exp", t] = do("act", partial(nc.scalar.activation, pr[:, i, :, :], pr[:, i, :, :], ACT.Exp, scale=SCALE0), s_exp)

        def denominators(t):
            i = t % 2
            wait("dve", ev["exp", t], ev.get(("av", t - 2)))
            e = do("dve", partial(nc.vector.tensor_reduce, den[:, i, :], pr[:, i, :, :], AX_X, ALU.add), s_den)
            wait("dve", e)
            e = do("dve", partial(nc.vector.reciprocal, rden[:, i, :], den[:, i, :]), s_rden)
            wait("dve", e)
            wait("pool", e)
            for b in range(2):
                e = do("pool", partial(nc.gpsimd.tensor_scalar, 
                    rdm[:, i, :, b, :, :],
                    rden[:, i, :].rearrange("p (r h) -> p r h", h=2).unsqueeze(3).to_broadcast([P, PAIRS, 2, DH]),
                    vec(f"row{b}"), 1.0, ALU.mult, ALU.mult), s_rdm)
            ev["rdm", t] = e

        def turn_p(t):
            i = t % 2
            wait("pe", ev["exp", t])
            for half in range(2):
                bank = banks[B_T[half]]
                wait("pe", bank.free)
                for r in range(4):
                    pair = 4 * half + r
                    e = do("pe", partial(nc.tensor.transpose, 
                        bank.ap[:, r * P:r * P + P], pr[:, i, 2 * pair:2 * pair + 2, :], ident[:]), s_pt)
                wait("act", e, ev.get(("av", t - 2)))
                bank.free = do("act", partial(nc.scalar.copy, 
                    pT[:, i, 4 * half:4 * half + 4, :], bank.ap), s_pT)
            ev["pt", t] = e
            ev["pT", t] = bank.free

        def attend(t):
            i = t % 2
            bank = banks[B_C]
            wait("pe", ev["pT", t], ev["vx", t], ev["rdm", t], bank.free)
            for pair in range(PAIRS):
                q = 32 * (pair % 4)
                dst = bank.ap[q:q + 32, (pair // 4) * P:(pair // 4) * P + P]
                do("pe", partial(nc.tensor.matmul, dst, vx[:, i, pair, :, :, :], pT[:, i, pair, :],
                                                              start=True, stop=True), s_av)
            for half in range(2):
                dst = bank.ap[:, 256 + half * P:256 + half * P + P]
                rep = rdm[:, i, 4 * half:4 * half + 4, :, :, :].rearrange("p r b h d -> p (r b h d)")
                e = do("pe", partial(nc.tensor.transpose, dst, rep, ident[:]), s_av)
            ev["av", t] = e
            wait("act", e, ev.get(("cn", t - 2)))
            e = do("act", partial(nc.scalar.copy, ctxn[:, i, :, :], bank.ap[:, 256:512].rearrange("p (a q) -> p a q", a=2)), s_rc)
            wait("dve", e, ev.get(("o", t - 2)))
            bank.free = ev["cn", t] = do("dve", partial(nc.vector.tensor_tensor, 
                ctxn[:, i, :, :], bank.ap[:, 0:256].rearrange("p (a q) -> p a q", a=2), ctxn[:, i, :, :], ALU.mult), s_cn)

        s_rc = sem("s_rc")

        def output(t):
            bank = banks[B_P]
            wait("pe", ev["cn", t], bank.free)
            for half in range(2):
                e = do("pe", partial(nc.tensor.matmul, bank.ap[:, 0:D], ctxn[:, t % 2, half, :], w_sb[:, 3 + half, :],
                                                         start=(half == 0), stop=(half == 1)), s_o)
            ev["o", t] = e
            wait("dve", e, ev["xb", t // TG])
            ev["x1", t] = bank.free = do("dve", partial(nc.vector.scalar_tensor_tensor, 
                out=x_sb[:, t, :], in0=bank.ap[:, 0:D], scalar=TGX[0], in1=x_sb[:, t, :],
                op0=ALU.mult, op1=ALU.add), s_x1)

        HG = HALF // TG
        NS = 16
        xg_dram = [nc.dram_tensor(f"xg{h}", (NBLOCKS * BLOCK, D), F32, kind="Internal").ap() for h in range(2)]
        yg_dram = [nc.dram_tensor(f"yg{h}", (NBLOCKS * BLOCK, D), F32, kind="Internal").ap() for h in range(2)]
        lg_sb = sb("lg_sb", [P, NT, NE])
        red = sb("red", [P, HALF])
        tmp = sb("tmp", [P, HALF, NE])
        left = sb("left", [P, HALF, NE])
        chosen = sb("chosen", [P, TOP + 1, HALF, NE])
        total = sb("total", [P, NE, HALF])
        upto = sb("upto", [P, NE, HALF])
        carry = sb("carry", [P, NE, HALF])
        nb = sb("nb", [P, 4, NE])
        nb_int = sb("nb_int", [P, NE], I32)
        owner = sb("owner", [1, NBLOCKS, NE])
        owner_sum = sb("owner_sum", [1, NBLOCKS])
        expert = sb("expert", [1, 2, NBLOCKS], I32)
        place_f = sb("place_f", [P, HALF])
        place = sb("place", [P, 2, TOP, HALF], mybir.dt.uint32)
        gate0 = sb("gate0", [P, 2, TOP, HALF])
        got_sb = cut(512, dict(i=4, k=TOP, d=D), "i k d")
        xg_sb = cut(2560, dict(i=3, s=BS, d=D), "i s d")
        xgT_sb = cut(3328, dict(i=2, n=BLOCK), "i n")
        yg_sb = sb("yg_sb", [P, 3, BS, D])
        w1g_sb = sb("w1g_sb", [D, 3, HID])
        s_lg, s_r, s_ex, s_count = sem("s_lg"), sem("s_r"), sem("s_ex"), sem("s_count")
        ones_row = sb("ones_row", [P, S])
        s_one = sem("s_one")
        e_one = do("pool", partial(nc.gpsimd.memset, ones_row[:], 1.0), s_one)
        e_carry = do("pool", partial(nc.gpsimd.memset, carry[:], 1.0), s_one)
        wait("pool", e_carry)
        e_carry = do("pool", partial(nc.gpsimd.memset, carry[:, :, 0:1], 0.0), s_one)
        e_fill0 = do("pool", partial(nc.gpsimd.memset, hid0[:], 0.0), s_one)
        s_fill = sem("s_fill")
        wait("act", e_fill0)
        zeros = hid0[:].rearrange("p i c n -> p (i c n)")
        per_row = NBLOCKS * BLOCK * D // P
        for h in range(2):
            rows = xg_dram[h].rearrange("(p n) d -> p (n d)", p=P)
            for at in range(0, per_row, zeros.shape[1]):
                n = min(zeros.shape[1], per_row - at)
                e_fill = do("act", partial(nc.scalar.dma_start, rows[:, at:at + n], zeros[:, 0:n]), s_fill, 16)

        def dve(fn, *w):
            wait("dve", *w)
            e = do("dve", fn, s_r)
            wait("dve", e)
            return e

        def router(layer, g, bank_turn, bank_lg):
            e_lnT = turn(g, 2, norm(g, 2), bank_turn)
            wait("pe", e_lnT, ld["wr"], bank_lg.free)
            for t in range(TG):
                e = do("pe", partial(nc.tensor.matmul, bank_lg.ap[:, NE * t:NE * t + NE], lnT[:, g % 2, t * P:t * P + P],
                                     wr_sb[:, layer, :], start=True, stop=True), s_lg)
            lnT_free[g % 2] = e
            return e, bank_lg.ap[:, 0:TG * NE].rearrange("p (t e) -> p t e", e=NE)

        def router0(g):
            e, src = router(0, g, banks[B_P], banks[B_P])
            banks[B_P].free = dve(partial(nc.vector.tensor_tensor, lg_sb[:, TG * g:TG * g + TG, :], src,
                                          small_sb[:, 0:1, :].to_broadcast([P, TG, NE]), ALU.add), e, ld["small"])

        def softmax8(lo, n):
            L, r = lg_sb[:, lo:lo + n, :], red[:, 0:n]
            bc = r.unsqueeze(2).to_broadcast([P, n, NE])
            dve(partial(nc.vector.tensor_reduce, r, L, AX_X, ALU.max))
            e = dve(partial(nc.vector.tensor_tensor, L, L, bc, ALU.subtract))
            wait("act", e)
            e = do("act", partial(nc.scalar.activation, L, L, ACT.Exp), s_ex)
            yield
            dve(partial(nc.vector.tensor_reduce, r, L, AX_X, ALU.add), e)
            dve(partial(nc.vector.reciprocal, r, r))
            ev["probabilities", lo] = dve(partial(nc.vector.tensor_tensor, L, L, bc, ALU.mult))
            yield

        def route0(h):
            lo = HALF * h
            yield from softmax8(lo, HALF)
            bc = red[:].unsqueeze(2).to_broadcast([P, HALF, NE])
            order = small_sb[:, 1:2, :].to_broadcast([P, HALF, NE])
            for k in range(TOP):
                src = lg_sb[:, lo:lo + HALF, :] if k == 0 else left[:]
                dve(partial(nc.vector.tensor_reduce, red[:], src, AX_X, ALU.max))
                dve(partial(nc.vector.tensor_scalar, gate0[:, h, k, :], red[:], TGF[0], None, ALU.mult))
                dve(partial(nc.vector.tensor_tensor, tmp[:], src, bc, ALU.is_equal))
                yield
                dve(partial(nc.vector.tensor_tensor, tmp[:], tmp[:], order, ALU.mult))
                dve(partial(nc.vector.tensor_reduce, red[:], tmp[:], AX_X, ALU.max))
                dve(partial(nc.vector.tensor_tensor, chosen[:, k, :, :], tmp[:], bc, ALU.is_equal))
                if k == 0:
                    dve(partial(nc.vector.scalar_tensor_tensor, out=left[:], in0=chosen[:, 0, :, :], scalar=-2.0,
                                in1=src, op0=ALU.mult, op1=ALU.add))
                yield
            e = dve(partial(nc.vector.tensor_tensor, chosen[:, TOP, :, :], chosen[:, 0, :, :], chosen[:, 1, :, :], ALU.add))
            bank = banks[B_P]
            wait("pe", e, ld["before"], bank.free)
            for k in range(2):
                e = do("pe", partial(nc.tensor.matmul, bank.ap[:, k * HALF * NE:(k + 1) * HALF * NE], before_sb[:, k, :],
                                     chosen[:, TOP, :, :].rearrange("p t e -> p (t e)"), start=True, stop=True), s_count)
            ahead = bank.ap[:, 0:HALF * NE].rearrange("p (t e) -> p t e", e=NE)
            dve(partial(nc.vector.tensor_copy, total[:], bank.ap[:, HALF * NE:2 * HALF * NE].rearrange("p (t e) -> p e t", e=NE)), e)
            bank.free = dve(partial(nc.vector.tensor_copy, tmp[:], ahead))
            yield
            dve(partial(nc.vector.tensor_tensor_scan, out=upto[:].rearrange("p e t -> p (e t)"),
                        data0=carry[:].rearrange("p e t -> p (e t)"), data1=total[:].rearrange("p e t -> p (e t)"),
                        initial=0.0, op0=ALU.mult, op1=ALU.add), e_carry, e_one)
            dve(partial(nc.vector.tensor_scalar, nb_int[:], upto[:, :, HALF - 1], float(BLOCK - 1), None, ALU.add))
            dve(partial(nc.vector.tensor_scalar, nb_int[:], nb_int[:], int(np.log2(BLOCK)), None, ALU.arith_shift_right))
            dve(partial(nc.vector.tensor_copy, nb[:, 1, :], nb_int[:]))
            dve(partial(nc.vector.tensor_tensor_scan, out=nb[:, 2, :], data0=ones_row[:, 0:NE], data1=nb[:, 1, :],
                        initial=0.0, op0=ALU.mult, op1=ALU.add))
            dve(partial(nc.vector.tensor_tensor, nb[:, 3, :], nb[:, 2, :], nb[:, 1, :], ALU.subtract))
            yield
            dve(partial(nc.vector.tensor_tensor, total[:], upto[:], total[:], ALU.subtract))
            dve(partial(nc.vector.scalar_tensor_tensor, out=upto[:], in0=nb[:, 3, :].unsqueeze(2).to_broadcast([P, NE, HALF]),
                        scalar=float(BLOCK), in1=total[:], op0=ALU.mult, op1=ALU.add))
            dve(partial(nc.vector.tensor_tensor, left[:], tmp[:], upto[:].rearrange("p e t -> p t e"), ALU.add))
            for k in range(TOP):
                dve(partial(nc.vector.tensor_tensor, tmp[:], chosen[:, k, :, :], left[:], ALU.mult))
                dve(partial(nc.vector.tensor_reduce, place_f[:], tmp[:], AX_X, ALU.add))
                ev["place", h] = dve(partial(nc.vector.tensor_copy, place[:, h, k, :], place_f[:]))
                yield
            dve(partial(nc.vector.tensor_tensor, owner[:], nb[0:1, 2, :].unsqueeze(1).to_broadcast([1, NBLOCKS, NE]),
                        block_sb[:].unsqueeze(2).to_broadcast([1, NBLOCKS, NE]), ALU.is_le), ld["block"])
            dve(partial(nc.vector.tensor_reduce, owner_sum[:], owner[:], AX_X, ALU.add))
            ev["expert", h] = dve(partial(nc.vector.tensor_scalar, expert[:, h, :], owner_sum[:], float(NE - 1), None, ALU.min))
            yield

        s_lnp = sem("s_lnp")
        s_put = [sem(f"s_put{i}") for i in range(4)]
        s_get = [sem(f"s_get{i}") for i in range(4)]
        s_comb = sem("s_comb")
        nc_rows = NBLOCKS * BLOCK - 1

        def put0(t):
            h, i = t // HALF, t % 4
            wait("dve", ev.get(("put", t - 4)))
            e = do("dve", partial(nc.vector.tensor_scalar, ln1[:, i, :], x_sb[:, t, :], mv[:, t, 0:1], rstd[:, t:t + 1],
                                  ALU.subtract, ALU.mult), s_lnp)
            wait("pool", e, e_fill, ev["place", h])
            for k in range(TOP):
                at = bass.IndirectOffsetOnAxis(ap=place[:, h, k, t % HALF:t % HALF + 1], axis=0)
                ev["put", t] = do("pool", partial(nc.gpsimd.indirect_dma_start, xg_dram[h], at, ln1[:, i, :], None,
                                                  bounds_check=nc_rows, oob_is_err=False), s_put[i], 16)

        def work0(h):
            yield from route0(h)
            for t in range(HALF * h, HALF * h + HALF):
                put0(t)
                yield

        def get0(t):
            h, i = t // HALF, t % 4
            wait("pool", *[ev["stored", h, n] for n in range(3)], ev.get(("x2", t - 4)))
            for k in range(TOP):
                at = bass.IndirectOffsetOnAxis(ap=place[:, h, k, t % HALF:t % HALF + 1], axis=0)
                ev["got", t] = do("pool", partial(nc.gpsimd.indirect_dma_start, got_sb[:, i, k, :], None, yg_dram[h], at,
                                                  bounds_check=nc_rows, oob_is_err=False), s_get[i], 16)

        def combine0(t):
            h, i = t // HALF, t % 4
            for n in range(t + 3 if t % HALF else t, min(t + 4, HALF * h + HALF)):
                get0(n)
            wait("dve", ev["got", t])
            for k in range(TOP):
                e = do("dve", partial(nc.vector.scalar_tensor_tensor, out=x_sb[:, t, :], in0=got_sb[:, i, k, :],
                                      scalar=gate0[:, h, k, t % HALF:t % HALF + 1], in1=x_sb[:, t, :],
                                      op0=ALU.mult, op1=ALU.add), s_comb)
                wait("dve", e)
            ev["x2", t] = e

        for f in (prep_norm, prep_turn, prep_q, prep_k):
            f(0)
        side = iter(())
        for t in range(NT + 2):
            g, r = t // TG + 1, t % TG
            if 0 <= t - 1 < NT:
                denominators(t - 1)
                prep_v(t - 1)
            if t < NT:
                scores(t)
                if r == 0 and g < NG:
                    prep_norm(g)
                largest(t)
            if 0 <= t - 2 < NT:
                attend(t - 2)
            if r > 0 and g < NG:
                (prep_turn, prep_q, prep_k)[r - 1](g)
            if t < NT:
                exponentials(t)
            if 0 <= t - 1 < NT:
                turn_p(t - 1)
            if 0 <= t - 2 < NT:
                output(t - 2)
            if r == TG - 1 and g - 1 >= 2:
                if (g - 1) % 2 == 0:
                    statistics(TG * (g - 3), 2 * TG, [ev["x1", TG * (g - 3) + n] for n in range(2 * TG)])
                router0(g - 3)
            if g - 3 == HG and r == 0:
                side = work0(0)
            for _ in range(2):
                next(side, None)

        s_w1g = [sem(f"s_w1g{i}") for i in range(3)]
        s_xg = [sem(f"s_xg{i}") for i in range(3)]
        s_yg = [sem(f"s_yg{i}") for i in range(3)]
        s_xt, s_xT, s_up, s_hg, s_dn, s_yb = sem("s_xt"), sem("s_xT"), sem("s_up"), sem("s_hg"), sem("s_dn"), sem("s_yb")
        number = {}

        def read_expert(engine, h, j):
            def emit():
                handle = {"sp": nc.sync, "act": nc.scalar, "pe": nc.tensor, "dve": nc.vector}[engine]
                number[engine] = handle.value_load(expert[0:1, h, j:j + 1], min_val=0, max_val=NE - 1)
            wait(engine, ev["expert", h])
            do(engine, emit)

        def fetch(h, j):
            i = j % 3
            read_expert("sp", h, j)
            wait("sp", ld["w1"], ev.get(("up0", h, j - 3)), ev.get(("up0", h - 1, NBLOCKS - 1)))
            ev["w1_read", i] = ev["w1g", h, j] = do("sp", lambda: nc.sync.dma_start(
                w1g_sb[:, i, :], w1_sb[:, bass.ds(number["sp"], 1), :].rearrange("p a n -> p (a n)")), s_w1g[i], 16)
            wait("sp", *[ev["put", HALF * h + HALF - 1 - n] for n in range(4)], ev.get(("xt", h, j - 3)), ev.get(("xt", h - 1, NBLOCKS - 1)))
            ev["xg", h, j] = do("sp", partial(
                nc.sync.dma_start, xg_sb[:, i, :, :],
                xg_dram[h][j * BLOCK:j * BLOCK + BLOCK, :].rearrange("(s p) d -> p s d", p=P)), s_xg[i], 16)

        def turn0(h, j):
            bank = banks[4]
            wait("pe", ev["xg", h, j], bank.free)
            for n in range(BS):
                e = do("pe", partial(nc.tensor.transpose, bank.ap[:, n * P:n * P + P], xg_sb[:, j % 3, n, :], ident[:]), s_xt)
            ev["xt", h, j] = e
            wait("dve", e, ev.get(("up0", h, j - 2)), ev.get(("up0", h - 1, NBLOCKS - 1)))
            bank.free = ev["xT", h, j] = do("dve", partial(nc.vector.tensor_copy, xgT_sb[:, j % 2, :], bank.ap[:, 0:BLOCK]), s_xT)

        def up0(h, j):
            read_expert("act", h, j)
            for c in range(HC):
                bank = banks[(HC * j + c) % 3]
                wait("pe", ev["xT", h, j], ev["w1g", h, j], bank.free)
                e = do("pe", partial(nc.tensor.matmul, bank.ap[:, 0:BLOCK], w1g_sb[:, j % 3, c * P:c * P + P], xgT_sb[:, j % 2, :],
                                     start=True, stop=True), s_up)
                wait("act", e, ld["b1"], e_fill, ev.get(("down0", h, j - 2)), ev.get(("down0", h - 1, NBLOCKS - 1)))

                def emit(c=c, bank=bank):
                    bias = b1_sb[:, 0, :].rearrange("p (e c) -> p e c", c=HC)[:, bass.ds(number["act"], 1), c]
                    return nc.scalar.activation(hid0[:, j % 2, c, :], bank.ap[:, 0:BLOCK], ACT.Gelu, bias=bias)
                bank.free = ev["hid0", h, j] = do("act", emit, s_hg)
            ev["up0", h, j] = e

        def down0(h, j):
            i, bank = j % 3, banks[3]
            read_expert("pe", h, j)
            read_expert("dve", h, j)
            wait("pe", ev["hid0", h, j], ld["w2"], bank.free)
            for n in range(BS):
                for c in range(HC):
                    e = do("pe", lambda n=n, c=c: nc.tensor.matmul(
                        bank.ap[:, n * D:n * D + D], hid0[:, j % 2, c, n * P:n * P + P],
                        w2_sb[:, bass.ds(number["pe"], 1), c, :].rearrange("p a d -> p (a d)"),
                        start=(c == 0), stop=(c == HC - 1)), s_dn)
            ev["down0", h, j] = e
            wait("dve", e, ld["b2"], ev.get(("stored", h, i)), ev.get(("stored", h - 1, i)))
            bank.free = e = do("dve", lambda: nc.vector.tensor_tensor(
                yg_sb[:, i, :, :], bank.ap[:, 0:BS * D].rearrange("p (n d) -> p n d", d=D),
                b2_sb[:, bass.ds(number["dve"], 1), :].to_broadcast([P, BS, D]), ALU.add), s_yb)
            wait("sp", e)
            ev["stored", h, i] = do("sp", partial(
                nc.sync.dma_start, yg_dram[h][j * BLOCK:j * BLOCK + BLOCK, :].rearrange("(s p) d -> p s d", p=P),
                yg_sb[:, i, :, :]), s_yg[i], 16)

        def rest_of_routing():
            statistics(NT - 2 * TG, 2 * TG, [ev["x1", NT - 2 * TG + n] for n in range(2 * TG)])
            yield
            for g in range(NG - 2, NG):
                router0(g)
                yield
            yield from work0(1)

        def combine_half(h):
            for t in range(HALF * h, HALF * h + HALF):
                combine0(t)
                yield

        for _ in side:
            pass
        for engine in ("sp", "dve", "pool"):
            wait(engine, ev["sc", NT - 1])
        for h in range(2):
            side = rest_of_routing() if h == 0 else combine_half(0)
            for j in range(2):
                fetch(h, j)
            turn0(h, 0)
            for j in range(NBLOCKS + 1):
                if j + 2 < NBLOCKS:
                    fetch(h, j + 2)
                if j + 1 < NBLOCKS:
                    turn0(h, j + 1)
                if j < NBLOCKS:
                    up0(h, j)
                for _ in range(2):
                    next(side, None)
                if j > 0:
                    down0(h, j - 1)
            for _ in side:
                pass

        wait("sp", *[ev["w1_read", k] for k in range(3)], ev["down0", 1, NBLOCKS - 1])
        load("w1_1", w1_sb[:], t_in["w1b"])
        load("w2_1", w2_sb[:], t_in["w2b"])
        ld["w1"], ld["w2"] = ld["w1_1"], ld["w2_1"]

        s1 = {n: sem("s1_" + n) for n in ["v", "ve", "s", "t", "m", "n", "e", "r", "pt", "pT", "c", "cT", "o", "x", "xb"]}
        SCALE1 = float(1.0 / np.sqrt(np.float32(D)))
        kT1 = kx.rearrange("p i b j k -> p i (b j k)")[:, :, 0:GC]
        v1 = cut(9216, dict(i=2, t=TG, d=D), "i t d")
        masked = cut(4096, dict(i=2, t=TG, k=P), "i t k")
        pT1 = cut(6144, dict(i=2, n=GC), "i n")
        cT1 = cut(7168, dict(i=2, n=GC), "i n")
        sm = sb("sm", [P, 2, 3, TG])

        def prep1(g):
            if g % 4 == 0:
                inverse_std(TG * g, 4 * TG)
            ev["ln1", g] = norm(g, g % 2)
            wait("pool", e_tbo, ev["ln1", g])
            ev["xb1", g] = do("pool", partial(nc.gpsimd.tensor_tensor,
                x_sb[:, TG * g:TG * g + TG, :], x_sb[:, TG * g:TG * g + TG, :],
                tbo_sb[:, 1:2, :].to_broadcast([P, TG, D]), ALU.add), s1["xb"])

        def project1(g, w, src, e_src, dst, bias, bank, sem_mm, sem_ev):
            wait("pe", e_src, bank.free)
            e = do("pe", partial(nc.tensor.matmul, bank.ap, w, src, start=True, stop=True), sem_mm)
            wait("act", e)
            bank.free = do("act", partial(nc.scalar.activation, dst, bank.ap, ACT.Identity, bias=bias), sem_ev)
            return e, bank.free

        def q1(g):
            i = g % 2
            wait("act", ev.get(("s1", g - 2)))
            lnT_free[i], ev["q1", g] = project1(g, w_sb[:, 5, :], lnT[:, i, :], ev["lnT1", g], qT[:, i, :], vec("bq1"), banks[7], s_q, s_qe)

        def k1(g):
            _, ev["k1", g] = project1(g, w_sb[:, 6, :], ctx_sb[:, g * GC:g * GC + GC], None, kT1[:, g % 2, :], vec("bk1"), banks[6], s_k, s_ke)

        def values1(g):
            i, bank = g % 2, banks[2]
            wait("pe", bank.free)
            for t in range(TG):
                c = (TG * g + t) * P
                e = do("pe", partial(nc.tensor.matmul, bank.ap[:, t * D:t * D + D], ctx_sb[:, c:c + P], w_sb[:, 7, :], start=True, stop=True), s1["v"])
            wait("dve", e, ev.get(("c1", g - 2)))
            bank.free = ev["v1", g] = do("dve", partial(nc.vector.tensor_tensor, v1[:, i, :, :], bank.ap.rearrange("p (t d) -> p t d", d=D),
                                                       row_sb[:, 2:3, :].to_broadcast([P, TG, D]), ALU.add), s1["ve"])

        def scores1(g):
            i, bank = g % 2, banks[g % 2]
            wait("pe", ev["q1", g], ev["k1", g], bank.free)
            for c in range(0, GC, P):
                e = do("pe", partial(nc.tensor.matmul, bank.ap[:, c:c + P], qT[:, i, c:c + P], kT1[:, i, c:c + P], start=True, stop=True), s1["s"])
            ev["s1", g] = e

        def mask1(g):
            i, bank = g % 2, banks[g % 2]
            m = masked[:, i, :, :]
            wait("dve", ev["s1", g], ld["mask"], ev.get(("pt1", g - 2)))
            bank.free = e = do("dve", partial(nc.vector.scalar_tensor_tensor,
                out=m, in0=bank.ap.rearrange("p (t k) -> p t k", k=P), scalar=SCALE1,
                in1=mask_sb[:, 0:1, :].to_broadcast([P, TG, P]), op0=ALU.mult, op1=ALU.mult), s1["t"])
            wait("dve", e)
            e = do("dve", partial(nc.vector.tensor_tensor, m, m, mask_sb[:, 1:2, :].to_broadcast([P, TG, P]), ALU.add), s1["m"])
            wait("dve", e, ev.get(("x3", TG * (g - 2))))
            ev["max1", g] = do("dve", partial(nc.vector.tensor_reduce, sm[:, i, 0, :], m, AX_X, ALU.max, negate=True), s1["n"])

        def exponentials1(g, tiles):
            i = g % 2
            wait("act", ev["max1", g])
            for t in tiles:
                ev["e1", g] = do("act", partial(nc.scalar.activation, masked[:, i, t, :], masked[:, i, t, :], ACT.Exp,
                                                bias=sm[:, i, 0, t:t + 1], accum_out=sm[:, i, 1, t:t + 1]), s1["e"])

        def denominators1(g):
            i = g % 2
            wait("dve", ev["e1", g])
            e = do("dve", partial(nc.vector.reciprocal, sm[:, i, 2, :], sm[:, i, 1, :]), s1["r"])
            wait("dve", e)
            ev["r1", g] = do("dve", partial(nc.vector.tensor_scalar, sm[:, i, 2, :], sm[:, i, 2, :], TGX[1], None, ALU.mult), s1["r"])

        def turn1(g):
            i, bank = g % 2, banks[3]
            wait("pe", ev["e1", g], bank.free)
            for t in range(TG):
                e = do("pe", partial(nc.tensor.transpose, bank.ap[:, t * P:t * P + P], masked[:, i, t, :], ident[:]), s1["pt"])
            ev["pt1", g] = e
            wait("act", e, ev.get(("c1", g - 2)))
            bank.free = ev["pT1", g] = do("act", partial(nc.scalar.copy, pT1[:, i, :], bank.ap), s1["pT"])

        def attend1(g):
            i, bank = g % 2, banks[4]
            wait("pe", ev["pT1", g], ev["v1", g], bank.free)
            for t in range(TG):
                e = do("pe", partial(nc.tensor.matmul, bank.ap[:, t * P:t * P + P], v1[:, i, t, :], pT1[:, i, t * P:t * P + P],
                                     start=True, stop=True), s1["c"])
            ev["c1", g] = e
            wait("act", e, ev.get(("o1", g - 2)))
            bank.free = ev["cT1", g] = do("act", partial(nc.scalar.copy, cT1[:, i, :], bank.ap), s1["cT"])

        def output1(g):
            i, bank = g % 2, banks[5]
            wait("pe", ev["cT1", g], ld["wo1"], bank.free)
            for t in range(TG):
                e = do("pe", partial(nc.tensor.matmul, bank.ap[:, t * D:t * D + D], cT1[:, i, t * P:t * P + P], wo1_sb[:], start=True, stop=True), s1["o"])
            ev["o1", g] = e
            wait("dve", e, ev["xb1", g], ev["r1", g])
            for t in range(TG):
                tt = TG * g + t
                ev["x3", tt] = bank.free = do("dve", partial(nc.vector.scalar_tensor_tensor,
                    out=x_sb[:, tt, :], in0=bank.ap[:, t * D:t * D + D], scalar=sm[:, i, 2, t:t + 1], in1=x_sb[:, tt, :],
                    op0=ALU.mult, op1=ALU.add), s1["x"])

        def attention1(side):
            def moments1(g):
                if g < NG:
                    moments(TG * g, TG, [ev["x2", TG * g + t] for t in range(TG)])

            for g in range(4):
                moments1(g)
            for u in range(-2, NG + 1):
                if u == 6:
                    side = side()
                here, last = 0 <= u < NG, 0 <= u - 1 < NG
                if 0 <= u + 1 < NG:
                    ev["lnT1", u + 1] = turn(u + 1, (u + 1) % 2, ev["ln1", u + 1], banks[6])
                if here:
                    mask1(u)
                if last:
                    turn1(u - 1)
                if here:
                    exponentials1(u, range(2))
                if 0 <= u + 1 < NG:
                    q1(u + 1)
                if here:
                    exponentials1(u, range(2, TG))
                if last:
                    attend1(u - 1)
                if 0 <= u + 1 < NG:
                    k1(u + 1)
                    values1(u + 1)
                if u >= -1:
                    moments1(u + 5)
                if 0 <= u + 2 < NG:
                    prep1(u + 2)
                if here:
                    denominators1(u)
                if last:
                    output1(u - 1)
                if 0 <= u + 1 < NG:
                    scores1(u + 1)
                if 0 <= u < HG:
                    for n in range(TG):
                        combine0(HALF + TG * u + n)
                if u >= 6:
                    for _ in range(4):
                        next(side, None)
            return side
        scores_r = sb("scores_r", [P, 2, S])
        left_r = sb("left_r", [P, 2, S])
        mask_r = sb("mask_r", [P, 2, S])
        both_r = sb("both_r", [P, 2, 2, S])
        count_r = sb("count_r", [P, 2, S])
        top = sb("top", [P, 3, 8])
        gp = chosen[:, 0:2, :, :].rearrange("p a t e -> p (a t e)").rearrange("p (i k t e) -> p i k t e", i=2, k=2, t=NS)
        n_pt, n_pk = 2 * TS * 3 * P, 2 * NE * SLOTS
        pickT = ctx_sb[:, 0:n_pt].rearrange("p (i t k q) -> p i t k q", i=2, t=TS, k=3)
        pick, pickg = [ctx_sb[:, n_pt + n * n_pk:n_pt + (n + 1) * n_pk].rearrange("p (i e s) -> p i e s", i=2, e=NE)
                       for n in range(2)]
        yr = ctx_sb[:, n_pt + 2 * n_pk:n_pt + 2 * n_pk + 6 * D].rearrange("p (i k d) -> p i k d", i=2, k=3)
        n_xg = TS * NE * SLOTS
        xgT = [cut(n_xg * i, dict(e=NE, t=TS, s=SLOTS), "e t s") for i in range(2)]
        yT = [cut(n_xg * (2 + i), dict(t=TS, e=NE, s=SLOTS), "t e s") for i in range(2)]
        hid = cut(n_xg * 4, dict(i=2, c=HC, t=TS, s=SLOTS), "i c t s")
        KS = [(0, 3), (3, 6), (6, 8)]
        z = {n: sem("z_" + n) for n in ["tr", "tb", "gp", "pk", "pg", "ga", "xg", "pt", "pT", "up", "hg", "dn", "y",
                                        "yt", "yr", "sc", "x"]}

        def route1(lo):
            for g in range(lo // TG, lo // TG + 4):
                if g % 4 == 0:
                    statistics(TG * g, 16, [ev["x3", TG * g + t] for t in range(16)])
                    yield
                e, src = router(1, g, banks[7], banks[6])
                banks[6].free = dve(partial(nc.vector.tensor_copy, lg_sb[:, TG * g:TG * g + TG, :], src), e)
                yield
            L = lg_sb[:, lo:lo + NS, :]
            yield from softmax8(lo, NS)
            bank = banks[6]
            wait("pe", ev["probabilities", lo], bank.free)
            e = do("pe", partial(nc.tensor.transpose, bank.ap[:, 0:P], L.rearrange("p t e -> p (t e)"), ident[:]), z["tr"])
            src = bank.ap[:, 0:P].rearrange("p (b k) -> p b k", k=S)
            wait("dve", e)
            do("dve", partial(nc.vector.tensor_copy, scores_r[:], src), s_r)
            bank.free = dve(partial(nc.vector.tensor_copy, left_r[:], src))
            yield
            for b in range(2):
                a, w, m, c = scores_r[:, b, :], left_r[:, b, :], mask_r[:, b, :], count_r[:, b, :]
                for k in range(CAP // 8):
                    dve(partial(nc.vector.max, top[:, k, :], w))
                    dve(partial(nc.vector.match_replace, out=w, in_to_replace=top[:, k, :], in_values=w, imm_value=-1.0))
                    yield
                dve(partial(nc.vector.max, top[:, 2, :], w))
                dve(partial(nc.vector.tensor_scalar, m, w, top[:, 2, 0:1], None, ALU.is_equal))
                dve(partial(nc.vector.tensor_tensor_scan, out=c, data0=ones_row[:], data1=m, initial=0.0,
                            op0=ALU.mult, op1=ALU.add), e_one)
                dve(partial(nc.vector.scalar_tensor_tensor, out=m, in0=c, scalar=1.0, in1=m, op0=ALU.is_equal, op1=ALU.mult))
                dve(partial(nc.vector.scalar_tensor_tensor, out=m, in0=w, scalar=0.0, in1=m, op0=ALU.is_lt, op1=ALU.add))
                yield
                dve(partial(nc.vector.scalar_tensor_tensor, out=both_r[:, 0, b, :], in0=a, scalar=TGF[1], in1=m,
                            op0=ALU.mult, op1=ALU.mult))
                dve(partial(nc.vector.tensor_tensor_scan, out=c, data0=ones_row[:], data1=m, initial=float(CAP * b),
                            op0=ALU.mult, op1=ALU.add))
                dve(partial(nc.vector.tensor_tensor, c, c, m, ALU.mult))
                e = dve(partial(nc.vector.tensor_scalar, both_r[:, 1, b, :], c, -1.0, None, ALU.add))
                yield
            wait("pe", e, bank.free)
            for k in range(2):
                e = do("pe", partial(nc.tensor.transpose, bank.ap[:, k * P:k * P + P],
                                     both_r[:, k, :, :].rearrange("p b k -> p (b k)"), ident[:]), z["tb"])
            h = (lo // NS) % 2
            wait("dve", e, ev.get(("pickg", lo - NS - 1)))
            ev["gp", lo] = bank.free = do("dve", partial(
                nc.vector.tensor_copy, gp[:, h, :, :, :], bank.ap[:, 0:2 * P].rearrange("p (k t e) -> p k t e", k=2, e=NE)), z["gp"])

        def pick1(t):
            i, h = t % 2, (t // NS) % 2
            place = gp[:, h, 1, t % NS, :].unsqueeze(2).to_broadcast([P, NE, SLOTS])
            gate = gp[:, h, 0, t % NS, :].unsqueeze(2).to_broadcast([P, NE, SLOTS])
            wait("dve", ev["gp", t // NS * NS], ld["slot"], ev.get(("ga", t - 2)), ev.get(("pickg", t - 2)))
            e = do("dve", partial(nc.vector.tensor_tensor, pick[:, i, :, :], slot_sb[:].unsqueeze(1).to_broadcast([P, NE, SLOTS]),
                                  place, ALU.is_equal), z["pk"])
            wait("pool", e, ev.get(("pt", t - 2)))
            ev["pickg", t] = do("pool", partial(nc.gpsimd.tensor_tensor, pickg[:, i, :, :], pick[:, i, :, :], gate, ALU.mult), z["pg"])
            ev["pick", t] = do("dve", partial(nc.vector.tensor_scalar, ln1[:, i, :], x_sb[:, t, :], mv[:, t, 0:1], rstd[:, t:t + 1],
                                              ALU.subtract, ALU.mult), z["pk"])

        def gather(t):
            sg, i, bank = t // TS, t % 2, banks[4]
            wait("pe", ev["pick", t], bank.free)
            ev["ga", t] = e = do("pe", partial(nc.tensor.matmul, bank.ap[:, 0:NE * SLOTS], ln1[:, i, :],
                                               pick[:, i, :, :].rearrange("p e s -> p (e s)"), start=True, stop=True), z["ga"])
            wait("act", e, ev.get(("up", sg - 2)))
            ev["xg1", sg] = bank.free = do("act", partial(
                nc.scalar.copy, xgT[sg % 2][:, :, t % TS, :], bank.ap[:, 0:NE * SLOTS].rearrange("p (e s) -> p e s", s=SLOTS)), z["xg"])

        def turn_pick(t):
            sg, i, bank = t // TS, t % 2, banks[5]
            wait("pe", ev["pickg", t], bank.free)
            for k, (a, b) in enumerate(KS):
                ev["pt", t] = e = do("pe", partial(
                    nc.tensor.transpose, bank.ap[0:(b - a) * SLOTS, k * P:k * P + P],
                    pickg[:, i, a:b, :].rearrange("p e s -> p (e s)"), ident[:]), z["pt"])
            wait("dve", e, ev.get(("sc", t - 2 * TS)))
            rows = KS[0][1] * SLOTS
            do("dve", partial(nc.vector.tensor_copy, pickT[0:rows, sg % 2, t % TS, 0:2, :],
                              bank.ap[0:rows, 0:2 * P].rearrange("p (k q) -> p k q", q=P)), z["pT"])
            rows = (KS[2][1] - KS[2][0]) * SLOTS
            bank.free = ev["pT", t] = do("dve", partial(nc.vector.tensor_copy, pickT[0:rows, sg % 2, t % TS, 2, :],
                                                       bank.ap[0:rows, 2 * P:3 * P]), z["pT"])

        def up1(sg, ex):
            for c in range(HC):
                bank = banks[(HC * ex + c) % 3]
                wait("pe", ev["xg1", sg], ld["w1"], bank.free)
                e = do("pe", partial(nc.tensor.matmul, bank.ap[:, 0:TS * SLOTS], w1_sb[:, ex, c * P:c * P + P],
                                     xgT[sg % 2][:, ex, :, :].rearrange("p t s -> p (t s)"), start=True, stop=True), z["up"])
                wait("act", e, ld["b1"], ev.get(("dn", ex % 2)))
                ev["hg", ex % 2] = bank.free = do("act", partial(
                    nc.scalar.activation, hid[:, ex % 2, c, :, :].rearrange("p t s -> p (t s)"), bank.ap[:, 0:TS * SLOTS],
                    ACT.Gelu, bias=b1_sb[:, 1, ex * HC + c:ex * HC + c + 1]), z["hg"])
            ev["up", sg] = e

        def down1(sg, ex):
            bank = banks[3]
            wait("pe", ev["hg", ex % 2], ld["w2"], bank.free)
            for c in range(HC):
                e = do("pe", partial(nc.tensor.matmul, bank.ap[:, 0:TS * SLOTS], w2_sb[:, ex, c, :],
                                     hid[:, ex % 2, c, :, :].rearrange("p t s -> p (t s)"), start=(c == 0), stop=(c == HC - 1)), z["dn"])
            ev["dn", ex % 2] = e
            wait("dve", e, ld["b2T"], ev.get(("yt", (sg - 1) * TS - 1)))
            ev["y", sg] = bank.free = do("dve", partial(
                nc.vector.tensor_scalar, yT[sg % 2][:, :, ex, :], bank.ap[:, 0:TS * SLOTS].rearrange("p (t s) -> p t s", s=SLOTS),
                b2T_sb[:, ex:ex + 1], None, ALU.add), z["y"])

        def turn_results(t):
            sg, i, bank = t // TS, t % 2, banks[6]
            wait("pe", ev["y", sg], bank.free)
            for k, (a, b) in enumerate(KS):
                e = do("pe", partial(nc.tensor.transpose, bank.ap[0:(b - a) * SLOTS, k * D:k * D + D],
                                     yT[sg % 2][:, t % TS, a:b, :].rearrange("p e s -> p (e s)"), ident[:]), z["yt"])
            ev["yt", t] = e
            wait("act", e, ev.get(("sc", t - 2)))
            rows = KS[0][1] * SLOTS
            do("act", partial(nc.scalar.copy, yr[0:rows, i, 0:2, :], bank.ap[0:rows, 0:2 * D].rearrange("p (k q) -> p k q", q=D)), z["yr"])
            rows = (KS[2][1] - KS[2][0]) * SLOTS
            ev["yr", t] = bank.free = do("act", partial(nc.scalar.copy, yr[0:rows, i, 2, :], bank.ap[0:rows, 2 * D:3 * D]), z["yr"])

        def scatter(t):
            sg, i, bank = t // TS, t % 2, banks[7]
            wait("pe", ev["yr", t], ev["pT", t], bank.free)
            for k, (a, b) in enumerate(KS):
                rows = (b - a) * SLOTS
                e = do("pe", partial(nc.tensor.matmul, bank.ap[:, 0:D], pickT[0:rows, sg % 2, t % TS, k, :], yr[0:rows, i, k, :],
                                     start=(k == 0), stop=(k == 2)), z["sc"])
            ev["sc", t] = e
            wait("dve", e)
            ev["x4", t] = bank.free = do("dve", partial(nc.vector.tensor_tensor, x_sb[:, t, :], bank.ap[:, 0:D], x_sb[:, t, :], ALU.add), z["x"])

        for _ in attention1(lambda: route1(0)):
            pass
        pick1(0)
        for t in range(TS):
            gather(t)
            turn_pick(t)
            pick1(t + 1)
        routing = route1(NS)
        for sg in range(NSG + 1):
            for ex in range(NE):
                t = (sg + 1) * TS + ex
                if sg < NSG:
                    up1(sg, ex)
                if ex > 0 and sg < NSG:
                    down1(sg, ex - 1)
                if ex == 0 and sg > 0:
                    down1(sg - 1, NE - 1)
                if sg > 0:
                    turn_results(t - 2 * TS)
                if t < NT:
                    gather(t)
                if sg > 0:
                    scatter(t - 2 * TS)
                if t < NT:
                    turn_pick(t)
                for _ in range(2):
                    next(routing, None)
                if (t + 1) % NS == 0:
                    for _ in routing:
                        pass
                    routing = route1(t + 1 + NS) if t + 1 + NS < NT else iter(())
                if TS < t + 1 < NT:
                    pick1(t + 1)

        s_out = sem("s_out")
        for g in range(NG):
            wait("sp", ev["x4", TG * g + TG - 1])
            e = do("sp", partial(nc.sync.dma_start, out[:, TG * g:TG * g + TG, :], x_sb[:, TG * g:TG * g + TG, :]), s_out, 16)
        wait("sp", e)

        block = ctx.enter_context(nc.Block())

        @block.sync
        def _(e):
            plan.run("sp", e)

        @block.scalar
        def _(e):
            plan.run("act", e)

        @block.tensor
        def _(e):
            plan.run("pe", e)

        @block.vector
        def _(e):
            plan.run("dve", e)

        @block.gpsimd
        def _(e):
            plan.run("pool", e)


def lay_out(i):
    a = {k: np.asarray(v) for k, v in i.items()}
    col = lambda v: np.broadcast_to(v.reshape(-1, 1) if v.size > 1 else v.reshape(1, 1), (P, 1))
    f = lambda *c: np.ascontiguousarray(np.concatenate(c, axis=1), np.float32)
    r = np.arange(P)
    quad = [((r // DH) % QUADS == j).astype(np.float32).reshape(P, 1) for j in range(QUADS)]
    row = [(r // S == b).astype(np.float32).reshape(P, 1) for b in range(2)]
    gx, gf = a["g_xattn"], a["g_ffn"]
    rr, bb, hh, dd = np.meshgrid(np.arange(4), np.arange(2), np.arange(2), np.arange(DH), indexing="ij")
    head = np.array([4 * quad + j for quad in (0, 2, 1, 3) for j in range(4)])
    dims = (head[:, None] * DH + np.arange(DH)).ravel()
    src = [(head[half * 8 + rr * 2 + hh] * DH + dd).ravel() for half in range(2)]
    w = [a["L0_xattn_w_q"], a["L0_xattn_w_k"], a["L0_xattn_w_v"][:, dims], a["L0_xattn_w_out"][src[0]], a["L0_xattn_w_out"][src[1]],
         a["L1_xattn_Wq"], a["L1_xattn_Wk"], a["L1_xattn_Wv"]]
    rows = [a["L0_xattn_b_v"][dims], a["L0_xattn_b_out"], a["L1_xattn_bv"], a["L1_xattn_bo"]]
    q, k = r[:, None], r[None, :]
    same = q // S == k // S
    mask = np.stack([(same & (k <= q)), np.where(same, np.where(k <= q, 0.0, NEG), OUTSIDE)], 1).astype(np.float32)
    small = np.zeros((P, 4, NE), np.float32)
    small[:, 0, :] = a["L0_ffn_bg"]
    small[:, 1, :] = NE - np.arange(NE)
    c = np.ascontiguousarray
    return {
        "x": c(a["x"].reshape(NT, P, D).transpose(1, 0, 2)),
        "ctxT": c(a["ctx_1024"].reshape(NT * P, D).T),
        "w": c(np.stack(w, 1)),
        "wo1": c(a["L1_xattn_Wo"]),
        "vecs": f(col(a["L0_xattn_b_q"]), col(a["L0_xattn_b_k"]), col(a["L1_xattn_bq"]), col(a["L1_xattn_bk"]),
                  col(gx[0:1]), col(gx[1:2]), col(gf[0:1]), col(gf[1:2]), *quad, *row),
        "rows": c(np.broadcast_to(np.stack(rows, 0)[None], (P, 4, D))),
        "ident": np.eye(P, dtype=np.float32),
        "small": small,
        "mask": mask,
        "wr": c(np.stack([a["L0_ffn_Wg"], a["L1_ffn_router_w"].T], 1)),
        "w1a": c(a["L0_ffn_W1"].transpose(1, 0, 2)),
        "w1b": c(a["L1_ffn_w1"].transpose(1, 0, 2)),
        "w2a": c(a["L0_ffn_W2"].reshape(NE, HC, P, D).transpose(2, 0, 1, 3)),
        "w2b": c(a["L1_ffn_w2"].reshape(NE, HC, P, D).transpose(2, 0, 1, 3)),
        "b1": c(np.stack([a["L0_ffn_b1"].reshape(NE * HC, P).T, a["L1_ffn_b1"].reshape(NE * HC, P).T], 1)),
        "b2T": c(a["L1_ffn_b2"].T),
        "slot": c(np.broadcast_to(np.arange(SLOTS, dtype=np.float32), (P, SLOTS))),
        "b2": c(np.broadcast_to(a["L0_ffn_b2"][None], (P, NE, D))),
        "before": c(np.stack([(q < k), np.ones((P, P))], 1).astype(np.float32)),
        "block": np.arange(NBLOCKS, dtype=np.float32).reshape(1, NBLOCKS),
    }


def kernel(**inputs):
    import concourse.bacc as bacc
    from concourse.bass_utils import run_bass_kernel_spmd

    arrays = lay_out(inputs)
    nc = bacc.Bacc("TRN2", target_bir_lowering=False, num_devices=1)
    t_in = {n: nc.dram_tensor("in_" + n, v.shape, mybir.dt.from_np(v.dtype), kind="ExternalInput").ap()
            for n, v in arrays.items()}
    out = nc.dram_tensor("out_x", (P, NT, D), F32, kind="ExternalOutput").ap()
    build(nc, t_in, out)
    r = run_bass_kernel_spmd(nc, [{"in_" + n: v for n, v in arrays.items()}], core_ids=[0])
    got = r.results[0]["out_x"]
    return np.ascontiguousarray(got.transpose(1, 0, 2)).reshape(NB, S, D)
```

```python
from contextlib import ExitStack
from functools import partial

import numpy as np
import concourse.bass as bass
from concourse import mybir

ALU = mybir.AluOpType
ACT = mybir.ActivationFunctionType
F32 = mybir.dt.float32
I32 = mybir.dt.int32
AX_X = mybir.AxisListType.X

P = 128
D = 128
NB, S = 128, 64
NT = NB * S // P
TG = 4
NG = NT // TG
GC = TG * P
HEADS, DH = 16, 8
QUADS = 4
PAIRS = HEADS // 2
NE, HID = 8, 512
HC = HID // P
CAP = max(1, int(S * 2.0 / NE) + 1)
SLOTS = 2 * CAP
TS = 8
NSG = NT // TS
ROUTER = 2
BLOCK = 256
HALF = NT // 2
TOP = 2
NBLOCKS = (HALF * P * TOP + NE * (BLOCK - 1)) // BLOCK
BS = BLOCK // P
EPS = 1e-5
NEG = -1.0e9
OUTSIDE = -3.0e38


class Sem:

    def __init__(self, handle):
        self.handle, self.n = handle, 0


class Plan:

    ENGINES = ("sp", "act", "pe", "dve", "pool")

    def __init__(self):
        self.queue = {e: [] for e in self.ENGINES}
        self.seen = {}

    def do(self, engine, emit, sem=None, by=1):
        self.queue[engine].append((emit, sem, by))
        if sem is not None:
            sem.n += by
            return (sem, sem.n)
        return None

    def wait(self, engine, *events):
        for event in events:
            if event is None:
                continue
            sem, n = event
            if self.seen.get((engine, sem), 0) < n:
                self.seen[(engine, sem)] = n
                self.queue[engine].append((None, sem, n))

    def run(self, engine, handle):
        for emit, sem, n in self.queue[engine]:
            if emit is None:
                handle.wait_ge(sem.handle, n)
                continue
            ins = emit()
            if sem is not None:
                ins.then_inc(sem.handle, n)


class Bank:
    def __init__(self, ap):
        self.ap, self.free = ap, None


def build(nc, t_in, out):
    with ExitStack() as ctx:
        def sb(name, shape, dt=F32):
            return ctx.enter_context(nc.sbuf_tensor(name, shape, dt))

        def sem(name):
            return Sem(ctx.enter_context(nc.semaphore(name)))

        plan = Plan()
        do, wait = plan.do, plan.wait

        x_sb = sb("x_sb", [P, NT, D])
        ctx_sb = sb("ctx_sb", [D, NT * P])
        w_sb = sb("w_sb", [P, 8, D])
        wo1_sb = sb("wo1_sb", [P, D])
        vec_sb = sb("vec_sb", [P, t_in["vecs"].shape[1]])
        row_sb = sb("row_sb", [P, 2, D])
        ident = sb("ident", [P, P])
        small_sb = sb("small_sb", [P, 2, NE])
        mask_sb = sb("mask_sb", [P, 2, P])
        wr_sb = sb("wr_sb", [P, 2, NE])
        w1_sb = sb("w1_sb", [D, NE, HID])
        w2_sb = sb("w2_sb", [P, NE, HC, D])
        b1_sb = sb("b1_sb", [P, 2, NE * HC])
        b2_sb = sb("b2_sb", [P, NE, D])
        before_sb = sb("before_sb", [P, 2, P])
        block_sb = sb("block_sb", [1, NBLOCKS])
        b2T_sb = sb("b2T_sb", [D, NE])
        slot_sb = sb("slot_sb", [P, SLOTS])
        ln1 = sb("ln1", [P, 4, D])
        tg_sb = sb("tg_sb", [P, 4])
        tbo_sb = sb("tbo_sb", [P, 2, D])

        stats = sb("stats", [P, 16, 6])
        mv = sb("mv", [P, NT, 2])
        rstd = sb("rstd", [P, NT])
        half_v = sb("half_v", [P, 16])
        newton = sb("newton", [P, 16])
        ln_sb = sb("ln_sb", [P, 3, TG, D])
        lnT = sb("lnT", [D, 3, GC])
        work = sb("work", [P, 10880])

        def cut(at, shape, names):
            n = int(np.prod(list(shape.values())))
            return work[:, at:at + n].rearrange(f"p ({names}) -> p {names}", **shape)

        kx = cut(0, dict(i=2, b=2 * TG, j=QUADS, k=S), "i b j k")
        pr = cut(4096, dict(i=2, h=HEADS, k=S), "i h k")
        pT = cut(6144, dict(i=2, r=PAIRS, q=P), "i r q")
        qT = cut(8192, dict(i=2, n=GC), "i n")
        kT = cut(9216, dict(i=2, n=GC), "i n")
        vx = sb("vx", [P, 2, PAIRS, 2, 2, DH])
        den = sb("den", [P, 2, HEADS])
        rden = sb("rden", [P, 2, HEADS])
        rdm = sb("rdm", [P, 2, PAIRS, 2, 2, DH])
        mx = sb("mx", [P, 2, HEADS])
        ctxn = sb("ctxn", [P, 2, 2, P])
        w1g_sb = sb("w1g_sb", [D, 3, HID])
        folded = w1g_sb[:].rearrange("p i n -> p (i n)")[:, 0:HEADS * S].rearrange("p (i h k) -> p i h k", i=2, k=S // 2)
        hid0 = sb("hid0", [P, 2, HC, BLOCK])

        psum = ctx.enter_context(nc.psum_tensor("psum", [P, 8, 512], F32))
        banks = [Bank(psum[:, i, :]) for i in range(8)]

        V = {n: i for i, n in enumerate(["bq0", "bk0", "bq1", "bk1", "gx0", "gx1", "gf0", "gf1",
                                         "quad0", "quad1", "quad2", "quad3", "row0", "row1", "own0", "bv0", "bv1", "bv_layer1"])}

        def vec(name, n=1):
            return vec_sb[:, V[name]:V[name] + n]

        ld = {}

        def load(name, dst, src, eng="sp"):
            ld[name] = do(eng, partial((nc.sync if eng == "sp" else nc.scalar).dma_start, dst, src), sem("ld_" + name), 16)

        load("vecs", vec_sb[:], t_in["vecs"])
        load("ident", ident[:], t_in["ident"], "act")
        for g in range(4):
            load(f"x{g}", x_sb[:, TG * g:TG * g + TG, :], t_in["x"][:, TG * g:TG * g + TG, :])
            load(f"c{g}", ctx_sb[:, GC * g:GC * g + GC], t_in["ctxT"][:, GC * g:GC * g + GC], "act")
            if g == 0:
                load("w", w_sb[:], t_in["w"])
                load("rows", row_sb[:], t_in["rows"], "act")
        for g in range(1, 4):
            load(f"x{3 + g}", x_sb[:, 16 * g:16 * g + 16, :], t_in["x"][:, 16 * g:16 * g + 16, :])
            load(f"c{3 + g}", ctx_sb[:, 2048 * g:2048 * g + 2048],
                 t_in["ctxT"][:, 2048 * g:2048 * g + 2048], "act")
        load("wo1", wo1_sb[:], t_in["wo1"])
        load("small", small_sb[:], t_in["small"])
        load("mask", mask_sb[:], t_in["mask"])
        load("wr", wr_sb[:], t_in["wr"])
        load("w1", w1_sb[:], t_in["w1a"])
        load("w2", w2_sb[:], t_in["w2a"])
        load("b1", b1_sb[:], t_in["b1"])
        load("b2", b2_sb[:], t_in["b2"])
        load("before", before_sb[:], t_in["before"])
        load("block", block_sb[:], t_in["block"])
        load("b2T", b2T_sb[:], t_in["b2T"])
        load("slot", slot_sb[:], t_in["slot"])

        def xload(g):
            return ld[f"x{g}"] if g < 4 else ld[f"x{3 + g // 4}"]

        def cload(g):
            return ld[f"c{g}"] if g < 4 else ld[f"c{3 + g // 4}"]

        ev = {}
        s_tg, s_tbo = sem("s_tg"), sem("s_tbo")

        s_bv = sem("s_bv")

        def gates():
            wait("act", ld["vecs"])
            ev["tg"] = do("act", partial(nc.scalar.activation, tg_sb[:], vec("gx0", 4), ACT.Tanh), s_tg)

        def output_bias(layer, columns, weights, e_weights):
            wait("dve", ld["vecs"], ld["rows"], ev["tg"])
            for n, (rows, bias) in enumerate(columns):
                e = do("dve", partial(nc.vector.tensor_scalar, ln1[:, n, :], rows, bias, None, ALU.mult), s_bv)
            wait("pe", e, e_weights, banks[7].free)
            for n, w in enumerate(weights):
                e = do("pe", partial(nc.tensor.matmul, banks[7].ap[:, 0:D], ln1[:, n, :], w,
                                     start=(n == 0), stop=(n == len(weights) - 1)), s_bv)
            row = row_sb[:, layer, :]
            wait("dve", e)
            banks[7].free = e = do("dve", partial(nc.vector.tensor_tensor, row, banks[7].ap[:, 0:D], row, ALU.add), s_bv)
            wait("dve", e)
            ev["tbo", layer] = do("dve", partial(nc.vector.tensor_scalar, tbo_sb[:, layer, :], row, tg_sb[:, layer:layer + 1],
                                                 None, ALU.mult), s_tbo)

        TGX = [tg_sb[:, 0:1], tg_sb[:, 1:2]]
        TGF = [tg_sb[:, 2:3], tg_sb[:, 3:4]]

        s_st, s_mv, s_rs, s_ln = sem("s_st"), sem("s_mv"), sem("s_rs"), sem("s_ln")
        s_lt, s_lnT = sem("s_lt"), sem("s_lnT")
        ln_free = [None] * 3
        lnT_free = [None] * 3

        def moments(lo, n, ready):
            wait("dve", *ready)
            for t in range(lo, lo + n):
                e = do("dve", partial(nc.vector.bn_stats, stats[:, t % 16, :], x_sb[:, t, :]), s_st)
            wait("dve", e)
            for t in range(lo, lo + n):
                e = do("dve", partial(nc.vector.bn_aggr, mv[:, t, :], stats[:, t % 16, :]), s_mv)
            wait("dve", e)

        def inverse_std(lo, n):
            def step(fn):
                wait("dve", do("dve", fn, s_rs))

            var, y, h, w = mv[:, lo:lo + n, 1], rstd[:, lo:lo + n], half_v[:, 0:n], newton[:, 0:n]
            step(partial(nc.vector.tensor_scalar, w, var, EPS, None, ALU.add))
            step(partial(nc.vector.tensor_scalar, h, w, -0.5, None, ALU.mult))
            step(partial(nc.vector.tensor_scalar, w.bitcast(I32), w.bitcast(I32), 1, None, ALU.arith_shift_right))
            step(partial(nc.vector.tensor_scalar, y.bitcast(I32), w.bitcast(I32), -1.0, float(0x5F3759DF), ALU.mult, ALU.add))
            for _ in range(3):
                step(partial(nc.vector.tensor_tensor, w, y, y, ALU.mult))
                step(partial(nc.vector.tensor_tensor, w, w, h, ALU.mult))
                step(partial(nc.vector.scalar_tensor_tensor, out=y, in0=w, scalar=1.5, in1=y, op0=ALU.add, op1=ALU.mult))

        def statistics(lo, n, ready):
            moments(lo, n, ready)
            inverse_std(lo, n)

        def norm(g, i):
            wait("dve", ln_free[i])
            for t in range(TG):
                tt = TG * g + t
                e = do("dve", partial(nc.vector.tensor_scalar, ln_sb[:, i, t, :], x_sb[:, tt, :], mv[:, tt, 0:1],
                                      rstd[:, tt:tt + 1], ALU.subtract, ALU.mult), s_ln)
            return e

        def turn(i, e_ln, bank):
            wait("pe", ld["ident"], e_ln, bank.free)
            for t in range(TG):
                e = do("pe", partial(nc.tensor.transpose, bank.ap[:, t * P:t * P + P], ln_sb[:, i, t, :], ident[:]), s_lt)
            ln_free[i] = e
            wait("act", e, lnT_free[i])
            bank.free = do("act", partial(nc.scalar.copy, lnT[:, i, :], bank.ap), s_lnT)
            return bank.free

        s_q, s_qe, s_k, s_ke, s_kx = sem("s_q"), sem("s_qe"), sem("s_k"), sem("s_ke"), sem("s_kx")
        s_v, s_vx, s_sc, s_mx, s_sub, s_exp = (sem("s_v"), sem("s_vx"), sem("s_sc"), sem("s_mx"),
                                               sem("s_sub"), sem("s_exp"))
        s_den, s_rden, s_rdm, s_pt, s_pT = sem("s_den"), sem("s_rden"), sem("s_rdm"), sem("s_pt"), sem("s_pT")
        s_fold, s_rc = sem("s_fold"), sem("s_rc")
        s_av, s_cn, s_o, s_x1, s_xb = sem("s_av"), sem("s_cn"), sem("s_o"), sem("s_x1"), sem("s_xb")
        s_zero = sem("s_zero")
        e_zero = do("pool", partial(nc.gpsimd.memset, vx[:], 0.0), s_zero)
        SCALE0 = float(1.0 / np.sqrt(np.float32(DH)))
        B_S, B_T, B_C, B_V, B_O, B_P = (0, 1), (2, 3), 4, 5, 6, 7

        def project(w, src, e_src, dst, bias, sem_mm, sem_ev):
            bank = banks[B_P]
            wait("pe", ld["w"], *e_src, bank.free)
            e = do("pe", partial(nc.tensor.matmul, bank.ap, w, src, start=True, stop=True), sem_mm)
            wait("act", e, ld["vecs"])
            bank.free = do("act", partial(nc.scalar.activation, dst, bank.ap, ACT.Identity, bias=bias), sem_ev)
            return bank.free

        def prep_norm(g):
            ev["ln", g] = norm(g, g % 2)

        def prep_bias(g):
            wait("pool", ev["tbo", 0], ev["ln", g])
            ev["xb", g] = do("pool", partial(nc.gpsimd.tensor_tensor,
                x_sb[:, TG * g:TG * g + TG, :], x_sb[:, TG * g:TG * g + TG, :],
                tbo_sb[:, 0:1, :].to_broadcast([P, TG, D]), ALU.add), s_xb)

        def prep_turn(g):
            ev["lnT", g] = turn(g % 2, ev["ln", g], banks[B_P])

        def prep_q(g):
            i = g % 2
            wait("act", ev.get(("sc", TG * (g - 2) + TG - 1)))
            ev["q", g] = project(w_sb[:, 0, :], lnT[:, i, :], [ev["lnT", g]], qT[:, i, :], vec("bq0"), s_q, s_qe)
            lnT_free[i] = ev["q", g]

        def prep_k(g):
            i = g % 2
            wait("act", ev.get(("kx", g - 2)))
            ev["k", g] = project(w_sb[:, 1, :], ctx_sb[:, g * GC:g * GC + GC], [cload(g)], kT[:, i, :],
                                 vec("bk0"), s_k, s_ke)
            wait("pool", ev["k", g], ev.get(("sc", TG * (g - 2) + TG - 1)))
            for j in range(QUADS):
                ev["kx", g] = do("pool", partial(nc.gpsimd.tensor_scalar, kx[:, i, :, j, :], kT[:, i, :].rearrange("p (b k) -> p b k", k=S),
                    vec(f"quad{j}"), 1.0, ALU.mult, ALU.mult), s_kx)

        def prep_v(t):
            bank = banks[B_V]
            wait("pe", ld["w"], cload(t // TG), bank.free)
            for hp in range(2):
                for b in range(2):
                    c = t * P + b * S
                    e = do("pe", partial(nc.tensor.matmul, bank.ap[64 * hp:64 * hp + 64, b * S:b * S + S], ctx_sb[:, c:c + S],
                                         w_sb[:, 2, :].rearrange("p (r h d) -> p r h d", r=PAIRS, h=2)[:, :, hp, :],
                                         start=True, stop=True), s_v)
            wait("act", e, e_zero, ev.get(("av", t - 2)))
            for hp in range(2):
                q = slice(64 * hp, 64 * hp + 64)
                for b in range(2):
                    e = do("act", partial(nc.scalar.copy, vx[q, t % 2, :, b, hp, :],
                                          bank.ap[q, b * S:b * S + S].rearrange("p (r d) -> p r d", d=DH)), s_vx)
            ev["vx", t] = bank.free = e

        def scores(t):
            g, i = t // TG, (t // TG) % 2
            two = [banks[n] for n in B_S]
            wait("pe", ev["q", g], ev["kx", g], *[b.free for b in two])
            done = []
            for quad in range(QUADS):
                q = slice(32 * quad, 32 * quad + 32)
                if quad >= 2:
                    wait("pe", done[quad - 2])
                for b in range(2):
                    c = (t % TG) * P + b * S
                    dst = two[quad % 2].ap[64 * b:64 * b + 64, 256 * (quad // 2):256 * (quad // 2) + 256]
                    e = do("pe", partial(nc.tensor.matmul, dst, qT[q, i, c:c + S], kx[q, i, 2 * (t % TG) + b, :, :], start=True, stop=True), s_sc)
                done.append(e)
            ev["sc", t] = e

        two_banks = psum[:, B_S[0]:B_S[1] + 1, :].rearrange("p a (h k) -> p (a h) k", k=S)

        def largest(t):
            i = t % 2
            wait("dve", ev["sc", t])
            ev["mx", t] = do("dve", partial(nc.vector.tensor_reduce, mx[:, i, :], two_banks, AX_X, ALU.max), s_mx)

        def shift(t):
            i = t % 2
            wait("dve", ev["mx", t], ev.get(("pt", t - 2)), ev.get(("fold", t - 2)))
            e = do("dve", partial(nc.vector.tensor_tensor, pr[:, i, :, :], two_banks, mx[:, i, :].unsqueeze(2).to_broadcast([P, HEADS, S]),
                                                    ALU.subtract), s_sub)
            for n in B_S:
                banks[n].free = e
            ev["sub", t] = e

        def exponentials(t):
            i = t % 2
            wait("act", ev["sub", t])
            ev["exp", t] = do("act", partial(nc.scalar.activation, pr[:, i, :, :], pr[:, i, :, :], ACT.Exp, scale=SCALE0), s_exp)

        def fold(t):
            wait("pool", ev["exp", t], ev.get(("den", t - 2)))
            ev["fold", t] = do("pool", partial(nc.gpsimd.tensor_tensor, folded[:, t % 2, :, :], pr[:, t % 2, :, 0:S // 2],
                                               pr[:, t % 2, :, S // 2:S], ALU.add), s_fold)

        def denominators(t):
            i = t % 2
            wait("dve", ev["fold", t])
            ev["den", t] = e = do("dve", partial(nc.vector.tensor_reduce, den[:, i, :], folded[:, i, :, :], AX_X, ALU.add), s_den)
            wait("dve", e, ev.get(("rdm", t - 2)))
            e = do("dve", partial(nc.vector.reciprocal, rden[:, i, :], den[:, i, :]), s_rden)
            ev["rden", t] = e

        def spread_rden(t):
            i = t % 2
            wait("act", ev["rden", t], ev.get(("av", t - 2)))
            for b in range(2):
                ev["rdm", t] = do("act", partial(
                    nc.scalar.activation, rdm[:, i, :, b, :, :],
                    rden[:, i, :].rearrange("p (r h) -> p r h", h=2).unsqueeze(3).to_broadcast([P, PAIRS, 2, DH]),
                    ACT.Identity, scale=vec(f"row{b}")), s_rdm)

        def turn_p(t):
            i = t % 2
            wait("pe", ev["exp", t])
            for half in range(2):
                bank = banks[B_T[half]]
                wait("pe", bank.free)
                for r in range(4):
                    pair = 4 * half + r
                    e = do("pe", partial(nc.tensor.transpose, bank.ap[:, r * P:r * P + P], pr[:, i, 2 * pair:2 * pair + 2, :], ident[:]), s_pt)
                wait("act", e, ev.get(("av", t - 2)))
                bank.free = do("act", partial(nc.scalar.copy, pT[:, i, 4 * half:4 * half + 4, :], bank.ap), s_pT)
            ev["pt", t] = e
            ev["pT", t] = bank.free

        def attend(t):
            i = t % 2
            bank = banks[B_C]
            wait("pe", ev["pT", t], ev["vx", t], ev["rdm", t], bank.free)
            for pair in range(PAIRS):
                q = 32 * (pair % 4)
                do("pe", partial(nc.tensor.matmul, bank.ap[q:q + 32, (pair // 4) * P:(pair // 4) * P + P], vx[:, i, pair, :, :, :],
                                 pT[:, i, pair, :], start=True, stop=True), s_av)
            for half in range(2):
                rep = rdm[:, i, 4 * half:4 * half + 4, :, :, :].rearrange("p r b h d -> p (r b h d)")
                e = do("pe", partial(nc.tensor.transpose, bank.ap[:, 256 + half * P:256 + half * P + P], rep, ident[:]), s_av)
            ev["av", t] = e
            wait("act", e, ev.get(("o", t - 2)))
            ev["rc", t] = do("act", partial(nc.scalar.copy, ctxn[:, i, :, :], bank.ap[:, 256:512].rearrange("p (a q) -> p a q", a=2)), s_rc)

        def normalise(t):
            i = t % 2
            bank = banks[B_C]
            wait("dve", ev["rc", t])
            bank.free = ev["cn", t] = do("dve", partial(nc.vector.tensor_tensor,
                ctxn[:, i, :, :], bank.ap[:, 0:256].rearrange("p (a q) -> p a q", a=2), ctxn[:, i, :, :], ALU.mult), s_cn)

        def output(t):
            bank = banks[B_O]
            wait("pe", ev["cn", t], bank.free)
            for half in range(2):
                e = do("pe", partial(nc.tensor.matmul, bank.ap[:, 0:D], ctxn[:, t % 2, half, :], w_sb[:, 3 + half, :],
                                                         start=(half == 0), stop=(half == 1)), s_o)
            ev["o", t] = e

        def add_output(t):
            wait("dve", ev["o", t], ev["xb", t // TG])
            ev["x1", t] = banks[B_O].free = do("dve", partial(nc.vector.scalar_tensor_tensor,
                out=x_sb[:, t, :], in0=banks[B_O].ap[:, 0:D], scalar=TGX[0], in1=x_sb[:, t, :],
                op0=ALU.mult, op1=ALU.add), s_x1)

        HG = HALF // TG
        NS = 16
        xg_dram = [nc.dram_tensor(f"xg{h}", (NBLOCKS * BLOCK, D), F32, kind="Internal").ap() for h in range(2)]
        yg_dram = [nc.dram_tensor(f"yg{h}", (NBLOCKS * BLOCK, D), F32, kind="Internal").ap() for h in range(2)]
        lg_sb = sb("lg_sb", [P, NT, NE])
        red = sb("red", [P, HALF])
        tmp = sb("tmp", [P, HALF, NE])
        left = sb("left", [P, HALF, NE])
        chosen = sb("chosen", [P, TOP + 1, HALF, NE])
        total = sb("total", [P, NE, HALF])
        upto = sb("upto", [P, NE, HALF])
        carry = sb("carry", [P, NE, HALF])
        nb = sb("nb", [P, 4, NE])
        nb_int = sb("nb_int", [P, NE], I32)
        owner = sb("owner", [1, NBLOCKS, NE])
        owner_sum = sb("owner_sum", [1, NBLOCKS])
        expert = sb("expert", [1, 2, NBLOCKS], I32)
        place_f = sb("place_f", [P, HALF])
        place = sb("place", [P, 2, TOP, HALF], mybir.dt.uint32)
        gate0 = sb("gate0", [P, 2, TOP, HALF])
        got_sb = cut(512, dict(i=4, k=TOP, d=D), "i k d")
        xg_sb = cut(2560, dict(i=4, s=BS, d=D), "i s d")
        xgT_sb = cut(3584, dict(i=2, n=BLOCK), "i n")
        yg_sb = sb("yg_sb", [P, 3, BS, D])
        s_lg, s_r, s_ex, s_count = sem("s_lg"), sem("s_r"), sem("s_ex"), sem("s_count")
        ones_row = sb("ones_row", [P, S])
        s_one = sem("s_one")
        e_one = do("pool", partial(nc.gpsimd.memset, ones_row[:], 1.0), s_one)
        e_carry = do("pool", partial(nc.gpsimd.memset, carry[:], 1.0), s_one)
        wait("pool", e_carry)
        e_carry = do("pool", partial(nc.gpsimd.memset, carry[:, :, 0:1], 0.0), s_one)
        e_zeros = do("pool", partial(nc.gpsimd.memset, hid0[:], 0.0), s_one)
        s_fill = sem("s_fill")
        wait("sp", e_zeros)
        zeros = hid0[:].rearrange("p i c n -> p (i c n)")
        per_row = NBLOCKS * BLOCK * D // P
        for h in range(2):
            rows = xg_dram[h].rearrange("(p n) d -> p (n d)", p=P)
            for at in range(0, per_row, zeros.shape[1]):
                n = min(zeros.shape[1], per_row - at)
                e_fill = do("sp", partial(nc.sync.dma_start, rows[:, at:at + n], zeros[:, 0:n]), s_fill, 16)

        def dve(fn, *w):
            wait("dve", *w)
            e = do("dve", fn, s_r)
            wait("dve", e)
            return e

        def logits(layer, i, e_lnT, bank):
            wait("pe", e_lnT, ld["wr"], bank.free)
            for t in range(TG):
                e = do("pe", partial(nc.tensor.matmul, bank.ap[:, NE * t:NE * t + NE], lnT[:, i, t * P:t * P + P],
                                     wr_sb[:, layer, :], start=True, stop=True), s_lg)
            lnT_free[i] = e
            return e, bank.ap[:, 0:TG * NE].rearrange("p (t e) -> p t e", e=NE)

        def logits0(g, i, e_lnT):
            e, src = logits(0, i, e_lnT, banks[B_P])
            banks[B_P].free = dve(partial(nc.vector.tensor_tensor, lg_sb[:, TG * g:TG * g + TG, :], src,
                                          small_sb[:, 0:1, :].to_broadcast([P, TG, NE]), ALU.add), e, ld["small"])

        def softmax8(lo, n):
            L, r = lg_sb[:, lo:lo + n, :], red[:, 0:n]
            bc = r.unsqueeze(2).to_broadcast([P, n, NE])
            dve(partial(nc.vector.tensor_reduce, r, L, AX_X, ALU.max))
            e = dve(partial(nc.vector.tensor_tensor, L, L, bc, ALU.subtract))
            wait("act", e)
            e = do("act", partial(nc.scalar.activation, L, L, ACT.Exp), s_ex)
            yield
            dve(partial(nc.vector.tensor_reduce, r, L, AX_X, ALU.add), e)
            dve(partial(nc.vector.reciprocal, r, r))
            ev["probabilities", lo] = dve(partial(nc.vector.tensor_tensor, L, L, bc, ALU.mult))
            yield

        def route0(h):
            lo = HALF * h
            yield from softmax8(lo, HALF)
            bc = red[:].unsqueeze(2).to_broadcast([P, HALF, NE])
            order = small_sb[:, 1:2, :].to_broadcast([P, HALF, NE])
            for k in range(TOP):
                src = lg_sb[:, lo:lo + HALF, :] if k == 0 else left[:]
                dve(partial(nc.vector.tensor_reduce, red[:], src, AX_X, ALU.max))
                dve(partial(nc.vector.tensor_scalar, gate0[:, h, k, :], red[:], TGF[0], None, ALU.mult))
                dve(partial(nc.vector.tensor_tensor, tmp[:], src, bc, ALU.is_equal))
                yield
                dve(partial(nc.vector.tensor_tensor, tmp[:], tmp[:], order, ALU.mult))
                dve(partial(nc.vector.tensor_reduce, red[:], tmp[:], AX_X, ALU.max))
                dve(partial(nc.vector.tensor_tensor, chosen[:, k, :, :], tmp[:], bc, ALU.is_equal))
                if k == 0:
                    dve(partial(nc.vector.scalar_tensor_tensor, out=left[:], in0=chosen[:, 0, :, :], scalar=-2.0,
                                in1=src, op0=ALU.mult, op1=ALU.add))
                yield
            e = dve(partial(nc.vector.tensor_tensor, chosen[:, TOP, :, :], chosen[:, 0, :, :], chosen[:, 1, :, :], ALU.add))
            bank = banks[B_P]
            wait("pe", e, ld["before"], bank.free)
            for k in range(2):
                e = do("pe", partial(nc.tensor.matmul, bank.ap[:, k * HALF * NE:(k + 1) * HALF * NE], before_sb[:, k, :],
                                     chosen[:, TOP, :, :].rearrange("p t e -> p (t e)"), start=True, stop=True), s_count)
            ahead = bank.ap[:, 0:HALF * NE].rearrange("p (t e) -> p t e", e=NE)
            dve(partial(nc.vector.tensor_copy, total[:], bank.ap[:, HALF * NE:2 * HALF * NE].rearrange("p (t e) -> p e t", e=NE)), e)
            bank.free = dve(partial(nc.vector.tensor_copy, tmp[:], ahead))
            yield
            dve(partial(nc.vector.tensor_tensor_scan, out=upto[:].rearrange("p e t -> p (e t)"),
                        data0=carry[:].rearrange("p e t -> p (e t)"), data1=total[:].rearrange("p e t -> p (e t)"),
                        initial=0.0, op0=ALU.mult, op1=ALU.add), e_carry, e_one)
            dve(partial(nc.vector.tensor_scalar, nb_int[:], upto[:, :, HALF - 1], float(BLOCK - 1), None, ALU.add))
            dve(partial(nc.vector.tensor_scalar, nb_int[:], nb_int[:], int(np.log2(BLOCK)), None, ALU.arith_shift_right))
            dve(partial(nc.vector.tensor_copy, nb[:, 1, :], nb_int[:]))
            dve(partial(nc.vector.tensor_tensor_scan, out=nb[:, 2, :], data0=ones_row[:, 0:NE], data1=nb[:, 1, :],
                        initial=0.0, op0=ALU.mult, op1=ALU.add))
            dve(partial(nc.vector.tensor_tensor, nb[:, 3, :], nb[:, 2, :], nb[:, 1, :], ALU.subtract))
            yield
            dve(partial(nc.vector.tensor_tensor, total[:], upto[:], total[:], ALU.subtract))
            dve(partial(nc.vector.scalar_tensor_tensor, out=upto[:], in0=nb[:, 3, :].unsqueeze(2).to_broadcast([P, NE, HALF]),
                        scalar=float(BLOCK), in1=total[:], op0=ALU.mult, op1=ALU.add))
            dve(partial(nc.vector.tensor_tensor, left[:], tmp[:], upto[:].rearrange("p e t -> p t e"), ALU.add))
            for k in range(TOP):
                dve(partial(nc.vector.tensor_tensor, tmp[:], chosen[:, k, :, :], left[:], ALU.mult))
                dve(partial(nc.vector.tensor_reduce, place_f[:], tmp[:], AX_X, ALU.add))
                ev["place", h] = dve(partial(nc.vector.tensor_copy, place[:, h, k, :], place_f[:]))
                yield
            dve(partial(nc.vector.tensor_tensor, owner[:], nb[0:1, 2, :].unsqueeze(1).to_broadcast([1, NBLOCKS, NE]),
                        block_sb[:].unsqueeze(2).to_broadcast([1, NBLOCKS, NE]), ALU.is_le), ld["block"])
            dve(partial(nc.vector.tensor_reduce, owner_sum[:], owner[:], AX_X, ALU.add))
            ev["expert", h] = dve(partial(nc.vector.tensor_scalar, expert[:, h, :], owner_sum[:], float(NE - 1), None, ALU.min))
            yield

        s_row = sem("s_row")
        s_put = [sem(f"s_put{i}") for i in range(4)]
        s_get = [sem(f"s_get{i}") for i in range(4)]
        s_comb = sem("s_comb")
        last_row = NBLOCKS * BLOCK - 1

        def put0(t):
            h, i = t // HALF, t % 4
            wait("dve", ev.get(("put", t - 4)))
            e = do("dve", partial(nc.vector.tensor_scalar, ln1[:, i, :], x_sb[:, t, :], mv[:, t, 0:1], rstd[:, t:t + 1],
                                  ALU.subtract, ALU.mult), s_row)
            wait("pool", e, e_fill, ev["place", h])
            for k in range(TOP):
                at = bass.IndirectOffsetOnAxis(ap=place[:, h, k, t % HALF:t % HALF + 1], axis=0)
                ev["put", t] = do("pool", partial(nc.gpsimd.indirect_dma_start, xg_dram[h], at, ln1[:, i, :], None,
                                                  bounds_check=last_row, oob_is_err=False), s_put[i], 16)

        def work0(h):
            yield from route0(h)
            for t in range(HALF * h, HALF * h + HALF):
                put0(t)
                yield

        def get0(t):
            h, i = t // HALF, t % 4
            wait("pool", *[ev["stored", h, n] for n in range(3)], ev.get(("x2", t - 4)))
            for k in range(TOP):
                at = bass.IndirectOffsetOnAxis(ap=place[:, h, k, t % HALF:t % HALF + 1], axis=0)
                ev["got", t] = do("pool", partial(nc.gpsimd.indirect_dma_start, got_sb[:, i, k, :], None, yg_dram[h], at,
                                                  bounds_check=last_row, oob_is_err=False), s_get[i], 16)

        def combine0(t):
            h, i = t // HALF, t % 4
            for n in range(t + 3 if t % HALF else t, min(t + 4, HALF * h + HALF)):
                get0(n)
            wait("dve", ev["got", t])
            for k in range(TOP):
                e = do("dve", partial(nc.vector.scalar_tensor_tensor, out=x_sb[:, t, :], in0=got_sb[:, i, k, :],
                                      scalar=gate0[:, h, k, t % HALF:t % HALF + 1], in1=x_sb[:, t, :],
                                      op0=ALU.mult, op1=ALU.add), s_comb)
                wait("dve", e)
            ev["x2", t] = e

        def moments0(g):
            if g < NG:
                moments(TG * g, TG, [xload(g)])

        moments0(0)
        inverse_std(0, TG)
        for f in (prep_norm, prep_turn, prep_q, prep_k):
            f(0)
        gates()
        own = vec("own0").to_broadcast([P, P])
        output_bias(0, [(own, vec("bv0")), (own, vec("bv1"))], [w_sb[:, 3, :], w_sb[:, 4, :]], ld["w"])
        prep_bias(0)
        moments0(1)
        inverse_std(TG, TG)
        prep_norm(1)
        prep_bias(1)

        side = iter(())
        for t in range(NT + 3):
            g, r = t // TG + 1, t % TG
            h = g - 4
            if t < NT:
                scores(t)
            if 0 <= t - 2 < NT:
                attend(t - 2)
            if 0 <= t - 3 < NT:
                add_output(t - 3)
            if t < NT:
                largest(t)
            if t < NT:
                shift(t)
            if 0 <= t - 2 < NT:
                normalise(t - 2)
            if 0 <= t - 1 < NT:
                denominators(t - 1)
            if r < 3 and g < NG:
                (prep_turn, prep_q, prep_k)[r](g)
            if r == 3 and ev.get(("ln0", h)):
                e_lnT0 = turn(ROUTER, ev["ln0", h], banks[B_P])
            if 0 <= t - 1 < NT:
                turn_p(t - 1)
                prep_v(t - 1)
            if 0 <= t - 2 < NT:
                output(t - 2)
            if t < NT:
                exponentials(t)
                fold(t)
            if 0 <= t - 1 < NT:
                spread_rden(t - 1)
            if r == 1 and g % 2 == 1:
                moments0(g + 1)
            if r == 2 and g % 2 == 1:
                moments0(g + 2)
            if r == 3 and g % 2 == 1 and g + 1 < NG:
                inverse_std(TG * (g + 1), 2 * TG)
            if r == 3 and g + 1 < NG:
                prep_norm(g + 1)
                prep_bias(g + 1)
            if g % 2 == 0 and r < 3 and g >= 4 and t < NT:
                if r < 2:
                    moments(TG * (h + r), TG, [ev["x1", TG * (h + r) + n] for n in range(TG)])
                else:
                    inverse_std(TG * h, 2 * TG)
            if r == 2 and h >= 0 and t < NT:
                ev["ln0", h] = norm(h, ROUTER)
            if r == 3 and ev.get(("ln0", h)):
                logits0(h, ROUTER, e_lnT0)
            if h == HG and r == 0:
                side = work0(0)
            for _ in range(2):
                next(side, None)

        s_w1g = [sem(f"s_w1g{i}") for i in range(3)]
        s_xg = [sem(f"s_xg{i}") for i in range(4)]
        s_yg = [sem(f"s_yg{i}") for i in range(3)]
        s_xt, s_xT, s_up, s_hg, s_dn, s_yb = sem("s_xt"), sem("s_xT"), sem("s_up"), sem("s_hg"), sem("s_dn"), sem("s_yb")
        number = {}

        def read_expert(engine, h, j):
            def emit():
                handle = {"sp": nc.sync, "act": nc.scalar, "pe": nc.tensor, "dve": nc.vector}[engine]
                number[engine] = handle.value_load(expert[0:1, h, j:j + 1], min_val=0, max_val=NE - 1)
            wait(engine, ev["expert", h])
            do(engine, emit)

        def fetch_weights(h, j):
            i = j % 3
            read_expert("sp", h, j)
            wait("sp", ld["w1"], ev.get(("up0", h, j - 3)), ev.get(("up0", h - 1, NBLOCKS - 1)))
            ev["w1_read", i] = ev["w1g", h, j] = do("sp", lambda: nc.sync.dma_start(
                w1g_sb[:, i, :], w1_sb[:, bass.ds(number["sp"], 1), :].rearrange("p a n -> p (a n)")), s_w1g[i], 16)

        def fetch_tokens(h, j):
            wait("sp", *[ev["put", HALF * h + HALF - 1 - n] for n in range(4)], ev.get(("xt", h, j - 4)), ev.get(("xt", h - 1, NBLOCKS - 1)))
            ev["xg", h, j] = do("sp", partial(
                nc.sync.dma_start, xg_sb[:, j % 4, :, :],
                xg_dram[h][j * BLOCK:j * BLOCK + BLOCK, :].rearrange("(s p) d -> p s d", p=P)), s_xg[j % 4], 16)

        def turn0(h, j):
            bank = banks[4]
            wait("pe", ev["xg", h, j], bank.free)
            for n in range(BS):
                e = do("pe", partial(nc.tensor.transpose, bank.ap[:, n * P:n * P + P], xg_sb[:, j % 4, n, :], ident[:]), s_xt)
            ev["xt", h, j] = e
            wait("dve", e, ev.get(("up0", h, j - 2)), ev.get(("up0", h - 1, NBLOCKS - 1)))
            bank.free = ev["xT", h, j] = do("dve", partial(nc.vector.tensor_copy, xgT_sb[:, j % 2, :], bank.ap[:, 0:BLOCK]), s_xT)

        def up0(h, j):
            read_expert("act", h, j)
            for c in range(HC):
                bank = banks[(HC * j + c) % 3]
                wait("pe", ev["xT", h, j], ev["w1g", h, j], bank.free)
                e = do("pe", partial(nc.tensor.matmul, bank.ap[:, 0:BLOCK], w1g_sb[:, j % 3, c * P:c * P + P], xgT_sb[:, j % 2, :],
                                     start=True, stop=True), s_up)
                wait("act", e, ld["b1"], e_fill, ev.get(("down0", h, j - 2)), ev.get(("down0", h - 1, NBLOCKS - 1)))

                def emit(c=c, bank=bank):
                    bias = b1_sb[:, 0, :].rearrange("p (e c) -> p e c", c=HC)[:, bass.ds(number["act"], 1), c]
                    return nc.scalar.activation(hid0[:, j % 2, c, :], bank.ap[:, 0:BLOCK], ACT.Gelu, bias=bias)
                bank.free = ev["hid0", h, j] = do("act", emit, s_hg)
            ev["up0", h, j] = e

        def down0(h, j):
            i, bank = j % 3, banks[3]
            read_expert("dve", h, j)
            wait("pe", ev["hid0", h, j], ld["w2"], bank.free)
            for n in range(BS):
                for c in range(HC):
                    e = do("pe", lambda n=n, c=c: nc.tensor.matmul(
                        bank.ap[:, n * D:n * D + D], hid0[:, j % 2, c, n * P:n * P + P],
                        w2_sb[:, bass.ds(number["pe"], 1), c, :].rearrange("p a d -> p (a d)"),
                        start=(c == 0), stop=(c == HC - 1)), s_dn)
            ev["down0", h, j] = e
            wait("dve", e, ld["b2"], ev.get(("stored", h, i)), ev.get(("stored", h - 1, i)))
            bank.free = e = do("dve", lambda: nc.vector.tensor_tensor(
                yg_sb[:, i, :, :], bank.ap[:, 0:BS * D].rearrange("p (n d) -> p n d", d=D),
                b2_sb[:, bass.ds(number["dve"], 1), :].to_broadcast([P, BS, D]), ALU.add), s_yb)
            wait("sp", e)
            ev["stored", h, i] = do("sp", partial(
                nc.sync.dma_start, yg_dram[h][j * BLOCK:j * BLOCK + BLOCK, :].rearrange("(s p) d -> p s d", p=P),
                yg_sb[:, i, :, :]), s_yg[i], 16)

        def rest_of_routing():
            for g in range(NG - 3, NG):
                e = turn(g % 3, ev["ln0", g], banks[7])
                yield
                logits0(g, g % 3, e)
                yield
            yield from work0(1)

        def combine_half_0():
            for t in range(HALF):
                combine0(t)
                yield
            yield from begin1()

        s1 = {n: sem("s1_" + n) for n in ["v", "ve", "s", "t", "m", "n", "e", "r", "pt", "pT", "c", "cT", "o", "x", "xb"]}
        SCALE1 = float(1.0 / np.sqrt(np.float32(D)))
        kT1 = kx.rearrange("p i b j k -> p i (b j k)")[:, :, 0:GC]
        v1 = cut(9216, dict(i=2, t=TG, d=D), "i t d")
        masked = cut(4096, dict(i=2, t=TG, k=P), "i t k")
        pT1 = cut(6144, dict(i=2, n=GC), "i n")
        cT1 = cut(7168, dict(i=2, n=GC), "i n")
        sm = sb("sm", [P, 2, 3, TG])

        def prep1(g):
            if g % 4 == 0:
                inverse_std(TG * g, 4 * TG)
            ev["ln1", g] = norm(g, g % 2)
            wait("pool", ev["tbo", 1], ev["ln1", g])
            ev["xb1", g] = do("pool", partial(nc.gpsimd.tensor_tensor,
                x_sb[:, TG * g:TG * g + TG, :], x_sb[:, TG * g:TG * g + TG, :],
                tbo_sb[:, 1:2, :].to_broadcast([P, TG, D]), ALU.add), s1["xb"])

        def project1(g, w, src, e_src, dst, bias, bank, sem_mm, sem_ev):
            wait("pe", e_src, bank.free)
            e = do("pe", partial(nc.tensor.matmul, bank.ap, w, src, start=True, stop=True), sem_mm)
            wait("act", e)
            bank.free = do("act", partial(nc.scalar.activation, dst, bank.ap, ACT.Identity, bias=bias), sem_ev)
            return e, bank.free

        def q1(g):
            i = g % 2
            wait("act", ev.get(("s1", g - 2)))
            lnT_free[i], ev["q1", g] = project1(g, w_sb[:, 5, :], lnT[:, i, :], ev["lnT1", g], qT[:, i, :], vec("bq1"), banks[7], s_q, s_qe)

        def k1(g):
            _, ev["k1", g] = project1(g, w_sb[:, 6, :], ctx_sb[:, g * GC:g * GC + GC], None, kT1[:, g % 2, :], vec("bk1"), banks[6], s_k, s_ke)

        def values1(g):
            i, bank = g % 2, banks[2]
            wait("pe", bank.free)
            for t in range(TG):
                c = (TG * g + t) * P
                e = do("pe", partial(nc.tensor.matmul, bank.ap[:, t * D:t * D + D], ctx_sb[:, c:c + P], w_sb[:, 7, :], start=True, stop=True), s1["v"])
            wait("act", e, ev.get(("c1", g - 2)))
            bank.free = ev["v1", g] = do("act", partial(nc.scalar.copy, v1[:, i, :, :], bank.ap.rearrange("p (t d) -> p t d", d=D)), s1["ve"])

        def scores1(g):
            i, bank = g % 2, banks[g % 2]
            wait("pe", ev["q1", g], ev["k1", g], bank.free)
            for c in range(0, GC, P):
                e = do("pe", partial(nc.tensor.matmul, bank.ap[:, c:c + P], qT[:, i, c:c + P], kT1[:, i, c:c + P], start=True, stop=True), s1["s"])
            ev["s1", g] = e

        def mask1(g):
            i, bank = g % 2, banks[g % 2]
            m = masked[:, i, :, :]
            wait("dve", ev["s1", g], ld["mask"], ev.get(("pt1", g - 2)))
            bank.free = e = do("dve", partial(nc.vector.scalar_tensor_tensor,
                out=m, in0=bank.ap.rearrange("p (t k) -> p t k", k=P), scalar=SCALE1,
                in1=mask_sb[:, 0:1, :].to_broadcast([P, TG, P]), op0=ALU.mult, op1=ALU.mult), s1["t"])
            wait("dve", e)
            e = do("dve", partial(nc.vector.tensor_tensor, m, m, mask_sb[:, 1:2, :].to_broadcast([P, TG, P]), ALU.add), s1["m"])
            wait("dve", e, ev.get(("x3", TG * (g - 2))))
            ev["max1", g] = do("dve", partial(nc.vector.tensor_reduce, sm[:, i, 0, :], m, AX_X, ALU.max, negate=True), s1["n"])

        def exponentials1(g, tiles):
            i = g % 2
            wait("act", ev["max1", g])
            for t in tiles:
                ev["e1", g] = do("act", partial(nc.scalar.activation, masked[:, i, t, :], masked[:, i, t, :], ACT.Exp,
                                                bias=sm[:, i, 0, t:t + 1], accum_out=sm[:, i, 1, t:t + 1]), s1["e"])

        def denominators1(g):
            i = g % 2
            wait("dve", ev["e1", g])
            e = do("dve", partial(nc.vector.reciprocal, sm[:, i, 2, :], sm[:, i, 1, :]), s1["r"])
            wait("dve", e)
            ev["r1", g] = do("dve", partial(nc.vector.tensor_scalar, sm[:, i, 2, :], sm[:, i, 2, :], TGX[1], None, ALU.mult), s1["r"])

        def turn1(g):
            i, bank = g % 2, banks[3]
            wait("pe", ev["e1", g], bank.free)
            for t in range(TG):
                e = do("pe", partial(nc.tensor.transpose, bank.ap[:, t * P:t * P + P], masked[:, i, t, :], ident[:]), s1["pt"])
            ev["pt1", g] = e
            wait("act", e, ev.get(("c1", g - 2)))
            bank.free = ev["pT1", g] = do("act", partial(nc.scalar.copy, pT1[:, i, :], bank.ap), s1["pT"])

        def attend1(g):
            i, bank = g % 2, banks[4]
            wait("pe", ev["pT1", g], ev["v1", g], bank.free)
            for t in range(TG):
                e = do("pe", partial(nc.tensor.matmul, bank.ap[:, t * P:t * P + P], v1[:, i, t, :], pT1[:, i, t * P:t * P + P],
                                     start=True, stop=True), s1["c"])
            ev["c1", g] = e
            wait("act", e, ev.get(("o1", g - 2)))
            bank.free = ev["cT1", g] = do("act", partial(nc.scalar.copy, cT1[:, i, :], bank.ap), s1["cT"])

        def output1(g):
            i, bank = g % 2, banks[5]
            wait("pe", ev["cT1", g], ld["wo1"], bank.free)
            for t in range(TG):
                e = do("pe", partial(nc.tensor.matmul, bank.ap[:, t * D:t * D + D], cT1[:, i, t * P:t * P + P], wo1_sb[:], start=True, stop=True), s1["o"])
            ev["o1", g] = e
            wait("dve", e, ev["xb1", g], ev["r1", g])
            for t in range(TG):
                tt = TG * g + t
                ev["x3", tt] = bank.free = do("dve", partial(nc.vector.scalar_tensor_tensor,
                    out=x_sb[:, tt, :], in0=bank.ap[:, t * D:t * D + D], scalar=sm[:, i, 2, t:t + 1], in1=x_sb[:, tt, :],
                    op0=ALU.mult, op1=ALU.add), s1["x"])

        def moments1(g):
            if g < NG:
                moments(TG * g, TG, [ev["x2", TG * g + t] for t in range(TG)])

        def begin1():
            for g in range(4):
                moments1(g)
                yield
            wait("dve", ev["put", NT - 4], e_one)
            output_bias(1, [(ones_row[:, 0:1].to_broadcast([P, P]), vec("bv_layer1"))], [wo1_sb[:]], ld["wo1"])
            yield
            prep1(0)

        def attention1(side):
            for u in range(-1, NG + 1):
                if u == 5:
                    side = side()
                here, last = 0 <= u < NG, 0 <= u - 1 < NG
                if 0 <= u + 1 < NG:
                    ev["lnT1", u + 1] = turn((u + 1) % 2, ev["ln1", u + 1], banks[6])
                if here:
                    mask1(u)
                if last:
                    turn1(u - 1)
                if 0 <= u + 1 < NG:
                    q1(u + 1)
                if here:
                    exponentials1(u, range(2))
                if last:
                    attend1(u - 1)
                if here:
                    exponentials1(u, range(2, TG))
                for n in range(3 * max(u + 1, 0), min(3 * u + 6, HALF)):
                    combine0(HALF + n)
                if u >= 5:
                    next(side, None)
                if 0 <= u + 1 < NG:
                    k1(u + 1)
                    values1(u + 1)
                if u >= -1:
                    moments1(u + 5)
                if 0 <= u + 2 < NG:
                    prep1(u + 2)
                if here:
                    denominators1(u)
                if last:
                    output1(u - 1)
                if u >= 5:
                    next(side, None)
                if 0 <= u + 1 < NG:
                    scores1(u + 1)
                if u >= 5:
                    next(side, None)
            return side

        for _ in side:
            pass
        for engine in ("sp", "dve", "pool"):
            wait(engine, ev["sc", NT - 1], ev["den", NT - 1])
        statistics(NT - 2 * TG, 2 * TG, [ev["x1", NT - 2 * TG + n] for n in range(2 * TG)])
        for g in range(NG - 3, NG):
            ev["ln0", g] = norm(g, g % 3)
        for h in range(2):
            side = rest_of_routing() if h == 0 else combine_half_0()
            for j in range(2):
                fetch_weights(h, j)
            for j in range(3):
                fetch_tokens(h, j)
            turn0(h, 0)
            for j in range(NBLOCKS + 1):
                if j + 3 < NBLOCKS:
                    fetch_tokens(h, j + 3)
                if j + 2 < NBLOCKS:
                    fetch_weights(h, j + 2)
                if j + 1 < NBLOCKS:
                    turn0(h, j + 1)
                if j > 0:
                    read_expert("pe", h, j - 1)
                if j < NBLOCKS:
                    up0(h, j)
                next(side, None)
                if j > 0:
                    down0(h, j - 1)
                if h == 0:
                    next(side, None)
            for _ in side:
                pass

        wait("sp", *[ev["w1_read", k] for k in range(3)], ev["down0", 1, NBLOCKS - 1])
        load("w1_layer1", w1_sb[:], t_in["w1b"])
        load("w2_layer1", w2_sb[:], t_in["w2b"])
        ld["w1"], ld["w2"] = ld["w1_layer1"], ld["w2_layer1"]

        both_r = total[:].rearrange("p e t -> p (e t)").rearrange("p (k b s) -> p k b s", k=2, b=2)
        scores_r = sb("scores_r", [P, 2, S])
        left_r = sb("left_r", [P, 2, S])
        mask_r = sb("mask_r", [P, 2, S])
        count_r = sb("count_r", [P, 2, S])
        top = sb("top", [P, 3, 8])
        gp = chosen[:, 0:2, :, :].rearrange("p a t e -> p (a t e)").rearrange("p (i k t e) -> p i k t e", i=2, k=2, t=NS)
        n_pt, n_pk = 2 * TS * 3 * P, 2 * NE * SLOTS
        pickT = ctx_sb[:, 0:n_pt].rearrange("p (i t k q) -> p i t k q", i=2, t=TS, k=3)
        pick, pickg = [ctx_sb[:, n_pt + n * n_pk:n_pt + (n + 1) * n_pk].rearrange("p (i e s) -> p i e s", i=2, e=NE)
                       for n in range(2)]
        yr = ctx_sb[:, n_pt + 2 * n_pk:n_pt + 2 * n_pk + 6 * D].rearrange("p (i k d) -> p i k d", i=2, k=3)
        n_xg = TS * NE * SLOTS
        xgT = [cut(n_xg * i, dict(e=NE, t=TS, s=SLOTS), "e t s") for i in range(2)]
        yT = [cut(n_xg * (2 + i), dict(t=TS, e=NE, s=SLOTS), "t e s") for i in range(2)]
        hid = cut(n_xg * 4, dict(i=2, c=HC, t=TS, s=SLOTS), "i c t s")
        KS = [(0, 3), (3, 6), (6, 8)]
        z = {n: sem("z_" + n) for n in ["tr", "tb", "gp", "pk", "pg", "ga", "xg", "pt", "pT", "up", "hg", "dn", "y",
                                        "yt", "yr", "sc", "x"]}

        def route1(lo):
            for g in range(lo // TG, (lo + NS) // TG):
                moments(TG * g, TG, [ev["x3", TG * g + t] for t in range(TG)])
                yield
            inverse_std(lo, NS)
            yield
            for g in range(lo // TG, (lo + NS) // TG):
                e = norm(g, ROUTER)
                yield
                e = turn(ROUTER, e, banks[7])
                yield
                e, src = logits(1, ROUTER, e, banks[7])
                banks[7].free = dve(partial(nc.vector.tensor_copy, lg_sb[:, TG * g:TG * g + TG, :], src), e)
                yield
            yield from softmax8(lo, NS)
            bank = banks[6]
            wait("pe", ev["probabilities", lo], bank.free)
            e = do("pe", partial(nc.tensor.transpose, bank.ap[:, 0:P], lg_sb[:, lo:lo + NS, :].rearrange("p t e -> p (t e)"), ident[:]), z["tr"])
            src = bank.ap[:, 0:P].rearrange("p (b k) -> p b k", k=S)
            wait("dve", e)
            do("dve", partial(nc.vector.tensor_copy, scores_r[:], src), s_r)
            bank.free = dve(partial(nc.vector.tensor_copy, left_r[:], src))
            yield
            for b in range(2):
                a, w, m, c = scores_r[:, b, :], left_r[:, b, :], mask_r[:, b, :], count_r[:, b, :]
                for k in range(CAP // 8):
                    dve(partial(nc.vector.max, top[:, k, :], w))
                    dve(partial(nc.vector.match_replace, out=w, in_to_replace=top[:, k, :], in_values=w, imm_value=-1.0))
                    yield
                dve(partial(nc.vector.max, top[:, 2, :], w))
                dve(partial(nc.vector.tensor_scalar, m, w, top[:, 2, 0:1], None, ALU.is_equal))
                dve(partial(nc.vector.tensor_tensor_scan, out=c, data0=ones_row[:], data1=m, initial=0.0,
                            op0=ALU.mult, op1=ALU.add), e_one)
                dve(partial(nc.vector.scalar_tensor_tensor, out=m, in0=c, scalar=1.0, in1=m, op0=ALU.is_equal, op1=ALU.mult))
                dve(partial(nc.vector.scalar_tensor_tensor, out=m, in0=w, scalar=0.0, in1=m, op0=ALU.is_lt, op1=ALU.add))
                yield
                dve(partial(nc.vector.scalar_tensor_tensor, out=both_r[:, 0, b, :], in0=a, scalar=TGF[1], in1=m,
                            op0=ALU.mult, op1=ALU.mult))
                dve(partial(nc.vector.tensor_tensor_scan, out=c, data0=ones_row[:], data1=m, initial=float(CAP * b),
                            op0=ALU.mult, op1=ALU.add))
                dve(partial(nc.vector.tensor_tensor, c, c, m, ALU.mult))
                e = dve(partial(nc.vector.tensor_scalar, both_r[:, 1, b, :], c, -1.0, None, ALU.add))
                yield
            wait("pe", e, bank.free)
            for k in range(2):
                e = do("pe", partial(nc.tensor.transpose, bank.ap[:, k * P:k * P + P],
                                     both_r[:, k, :, :].rearrange("p b k -> p (b k)"), ident[:]), z["tb"])
            h = (lo // NS) % 2
            wait("dve", e, ev.get(("pickg", lo - NS - 1)))
            ev["gp", lo] = bank.free = do("dve", partial(
                nc.vector.tensor_copy, gp[:, h, :, :, :], bank.ap[:, 0:2 * P].rearrange("p (k t e) -> p k t e", k=2, e=NE)), z["gp"])

        def pick1(t):
            i, h = t % 2, (t // NS) % 2
            place = gp[:, h, 1, t % NS, :].unsqueeze(2).to_broadcast([P, NE, SLOTS])
            gate = gp[:, h, 0, t % NS, :].unsqueeze(2).to_broadcast([P, NE, SLOTS])
            wait("dve", ev["gp", t // NS * NS], ld["slot"], ev.get(("ga", t - 2)), ev.get(("pickg", t - 2)))
            e = do("dve", partial(nc.vector.tensor_tensor, pick[:, i, :, :], slot_sb[:].unsqueeze(1).to_broadcast([P, NE, SLOTS]),
                                  place, ALU.is_equal), z["pk"])
            wait("pool", e, ev.get(("pt", t - 2)))
            ev["pickg", t] = do("pool", partial(nc.gpsimd.tensor_tensor, pickg[:, i, :, :], pick[:, i, :, :], gate, ALU.mult), z["pg"])
            ev["pick", t] = do("dve", partial(nc.vector.tensor_scalar, ln1[:, i, :], x_sb[:, t, :], mv[:, t, 0:1], rstd[:, t:t + 1],
                                              ALU.subtract, ALU.mult), z["pk"])

        def gather(t, bank=4):
            sg, i, bank = t // TS, t % 2, banks[bank]
            wait("pe", ev["pick", t], bank.free)
            ev["ga", t] = e = do("pe", partial(nc.tensor.matmul, bank.ap[:, 0:NE * SLOTS], ln1[:, i, :],
                                               pick[:, i, :, :].rearrange("p e s -> p (e s)"), start=True, stop=True), z["ga"])
            wait("act", e, ev.get(("up", sg - 2)))
            ev["xg1", sg] = bank.free = do("act", partial(
                nc.scalar.copy, xgT[sg % 2][:, :, t % TS, :], bank.ap[:, 0:NE * SLOTS].rearrange("p (e s) -> p e s", s=SLOTS)), z["xg"])

        def turn_pick(t, bank=5):
            sg, i, bank = t // TS, t % 2, banks[bank]
            wait("pe", ev["pickg", t], bank.free)
            for k, (a, b) in enumerate(KS):
                ev["pt", t] = e = do("pe", partial(
                    nc.tensor.transpose, bank.ap[0:(b - a) * SLOTS, k * P:k * P + P],
                    pickg[:, i, a:b, :].rearrange("p e s -> p (e s)"), ident[:]), z["pt"])

        def copy_pick(t, bank=5):
            sg, bank = t // TS, banks[bank]
            wait("dve", ev["pt", t], ev.get(("sc", t - 2 * TS)))
            rows = KS[0][1] * SLOTS
            do("dve", partial(nc.vector.tensor_copy, pickT[0:rows, sg % 2, t % TS, 0:2, :],
                              bank.ap[0:rows, 0:2 * P].rearrange("p (k q) -> p k q", q=P)), z["pT"])
            rows = (KS[2][1] - KS[2][0]) * SLOTS
            bank.free = ev["pT", t] = do("dve", partial(nc.vector.tensor_copy, pickT[0:rows, sg % 2, t % TS, 2, :],
                                                       bank.ap[0:rows, 2 * P:3 * P]), z["pT"])

        def up1(sg, ex):
            for c in range(HC):
                bank = banks[(HC * ex + c) % 3]
                wait("pe", ev["xg1", sg], ld["w1"], bank.free)
                e = do("pe", partial(nc.tensor.matmul, bank.ap[:, 0:TS * SLOTS], w1_sb[:, ex, c * P:c * P + P],
                                     xgT[sg % 2][:, ex, :, :].rearrange("p t s -> p (t s)"), start=True, stop=True), z["up"])
                wait("act", e, ld["b1"], ev.get(("dn", ex % 2)))
                ev["hg", ex % 2] = bank.free = do("act", partial(
                    nc.scalar.activation, hid[:, ex % 2, c, :, :].rearrange("p t s -> p (t s)"), bank.ap[:, 0:TS * SLOTS],
                    ACT.Gelu, bias=b1_sb[:, 1, ex * HC + c:ex * HC + c + 1]), z["hg"])
            ev["up", sg] = e

        def down1(sg, ex):
            bank = banks[3]
            wait("pe", ev["hg", ex % 2], ld["w2"], bank.free)
            for c in range(HC):
                e = do("pe", partial(nc.tensor.matmul, bank.ap[:, 0:TS * SLOTS], w2_sb[:, ex, c, :],
                                     hid[:, ex % 2, c, :, :].rearrange("p t s -> p (t s)"), start=(c == 0), stop=(c == HC - 1)), z["dn"])
            ev["dn", ex % 2] = e
            wait("dve", e, ld["b2T"], ev.get(("yt", (sg - 1) * TS - 1)))
            ev["y", sg] = bank.free = do("dve", partial(
                nc.vector.tensor_scalar, yT[sg % 2][:, :, ex, :], bank.ap[:, 0:TS * SLOTS].rearrange("p (t s) -> p t s", s=SLOTS),
                b2T_sb[:, ex:ex + 1], None, ALU.add), z["y"])

        def turn_results(t, bank=6):
            sg, i, bank = t // TS, t % 2, banks[bank]
            wait("pe", ev["y", sg], bank.free)
            for k, (a, b) in enumerate(KS):
                e = do("pe", partial(nc.tensor.transpose, bank.ap[0:(b - a) * SLOTS, k * D:k * D + D],
                                     yT[sg % 2][:, t % TS, a:b, :].rearrange("p e s -> p (e s)"), ident[:]), z["yt"])
            ev["yt", t] = e
            wait("act", e, ev.get(("sc", t - 2)))
            rows = KS[0][1] * SLOTS
            do("act", partial(nc.scalar.copy, yr[0:rows, i, 0:2, :], bank.ap[0:rows, 0:2 * D].rearrange("p (k q) -> p k q", q=D)), z["yr"])
            rows = (KS[2][1] - KS[2][0]) * SLOTS
            ev["yr", t] = bank.free = do("act", partial(nc.scalar.copy, yr[0:rows, i, 2, :], bank.ap[0:rows, 2 * D:3 * D]), z["yr"])

        def scatter(t, bank=7):
            sg, i, bank = t // TS, t % 2, banks[bank]
            wait("pe", ev["yr", t], ev["pT", t], bank.free)
            for k, (a, b) in enumerate(KS):
                rows = (b - a) * SLOTS
                e = do("pe", partial(nc.tensor.matmul, bank.ap[:, 0:D], pickT[0:rows, sg % 2, t % TS, k, :], yr[0:rows, i, k, :],
                                     start=(k == 0), stop=(k == 2)), z["sc"])
            ev["sc", t] = e
            wait("dve", e)
            ev["x4", t] = bank.free = do("dve", partial(nc.vector.tensor_tensor, x_sb[:, t, :], bank.ap[:, 0:D], x_sb[:, t, :], ALU.add), z["x"])

        for _ in attention1(lambda: route1(0)):
            pass

        pick1(0)
        for t in range(TS):
            pick1(t + 1)
            gather(t, (4, 0)[t % 2])
            turn_pick(t, (5, 1)[t % 2])
            copy_pick(t, (5, 1)[t % 2])
        routing = route1(NS)
        for sg in range(NSG):
            for ex in range(NE):
                t = (sg + 1) * TS + ex
                up1(sg, ex)
                if ex > 0:
                    down1(sg, ex - 1)
                if ex == 0 and sg > 0:
                    down1(sg - 1, NE - 1)
                next(routing, None)
                if sg > 0:
                    turn_results(t - 2 * TS)
                if t < NT:
                    gather(t)
                if t < NT:
                    turn_pick(t)
                if sg > 0:
                    scatter(t - 2 * TS)
                if t < NT:
                    copy_pick(t)
                next(routing, None)
                if (t + 1) % NS == 0:
                    for _ in routing:
                        pass
                    routing = route1(t + 1 + NS) if t + 1 + NS < NT else iter(())
                if TS < t + 1 < NT:
                    pick1(t + 1)
        down1(NSG - 1, NE - 1)
        for t in range(NT - TS, NT + 1):
            if t < NT:
                turn_results(t, (6, 4)[t % 2])
            if t > NT - TS:
                scatter(t - 1, (7, 5)[t % 2])

        s_out = sem("s_out")
        for g in range(NG):
            wait("sp", ev["x4", TG * g + TG - 1])
            e = do("sp", partial(nc.sync.dma_start, out[:, TG * g:TG * g + TG, :], x_sb[:, TG * g:TG * g + TG, :]), s_out, 16)
        wait("sp", e)

        block = ctx.enter_context(nc.Block())

        @block.sync
        def _(e):
            plan.run("sp", e)

        @block.scalar
        def _(e):
            plan.run("act", e)

        @block.tensor
        def _(e):
            plan.run("pe", e)

        @block.vector
        def _(e):
            plan.run("dve", e)

        @block.gpsimd
        def _(e):
            plan.run("pool", e)


def lay_out(i):
    a = {k: np.asarray(v) for k, v in i.items()}
    col = lambda v: np.broadcast_to(v.reshape(-1, 1) if v.size > 1 else v.reshape(1, 1), (P, 1))
    f = lambda *c: np.ascontiguousarray(np.concatenate(c, axis=1), np.float32)
    r = np.arange(P)
    quad = [((r // DH) % QUADS == j).astype(np.float32).reshape(P, 1) for j in range(QUADS)]
    row = [(r // S == b).astype(np.float32).reshape(P, 1) for b in range(2)]
    own = ((r // (2 * DH)) % 2 == 0).astype(np.float32).reshape(P, 1)
    gx, gf = a["g_xattn"], a["g_ffn"]
    rr, bb, hh, dd = np.meshgrid(np.arange(4), np.arange(2), np.arange(2), np.arange(DH), indexing="ij")
    head = np.array([4 * quad + j for quad in (0, 2, 1, 3) for j in range(4)])
    dims = (head[:, None] * DH + np.arange(DH)).ravel()
    src = [(head[half * 8 + rr * 2 + hh] * DH + dd).ravel() for half in range(2)]
    w = [a["L0_xattn_w_q"], a["L0_xattn_w_k"], a["L0_xattn_w_v"][:, dims], a["L0_xattn_w_out"][src[0]], a["L0_xattn_w_out"][src[1]],
         a["L1_xattn_Wq"], a["L1_xattn_Wk"], a["L1_xattn_Wv"]]
    rows = [a["L0_xattn_b_out"], a["L1_xattn_bo"]]
    q, k = r[:, None], r[None, :]
    same = q // S == k // S
    mask = np.stack([(same & (k <= q)), np.where(same, np.where(k <= q, 0.0, NEG), OUTSIDE)], 1).astype(np.float32)
    small = np.zeros((P, 2, NE), np.float32)
    small[:, 0, :] = a["L0_ffn_bg"]
    small[:, 1, :] = NE - np.arange(NE)
    c = np.ascontiguousarray
    return {
        "x": c(a["x"].reshape(NT, P, D).transpose(1, 0, 2)),
        "ctxT": c(a["ctx_1024"].reshape(NT * P, D).T),
        "w": c(np.stack(w, 1)),
        "wo1": c(a["L1_xattn_Wo"]),
        "vecs": f(col(a["L0_xattn_b_q"]), col(a["L0_xattn_b_k"]), col(a["L1_xattn_bq"]), col(a["L1_xattn_bk"]),
                  col(gx[0:1]), col(gx[1:2]), col(gf[0:1]), col(gf[1:2]), *quad, *row, own,
                  col(a["L0_xattn_b_v"][src[0]]), col(a["L0_xattn_b_v"][src[1]]), col(a["L1_xattn_bv"])),
        "rows": c(np.broadcast_to(np.stack(rows, 0)[None], (P, 2, D))),
        "ident": np.eye(P, dtype=np.float32),
        "small": small,
        "mask": mask,
        "wr": c(np.stack([a["L0_ffn_Wg"], a["L1_ffn_router_w"].T], 1)),
        "w1a": c(a["L0_ffn_W1"].transpose(1, 0, 2)),
        "w1b": c(a["L1_ffn_w1"].transpose(1, 0, 2)),
        "w2a": c(a["L0_ffn_W2"].reshape(NE, HC, P, D).transpose(2, 0, 1, 3)),
        "w2b": c(a["L1_ffn_w2"].reshape(NE, HC, P, D).transpose(2, 0, 1, 3)),
        "b1": c(np.stack([a["L0_ffn_b1"].reshape(NE * HC, P).T, a["L1_ffn_b1"].reshape(NE * HC, P).T], 1)),
        "b2T": c(a["L1_ffn_b2"].T),
        "slot": c(np.broadcast_to(np.arange(SLOTS, dtype=np.float32), (P, SLOTS))),
        "b2": c(np.broadcast_to(a["L0_ffn_b2"][None], (P, NE, D))),
        "before": c(np.stack([(q < k), np.ones((P, P))], 1).astype(np.float32)),
        "block": np.arange(NBLOCKS, dtype=np.float32).reshape(1, NBLOCKS),
    }


def kernel(**inputs):
    import concourse.bacc as bacc
    from concourse.bass_utils import run_bass_kernel_spmd

    arrays = lay_out(inputs)
    nc = bacc.Bacc("TRN2", target_bir_lowering=False, num_devices=1)
    t_in = {n: nc.dram_tensor("in_" + n, v.shape, mybir.dt.from_np(v.dtype), kind="ExternalInput").ap()
            for n, v in arrays.items()}
    out = nc.dram_tensor("out_x", (P, NT, D), F32, kind="ExternalOutput").ap()
    build(nc, t_in, out)
    r = run_bass_kernel_spmd(nc, [{"in_" + n: v for n, v in arrays.items()}], core_ids=[0])
    got = r.results[0]["out_x"]
    return np.ascontiguousarray(got.transpose(1, 0, 2)).reshape(NB, S, D)
```
